# Optimizing a Trainium2 kernel written in Bass

```python
import numpy as np
import jax
import jax.numpy as jnp

def _softmax(x, axis=-1):
    return jax.nn.softmax(x, axis=axis)

def _gelu(x):
    return jax.nn.gelu(x, approximate=True)

def _silu(x):
    return jax.nn.silu(x)

def _sigmoid(x):
    return jax.nn.sigmoid(x)

def _layernorm(x, axis=-1, eps=1e-05):
    m = jnp.mean(x, axis=axis, keepdims=True)
    v = jnp.var(x, axis=axis, keepdims=True)
    return (x - m) / jnp.sqrt(v + eps)

def _scatter_add(tgt, idx, src, axis=0):
    return tgt.at[idx].add(src)

def _segment_sum(src, seg, n):
    return jax.ops.segment_sum(src, seg, n)
kernel_name = 'mk_hybrid_d1_jaxref_r8_e373a1'

def setup_inputs(seed: int=0):
    np.random.seed(seed)
    _w = jnp.asarray

    def _L0_attn_a_setup():
        import jax, jax.numpy as jnp
        import numpy as np
        B, T, E = (4, 128, 128)
        H, D = (16, 64)
        HID = H * D
        WINDOW = 32
        INF = 10000.0

        def _sin_cos_neg(seq_len, d):
            pos = jnp.arange(-seq_len + 1, seq_len, dtype=jnp.float32)
            freqs = jnp.arange(0, d, 2, dtype=jnp.float32)
            inv = 1.0 / 10000.0 ** (freqs / d)
            pe = pos[:, None] * inv[None, :]
            return jnp.concatenate([jnp.sin(pe), jnp.cos(pe)], axis=-1)
        key = jax.random.key(seed)
        ks = jax.random.split(key, 8)
        return {'x': jax.random.normal(ks[0], (B, T, E), jnp.float32), 'W_q': jax.random.normal(ks[1], (E, HID), jnp.float32) / np.sqrt(E), 'W_k': jax.random.normal(ks[2], (E, HID), jnp.float32) / np.sqrt(E), 'W_v': jax.random.normal(ks[3], (E, HID), jnp.float32) / np.sqrt(E), 'content_bias': 0.02 * jax.random.normal(ks[4], (H, D), jnp.float32), 'relative_bias': 0.02 * jax.random.normal(ks[5], (H, D), jnp.float32), 'W_rel': jax.random.normal(ks[6], (D, D), jnp.float32) / np.sqrt(D), 'b_rel': jnp.zeros((D,), jnp.float32), 'W_o': jax.random.normal(ks[7], (HID, E), jnp.float32) / np.sqrt(HID), 'b_o': jnp.zeros((E,), jnp.float32)}
    _L0_attn_a_in = _L0_attn_a_setup()

    def _L0_attn_b_setup():
        import jax, jax.numpy as jnp
        import numpy as np

        def apply_rope(x):
            b, h, n, d = x.shape
            half = d // 2
            freqs = jnp.arange(0, half, dtype=x.dtype) / half
            theta = 1.0 / 1250 ** freqs
            positions = jnp.arange(n, dtype=x.dtype)
            angles = positions[:, None] * theta[None, :]
            cos = jnp.cos(angles)[None, None, :, :]
            sin = jnp.sin(angles)[None, None, :, :]
            x1 = x[..., ::2]
            x2 = x[..., 1::2]
            r1 = x1 * cos - x2 * sin
            r2 = x1 * sin + x2 * cos
            return jnp.stack([r1, r2], axis=-1).reshape(b, h, n, d)
        key = jax.random.key(seed)
        ks = jax.random.split(key, 4)
        B, N, D = (2, 256, 128)
        x = jax.random.normal(ks[0], (B, N, D), dtype=jnp.float32)
        w_qkv = jax.random.normal(ks[1], (D, 3 * D), dtype=jnp.float32) * (1.0 / np.sqrt(D))
        b_qkv = jnp.zeros((3 * D,), dtype=jnp.float32)
        w_out = jax.random.normal(ks[2], (D, D), dtype=jnp.float32) * (1.0 / np.sqrt(D))
        b_out = jnp.zeros((D,), dtype=jnp.float32)
        return {'x': x, 'w_qkv': w_qkv, 'b_qkv': b_qkv, 'w_out': w_out, 'b_out': b_out}
    _L0_attn_b_in = _L0_attn_b_setup()

    def _L0_ffn_setup():
        import jax, jax.numpy as jnp
        import numpy as np
        DIM = 128

        def _reference_tuple_inner(x, W_r, W_k, W_v, mu_r, mu_k):
            B, T, C = x.shape
            x_prev = jnp.concatenate([jnp.zeros((B, 1, C), x.dtype), x[:, :-1, :]], axis=1)
            xr = mu_r * x + (1.0 - mu_r) * x_prev
            xk = mu_k * x + (1.0 - mu_k) * x_prev
            r = jax.nn.sigmoid(jnp.einsum('btc,dc->btd', xr, W_r))
            k = jnp.einsum('btc,dc->btd', xk, W_k)
            k_act = jnp.square(jax.nn.relu(k))
            out = r * jnp.einsum('btc,dc->btd', k_act, W_v)
            new_state = x[:, -1, :]
            return (out, new_state)
        key = jax.random.key(seed)
        ks = jax.random.split(key, 6)
        B, T, C = (8, 256, DIM)
        x = jax.random.normal(ks[0], (B, T, C), dtype=jnp.float32)
        s = 1.0 / np.sqrt(C)
        W_r = jax.random.uniform(ks[1], (C, C), jnp.float32, -s, s)
        W_k = jax.random.uniform(ks[2], (C, C), jnp.float32, -s, s)
        W_v = jax.random.uniform(ks[3], (C, C), jnp.float32, -s, s)
        mu_r = jax.random.uniform(ks[4], (C,), jnp.float32)
        mu_k = jax.random.uniform(ks[5], (C,), jnp.float32)
        return {'x': x, 'W_r': W_r, 'W_k': W_k, 'W_v': W_v, 'mu_r': mu_r, 'mu_k': mu_k}
    _L0_ffn_in = _L0_ffn_setup()
    _d = {'L0_attn_a_x': _L0_attn_a_in['x'], 'L0_attn_a_W_q': _L0_attn_a_in['W_q'], 'L0_attn_a_W_k': _L0_attn_a_in['W_k'], 'L0_attn_a_W_v': _L0_attn_a_in['W_v'], 'L0_attn_a_content_bias': _L0_attn_a_in['content_bias'], 'L0_attn_a_relative_bias': _L0_attn_a_in['relative_bias'], 'L0_attn_a_W_rel': _L0_attn_a_in['W_rel'], 'L0_attn_a_b_rel': _L0_attn_a_in['b_rel'], 'L0_attn_a_W_o': _L0_attn_a_in['W_o'], 'L0_attn_a_b_o': _L0_attn_a_in['b_o'], 'L0_attn_b_w_qkv': _L0_attn_b_in['w_qkv'], 'L0_attn_b_b_qkv': _L0_attn_b_in['b_qkv'], 'L0_attn_b_w_out': _L0_attn_b_in['w_out'], 'L0_attn_b_b_out': _L0_attn_b_in['b_out'], 'L0_ffn_W_r': _L0_ffn_in['W_r'], 'L0_ffn_W_k': _L0_ffn_in['W_k'], 'L0_ffn_W_v': _L0_ffn_in['W_v'], 'L0_ffn_mu_r': _L0_ffn_in['mu_r'], 'L0_ffn_mu_k': _L0_ffn_in['mu_k']}
    _x0 = _d['L0_attn_a_x']
    _d['L0_attn_a_x'] = jax.random.normal(jax.random.fold_in(jax.random.key(seed), 1), (2, 1024, 128), dtype=_x0.dtype)
    del _x0
    return _d

def reference(L0_attn_a_x, L0_attn_a_W_q, L0_attn_a_W_k, L0_attn_a_W_v, L0_attn_a_content_bias, L0_attn_a_relative_bias, L0_attn_a_W_rel, L0_attn_a_b_rel, L0_attn_a_W_o, L0_attn_a_b_o, L0_attn_b_w_qkv, L0_attn_b_b_qkv, L0_attn_b_w_out, L0_attn_b_b_out, L0_ffn_W_r, L0_ffn_W_k, L0_ffn_W_v, L0_ffn_mu_r, L0_ffn_mu_k):

    def _L0_attn_a_ref(x, W_q, W_k, W_v, content_bias, relative_bias, W_rel, b_rel, W_o, b_o):
        import jax, jax.numpy as jnp
        import numpy as np
        B, T, E = (4, 128, 128)
        H, D = (16, 64)
        HID = H * D
        WINDOW = 32
        INF = 10000.0

        def _sin_cos_neg(seq_len, d):
            pos = jnp.arange(-seq_len + 1, seq_len, dtype=jnp.float32)
            freqs = jnp.arange(0, d, 2, dtype=jnp.float32)
            inv = 1.0 / 10000.0 ** (freqs / d)
            pe = pos[:, None] * inv[None, :]
            return jnp.concatenate([jnp.sin(pe), jnp.cos(pe)], axis=-1)
        b, t, e = x.shape
        q = (x @ W_q).reshape(b, t, H, D)
        k = (x @ W_k).reshape(b, t, H, D)
        v = (x @ W_v).reshape(b, t, H, D)
        content_logits = jnp.einsum('bthd,bThd->bhtT', q + content_bias, k)
        enc = _sin_cos_neg(t, D)
        i = jnp.arange(t)
        idx = i[None, :] - i[:, None] + t - 1
        rel_keys = enc[idx] @ W_rel + b_rel
        relative_logits = jnp.einsum('bthd,Ttd->bhtT', q + relative_bias, rel_keys)
        attn = (content_logits + relative_logits) * (1.0 / jnp.sqrt(jnp.float32(HID)))
        band = (jnp.abs(i[:, None] - i[None, :]) <= WINDOW // 2).astype(attn.dtype)
        attn = attn + -INF * (1.0 - band)
        p = jax.nn.softmax(attn, axis=-1)
        out = jnp.einsum('bhtT,bThd->bthd', p, v).reshape(b, t, HID)
        return out @ W_o + b_o

    def _L0_attn_b_ref(x, w_qkv, b_qkv, w_out, b_out):
        import jax, jax.numpy as jnp
        import numpy as np

        def apply_rope(x):
            b, h, n, d = x.shape
            half = d // 2
            freqs = jnp.arange(0, half, dtype=x.dtype) / half
            theta = 1.0 / 1250 ** freqs
            positions = jnp.arange(n, dtype=x.dtype)
            angles = positions[:, None] * theta[None, :]
            cos = jnp.cos(angles)[None, None, :, :]
            sin = jnp.sin(angles)[None, None, :, :]
            x1 = x[..., ::2]
            x2 = x[..., 1::2]
            r1 = x1 * cos - x2 * sin
            r2 = x1 * sin + x2 * cos
            return jnp.stack([r1, r2], axis=-1).reshape(b, h, n, d)
        B, N, D = x.shape
        H = 16
        hd = D // H
        qkv = x @ w_qkv + b_qkv
        q, k, v = jnp.split(qkv, 3, axis=-1)
        to_heads = lambda t: t.reshape(B, N, H, hd).transpose(0, 2, 1, 3)
        q, k, v = (to_heads(q), to_heads(k), to_heads(v))
        q = jax.nn.elu(q) + 1
        k = jax.nn.elu(k) + 1
        rot_q = apply_rope(q)
        rot_k = apply_rope(k)
        attn_num = jnp.einsum('bhid,bhjd->bhij', rot_q, rot_k)
        attn_denom = jnp.einsum('bhid,bhjd->bhij', q, k)
        attn_weights = attn_num / attn_denom
        out = jnp.einsum('bhij,bhjd->bhid', attn_weights, v)
        out = out.transpose(0, 2, 1, 3).reshape(B, N, D)
        return out @ w_out + b_out

    def _L0_ffn_ref(x, W_r, W_k, W_v, mu_r, mu_k):
        import jax, jax.numpy as jnp
        import numpy as np
        DIM = 128

        def _reference_tuple_inner(x, W_r, W_k, W_v, mu_r, mu_k):
            B, T, C = x.shape
            x_prev = jnp.concatenate([jnp.zeros((B, 1, C), x.dtype), x[:, :-1, :]], axis=1)
            xr = mu_r * x + (1.0 - mu_r) * x_prev
            xk = mu_k * x + (1.0 - mu_k) * x_prev
            r = jax.nn.sigmoid(jnp.einsum('btc,dc->btd', xr, W_r))
            k = jnp.einsum('btc,dc->btd', xk, W_k)
            k_act = jnp.square(jax.nn.relu(k))
            out = r * jnp.einsum('btc,dc->btd', k_act, W_v)
            new_state = x[:, -1, :]
            return (out, new_state)
        return _reference_tuple_inner(x, W_r, W_k, W_v, mu_r, mu_k)[0]
    x = L0_attn_a_x
    x = x + _L0_attn_a_ref(_layernorm(x, axis=-1), L0_attn_a_W_q, L0_attn_a_W_k, L0_attn_a_W_v, L0_attn_a_content_bias, L0_attn_a_relative_bias, L0_attn_a_W_rel, L0_attn_a_b_rel, L0_attn_a_W_o, L0_attn_a_b_o)
    x = x + _L0_ffn_ref(_layernorm(x, axis=-1), L0_ffn_W_r, L0_ffn_W_k, L0_ffn_W_v, L0_ffn_mu_r, L0_ffn_mu_k)
    x = x + _L0_attn_b_ref(_layernorm(x, axis=-1), L0_attn_b_w_qkv, L0_attn_b_b_qkv, L0_attn_b_w_out, L0_attn_b_b_out)
    x = x + _L0_ffn_ref(_layernorm(x, axis=-1), L0_ffn_W_r, L0_ffn_W_k, L0_ffn_W_v, L0_ffn_mu_r, L0_ffn_mu_k)
    return x

_drawn_inputs = setup_inputs


def setup_inputs(seed=0):
    import zlib

    import numpy as np

    out = dict(_drawn_inputs(seed))
    spreads = {'L0_attn_a_b_rel': (0.0, 2.0),
     'L0_attn_a_b_o': (0.0, 0.1),
     'L0_attn_b_b_qkv': (0.0, 0.1),
     'L0_attn_b_b_out': (0.0, 0.8)}
    factors = {'L0_attn_a_content_bias': 22.086,
     'L0_attn_a_relative_bias': 35.051,
     'L0_attn_a_W_rel': 3.0,
     'L0_ffn_W_r': 2.705,
     'L0_ffn_mu_r': 6.001}
    for name, (base, spread) in spreads.items():
        noise = np.random.default_rng([zlib.crc32(name.encode()), seed]).standard_normal(out[name].shape)
        drawn = base * np.exp(spread * noise) if base else spread * noise
        out[name] = jnp.asarray(drawn.astype(out[name].dtype))
    for name, factor in factors.items():
        out[name] = (out[name] * factor).astype(out[name].dtype)
    return out
```

```python
from contextlib import ExitStack

import numpy as np
import concourse.bass as bass
from concourse import mybir

P = 128
E = 128
NB, NT = 2, 1024
BLK = NT // P
H, D = 16, 64
NP_ = H // 2
CH = 512
CB = CH // P
HALO = 16
SUB = 32
WIN = SUB + 2 * HALO
NW = CH // SUB
CK = CH + 2 * HALO
KH = CK // 2
SIDE = WIN
EDGE = HALO + SIDE
XC = CK + 2 * SIDE
NX = NW + 2
HB, DB = 16, 8
PARTS = 3
KROWS = PARTS * PARTS * DB
EPS = 1e-5
INF = 10000.0
SCALE = 1.0 / float(np.sqrt(np.float32(H * D)))

ALU = mybir.AluOpType
ACT = mybir.ActivationFunctionType
AX = mybir.AxisListType
F32 = mybir.dt.float32
BF16 = mybir.dt.bfloat16


def constants():
    inv = (1.0 / np.float32(10000.0) ** (np.arange(0, D, 2, dtype=np.float32) / np.float32(D))).astype(np.float64)
    q_angle = inv[:, None] * np.arange(CH)[None, :]
    k_angle = inv[:, None] * (np.arange(CK) - HALO)[None, :]
    sin_q = np.concatenate([np.sin(q_angle)] * 4, 0)
    cos_q = np.concatenate([np.cos(q_angle), -np.cos(q_angle)] * 2, 0)
    enc_k = np.concatenate([np.cos(k_angle), np.sin(k_angle)], 0)
    mask = np.zeros((P, NT // CH, CB, WIN), np.float32)
    for half in range(NT // CH):
        for blk in range(CB):
            for p in range(P):
                ql = p % SUB
                rel = np.arange(WIN)
                key = half * CH + blk * P + (p // SUB) * SUB - HALO + rel
                ok = (rel >= ql) & (rel - ql <= 2 * HALO) & (key >= 0) & (key < NT)
                mask[p, half, blk] = np.where(ok, 0.0, -INF / SCALE)
    theta = (1.0 / np.float32(1250.0) ** (np.arange(0, DB // 2, dtype=np.float32) / np.float32(DB // 2))).astype(np.float32)
    angle = (np.arange(NT, dtype=np.float32)[:, None] * theta[None, :]).astype(np.float32).astype(np.float64)
    rot_cos = np.repeat(np.cos(angle), 2, axis=1)
    rot_sin = np.stack([-np.sin(angle), np.sin(angle)], -1).reshape(NT, DB)
    rows = lambda a: a.reshape(BLK, P, DB).transpose(1, 0, 2)
    return {
        "ident": np.eye(P), "sin_q": sin_q, "cos_q": cos_q, "enc_k": enc_k, "mask": mask,
        "rot_cos": rows(rot_cos), "rot_sin": rows(rot_sin),
    }


def layouts(i):
    a = {k: np.asarray(v) for k, v in i.items()}
    rel_t = a["L0_attn_a_W_rel"].T
    rel_sw = np.concatenate([rel_t[:, D // 2:], rel_t[:, :D // 2]], 1)
    heads_t = lambda w: w.reshape(E, H, D).transpose(2, 1, 0)
    w_out = a["L0_attn_b_w_out"].reshape(HB // 2, 2, 1, DB, E)
    w_out = np.broadcast_to(w_out, (HB // 2, 2, DB, DB, E)).reshape(HB // 2, P, E).transpose(1, 0, 2)
    return {
        "x": a["L0_attn_a_x"].reshape(NB * BLK, P, E).transpose(1, 0, 2),
        "wq": a["L0_attn_a_W_q"], "wk": a["L0_attn_a_W_k"],
        "wq_t": heads_t(a["L0_attn_a_W_q"]), "wv_t": heads_t(a["L0_attn_a_W_v"]),
        "wo": a["L0_attn_a_W_o"].reshape(H, D, E).transpose(1, 0, 2),
        "rel": np.concatenate([rel_t, rel_t, rel_sw, rel_sw], 1),
        "cb_pair": a["L0_attn_a_content_bias"].reshape(NP_, P).T,
        "cb_t": a["L0_attn_a_content_bias"].T, "rb_t": a["L0_attn_a_relative_bias"].T,
        "brel": np.tile(a["L0_attn_a_b_rel"], 2)[:, None],
        "bo": a["L0_attn_a_b_o"][None, :],
        "wr_t": a["L0_ffn_W_r"].T, "wk_t": a["L0_ffn_W_k"].T, "wv2_t": a["L0_ffn_W_v"].T,
        "mu": np.stack([a["L0_ffn_mu_r"], a["L0_ffn_mu_k"]], 1),
        "wqkv": a["L0_attn_b_w_qkv"], "bqkv": np.broadcast_to(a["L0_attn_b_b_qkv"], (P, 3 * HB * DB)),
        "wout": w_out, "bout": np.broadcast_to(a["L0_attn_b_b_out"], (P, E)),
    }


def program(nc, ins, out_dram, split_dram, rq_dram):
    ctx = ExitStack()
    with ctx:
        def sb(name, shape, dt=F32):
            return ctx.enter_context(nc.sbuf_tensor(name, shape, dt))

        def sem(name):
            return ctx.enter_context(nc.semaphore(name))

        ps = ctx.enter_context(nc.psum_tensor("ps", [P, 8, 512], F32))

        x_tok = sb("x_tok", [P, NB * BLK, E])
        ident = sb("ident", [P, P])
        wq = sb("wq_sb", [P, H * D])
        wk = sb("wk_sb", [P, H * D])
        rel = sb("rel_sb", [D, 4 * D])
        cb_pair = sb("cb_pair_sb", [P, NP_])
        cb_t = sb("cb_t_sb", [D, H])
        rb_t = sb("rb_t_sb", [D, H])
        brel = sb("brel_sb", [P, 1])
        bo = sb("bo_sb", [1, E])
        bout = sb("bout_sb", [P, E])
        wr_t = sb("wr_t_sb", [P, E])
        wk_t = sb("wk_t_sb", [P, E])
        wv2_t = sb("wv2_t_sb", [P, E])
        mu = sb("mu_sb", [P, 2])
        wqkv = sb("wqkv_sb", [P, 3 * E])
        bqkv = sb("bqkv_sb", [P, 3 * E])
        wout = sb("wout_sb", [P, NP_, E])
        sin_q = sb("sin_q_sb", [P, CH])
        cos_q = sb("cos_q_sb", [P, CH])
        mask = sb("mask_sb", [P, NT // CH, CB, WIN])
        rot_cos = sb("rot_cos_sb", [P, BLK, DB])
        rot_sin = sb("rot_sin_sb", [P, BLK, DB])

        wu = sb("wu", [P, 2, NP_, 2, D])
        u_bias = sb("u_bias", [P, 2, NP_])
        head_const = sb("head_const", [P, H])
        bias_gap = sb("bias_gap", [D, H])
        brel_wide = sb("brel_wide", [D, P])
        ones = sb("ones", [1, P])
        mu_rest = sb("mu_rest", [P, 2])
        wvo = sb("wvo", [P, H, E])
        eps = sb("eps", [P, 1])
        idle = sb("idle", [P, 2])
        xT = sb("xT", [P, NB, NT + 2 * EDGE])

        xc = sb("xc", [P, XC])
        qt = sb("qt", [P, 2, 2, CH])
        kt = sb("kt", [P, 2, 2, CK])
        mx = sb("mx", [P, 2, CB * 2])
        tot = sb("tot", [P, 2, CB * 2])
        rtot = sb("rtot", [P, 2, CB * 2])
        xw = sb("xw", [P, NX, E])
        arena = sb("arena", [P, 16384])
        zh = arena[:, 0:8192].rearrange("p (h t) -> p h t", h=H)
        pt = arena[:, 8192:12288].rearrange("p (g t) -> p g t", g=NP_)
        turn = arena[:, 12288:14336].rearrange("p (b k t) -> p b k t", b=2, k=2)
        sm = arena[:, 14336:15360].rearrange("p (b k h w) -> p b k h w", b=2, k=CB, h=2)
        pr = arena[:, 15360:16384].rearrange("p (b k h w) -> p b k h w", b=2, k=CB, h=2)
        wq_t = arena[0:D, 0:2048].rearrange("p (h e) -> p h e", h=H)
        wv_t = arena[0:D, 2048:4096].rearrange("p (h e) -> p h e", h=H)
        wo = arena[0:D, 4096:6144].rearrange("p (h e) -> p h e", h=H)
        xn = arena[:, 6144:8192].rearrange("p (k e) -> p k e", e=E)
        z_sb = arena[:, 0:2048].rearrange("p (s t) -> p s t", s=2)
        g_sb = arena[:, 2048:4096].rearrange("p (s t) -> p s t", s=2)
        half_ln = arena[:, 4096:4608]
        r_buf = arena[:, 8192:16384].rearrange("p (g t) -> p g t", g=8)

        stat = sb("stat", [P, NB * BLK, 6])
        mv = sb("mv", [P, NB * BLK, 2])
        lnv = sb("lnv", [P, NB * BLK])
        rstd = sb("rstd", [P, NB * BLK])
        x1 = sb("x1", [P, CB, E])
        xh = sb("xh", [P, CB, E])
        fx = sb("fx", [P, NB, NT + 1])
        fmix = sb("fmix", [P, 2, CH])
        fprev = sb("fprev", [P, 2, CH])
        fk = sb("fk", [P, CH])
        fk2 = sb("fk2", [P, CH])
        fe = sb("fe", [P, CH])
        fs = sb("fs", [P, CH])
        fo = sb("fo", [P, CH])
        x_mid = x_tok
        x_out = x1
        qkv = arena[:, 8192:9216].rearrange("p (k n) -> p k n", k=CB)
        qk_neg = arena[:, 9216:10240].rearrange("p (k n) -> p k n", k=CB)
        rest = arena[:, 10240:11264].rearrange("p (a t) -> p a t", a=2)
        rqt = arena[:, 11264:11776]
        x3t = arena[:, 11776:12288]
        rq = sb("rq", [P, CB, E])
        rk = sb("rk", [P, NB * BLK, E])
        v_tok = sb("v_tok", [P, NB * BLK, E])
        parts = sb("parts", [P, 2, PARTS, CH], BF16)

        qs = wu[:].rearrange("p a g s d -> p (a g s d)").bitcast(BF16).rearrange("p (b h t) -> p b h t", b=2, h=2)
        ks = wvo[:].rearrange("p h e -> p (h e)").bitcast(BF16).rearrange("p (b h t) -> p b h t", b=2, h=2)
        rqx = qt[:].rearrange("p b h t -> p b (h t)")
        wf = xw[:].rearrange("p w e -> p (w e)")[:, 0:2 * 2 * BLK * DB * DB].rearrange("p (s h k a d) -> p s h k a d", s=2, h=2, k=BLK, a=DB)

        x_loaded, w_loaded, enc_loaded = sem("x_loaded"), sem("w_loaded"), sem("enc_loaded")
        cleared, small_ready, gap_ready = sem("cleared"), sem("small_ready"), sem("gap_ready")
        wu_ps, wu_ev, ub_ps, ub_ev, wvo_ps, wvo_ev = map(sem, ("wu_ps", "wu_ev", "ub_ps", "ub_ev", "wvo_ps", "wvo_ev"))
        st0, mv0, lnv0, rstd0, xn0, xt_ps, xt_ev = map(sem, ("st0", "mv0", "lnv0", "rstd0", "xn0", "xt_ps", "xt_ev"))
        names = ("xc_ready xw_ps xw_ev q_ps u_ps k_ps q_ev u_ev k_ev rot_half rot_done s_ps s_masked mx_done sub_done "
                 "exp_done sum_done rec_done norm_done pt_ps pt_ev pv_ps ze_ev zo_ev y_ps x1_done").split()
        (xc_ready, xw_ps, xw_ev, q_ps, u_ps, k_ps, q_ev, u_ev, k_ev, rot_half, rot_done, s_ps, s_masked, mx_done, sub_done,
         exp_done, sum_done, rec_done, norm_done, pt_ps, pt_ev, pv_ps, ze_ev, zo_ev, y_ps, x1_done) = map(sem, names)
        ln = {k: {n: sem(f"{k}_{n}") for n in ("st", "mv", "lnv", "rstd", "xh", "t_ps", "t_ev")} for k in "fb"}
        names = "f_prev f_mix f_r_ps f_k_ps f_relu f_sq f_exp f_one f_sig f_v_ps f_gate f_out".split()
        f_prev, f_mix, f_r_ps, f_k_ps, f_relu, f_sq, f_exp, f_one, f_sig, f_v_ps, f_gate, f_out = map(sem, names)
        names = ("b_qkv_ps b_qkv b_min b_exp b_elu b_t1 b_t2 b_rot b_qk_t b_rq_t b_hi b_r1 b_mid b_lo b_rqt "
                 "parts_stored rq_stored").split()
        (b_qkv_ps, b_qkv, b_min, b_exp, b_elu, b_t1, b_t2, b_rot, b_qk_t, b_rq_t, b_hi, b_r1, b_mid, b_lo, b_rqt,
         parts_stored, rq_stored) = map(sem, names)
        names = "wf_done den_act ln_done r_act r_free item_ps item_done b_bias out_stored".split()
        (wf_done, den_act, ln_done, r_act, r_free, item_ps, item_done, b_bias, out_stored) = map(sem, names)
        stack_in, rqx_in, z_ev, g_done = ([sem(f"{n}{s}") for s in range(2)]
                                                  for n in ("stack_in", "rqx_in", "z_ev", "g_done"))

        loads = [(ident, "ident"), (wq, "wq"), (wk, "wk"), (wq_t, "wq_t"), (wv_t, "wv_t"), (wo, "wo"), (rel, "rel"),
                 (cb_pair, "cb_pair"), (cb_t, "cb_t"), (rb_t, "rb_t"), (brel, "brel"), (bo, "bo"), (bout, "bout"),
                 (wr_t, "wr_t"), (wk_t, "wk_t"), (wv2_t, "wv2_t"), (mu, "mu"), (wqkv, "wqkv"), (bqkv, "bqkv"),
                 (wout, "wout"), (sin_q, "sin_q"), (cos_q, "cos_q"), (mask, "mask"), (rot_cos, "rot_cos"),
                 (rot_sin, "rot_sin")]
        W_ALL = 16 * len(loads)

        def zh_view(v, par):
            return zh[:, par::2, 2 * v * SUB:(2 * v + 2) * SUB].rearrange("p g (w t) -> p w g t", w=2)

        def ln_dve(d, n, k, src):
            s = ln[k]
            d.memset(idle[:, 0:1], 0.0)
            for blk in range(CB):
                ins_ = d.bn_stats(stat[:, blk, :], src(blk))
            ins_.then_inc(s["st"], 1)
            d.wait_ge(s["st"], n + 1)
            d.memset(idle[:, 1:2], 0.0)
            for blk in range(CB):
                ins_ = d.bn_aggr(mv[:, blk, :], stat[:, blk, :])
            ins_.then_inc(s["mv"], 1)
            d.wait_ge(s["mv"], n + 1)
            d.wait_ge(s["rstd"], n + 1)
            for blk in range(CB):
                ins_ = d.tensor_scalar(xh[:, blk, :], src(blk), mv[:, blk, 0:1], rstd[:, blk:blk + 1], ALU.subtract, ALU.mult)
            ins_.then_inc(s["xh"], 1)

        def ln_act(a, n, k):
            s = ln[k]
            a.wait_ge(s["mv"], n + 1)
            a.activation(lnv[:, 0:CB], mv[:, 0:CB, 1], ACT.Ln, bias=eps[:, 0:1]).then_inc(s["lnv"], 1)
            a.wait_ge(s["lnv"], n + 1)
            a.activation(rstd[:, 0:CB], lnv[:, 0:CB], ACT.Exp, scale=-0.5).then_inc(s["rstd"], 1)

        def ffn_pe(t, n):
            t.wait_ge(ln["f"]["xh"], n + 1)
            t.wait_ge(f_exp, n + START)
            for blk in range(CB):
                mm = t.transpose(ps[:, 5, blk * P:(blk + 1) * P], xh[:, blk, :], ident[:])
            mm.then_inc(ln["f"]["t_ps"], 1)
            t.wait_ge(f_mix, n * 2 + 2)
            t.wait_ge(f_relu, n + START)
            t.matmul(ps[:, 6, :], wk_t[:], fmix[:, 1, :], start=True, stop=True).then_inc(f_k_ps, 1)
            t.wait_ge(ln["f"]["t_ev"], n + 1)
            for blk in range(CB):
                mm = t.matmul(ps[:, 5, blk * P:(blk + 1) * P], fmix[:, 0, blk * P:(blk + 1) * P], wr_t[:], start=True, stop=True)
            mm.then_inc(f_r_ps, 1)
            t.wait_ge(f_sq, n + 1)
            t.wait_ge(f_gate, n + START)
            for blk in range(CB):
                mm = t.matmul(ps[:, 7, blk * P:(blk + 1) * P], fk2[:, blk * P:(blk + 1) * P], wv2_t[:], start=True, stop=True)
            mm.then_inc(f_v_ps, 1)

        def ffn_act(a, n, b, hf):
            ln_act(a, n, "f")
            a.wait_ge(ln["f"]["t_ps"], n + 1)
            a.copy(fx[:, bass.ds(b, 1), bass.ds(hf * CH + 1, CH)].rearrange("p a t -> p (a t)"), ps[:, 5, :]).then_inc(ln["f"]["t_ev"], 1)
            a.wait_ge(f_k_ps, n + 1)
            a.activation(fk[:], ps[:, 6, :], ACT.Relu).then_inc(f_relu, 1)
            a.wait_ge(f_relu, n + 1 + START)
            a.wait_ge(f_v_ps, n + START)
            a.activation(fk2[:], fk[:], ACT.Square).then_inc(f_sq, 1)
            a.wait_ge(f_r_ps, n + 1)
            a.activation(fe[:], ps[:, 5, :], ACT.Exp, scale=-1.0).then_inc(f_exp, 1)

        def ffn_dve(d, n, b, hf, src, res, dst):
            ln_dve(d, n, "f", src)
            d.wait_ge(ln["f"]["t_ev"], n + 1)
            cur = fx[:, bass.ds(b, 1), bass.ds(hf * CH + 1, CH)].rearrange("p a t -> p (a t)")
            prev = fx[:, bass.ds(b, 1), bass.ds(hf * CH, CH)].rearrange("p a t -> p (a t)")
            for k in (1, 0):
                d.tensor_scalar(fprev[:, k, :], prev, mu_rest[:, k:k + 1], None, ALU.mult).then_inc(f_prev, 1)
            for m, k in enumerate((1, 0)):
                d.wait_ge(f_prev, n * 2 + m + 1)
                d.scalar_tensor_tensor(fmix[:, k, :], cur, mu[:, k:k + 1], fprev[:, k, :], ALU.mult, ALU.add).then_inc(f_mix, 1)
            d.wait_ge(f_exp, n + 1 + START)
            d.tensor_scalar(fs[:], fe[:], 1.0, None, ALU.add).then_inc(f_one, 1)
            d.wait_ge(f_one, n + 1)
            d.reciprocal(fo[:], fs[:]).then_inc(f_sig, 1)
            d.wait_ge(f_sig, n + 1)
            d.wait_ge(f_v_ps, n + 1 + START)
            d.tensor_tensor(fs[:], ps[:, 7, :], fo[:], ALU.mult).then_inc(f_gate, 1)
            d.wait_ge(f_gate, n + 1 + START)
            d.tensor_tensor(dst, fs[:].rearrange("p (k e) -> p k e", e=E), res, ALU.add).then_inc(f_out, 1)

        START, START_DMA = 1, 16
        RF = 5
        first = {
            "sp": (parts_stored, rq_stored, out_stored),
            "pool": (rot_done, norm_done, b_rot, g_done[0], g_done[1]),
            "pe": (s_ps, pt_ps, pv_ps, y_ps, k_ps, f_v_ps),
            "act": (q_ev, k_ev, pt_ev, b_rqt, b_hi, f_exp, f_relu, exp_done),
            "dve": (u_ev, x1_done, s_masked, b_qkv, b_r1, b_lo, f_gate),
        }

        def start(eng, name):
            for s in first[name]:
                eng.sem_inc(s, START_DMA if name == "sp" else START)
            if name == "pe":
                eng.sem_inc(r_free, RF)

        NI = NB * NP_ // 2
        ACT_LIST = [0, 1, 2, 4, 5, 6, 8, 9, 10, 12, 13, 15, 14]
        NA = len(ACT_LIST)
        ITEMS = [("U", 0), ("U", 1), ("U", 2), ("U", 3), ("O", 0), ("U", 4), ("U", 5), ("O", 1), ("U", 6)]
        PER = len(ITEMS)

        def turn_no(i, s):
            return 2 * i + s

        def items_of(it):
            if isinstance(it, int) and it == 0:
                return [x for x in ITEMS if x[0] == "U"], 0
            return ITEMS, it * PER - 2

        def before(i, s):
            return (i, 0) if s else (i - 1, 1)

        def if_any(eng, s, n):
            if not isinstance(n, int) or n > 0:
                eng.wait_ge(s, n)

        def turns(eng, body):
            for s in range(2):
                body(0, s)
            with eng.Fori(1, NI - 1) as i:
                for s in range(2):
                    body(i, s)
            for s in range(2):
                body(NI - 1, s)

        block = ctx.enter_context(nc.Block())

        @block.sync
        def _(sp):
            start(sp, "sp")
            sp.dma_start(x_tok[:], ins["x"]).then_inc(x_loaded, 16)
            for dst, name in loads:
                src = ins[name]
                sp.dma_start(dst[:] if not isinstance(dst, bass.AP) else dst, src).then_inc(w_loaded, 16)
            for buf in range(2):
                sp.dma_start(kt[D:P, buf, 0, :], ins["enc_k"]).then_inc(enc_loaded, 16)
                sp.dma_start(kt[0:D, buf, 1, :], ins["enc_k"]).then_inc(enc_loaded, 16)
            with sp.Fori(0, NB) as b:
                with sp.Fori(0, NT // CH) as hf:
                    c = b * 2 + hf
                    sp.wait_ge(b_lo, c * 2 + 2 + START)
                    for w in range(2):
                        sp.dma_start(split_dram[w, bass.ds(b, 1), :, :, bass.ds(hf * CH, CH)].rearrange("a s p t -> p (a s) t"),
                                     parts[:, w]).then_inc(parts_stored, 16)
                    sp.wait_ge(b_rqt, c + 1 + START)
                    sp.dma_start(rq_dram[bass.ds(b, 1), :, bass.ds(hf * CH, CH)].rearrange("a p t -> p (a t)"),
                                 rqt[:]).then_inc(rq_stored, 16)
            sp.wait_ge(parts_stored, 2 * 16 * NB * (NT // CH) + START_DMA)
            sp.wait_ge(rq_stored, 16 * NB * (NT // CH) + START_DMA)
            with sp.Fori(0, NI) as i:
                for s in range(2):
                    it = turn_no(i, s)
                    sp.wait_ge(r_free, (it - 1) * 4 + RF)
                    for h in range(2):
                        b, row = it // NP_, ((it % NP_) * 2 + h) * DB
                        for side, dst in ((0, qs), (1, ks)):
                            src = split_dram[side, bass.ds(b, 1), :, bass.ds(row, DB), :].rearrange("a s p t -> (a s) p t")
                            src = src.unsqueeze(1 - side).broadcast_to([PARTS, PARTS, DB, NT])
                            for part in range(PARTS):
                                sp.dma_start(dst[part * PARTS * DB:(part + 1) * PARTS * DB, s, h, :],
                                             src[part]).then_inc(stack_in[s], 16)
                    sp.wait_ge(g_done[s], i + START)
                    src = rq_dram[bass.ds(it // NP_, 1), bass.ds((it % NP_) * 16, 16), :].rearrange("a p t -> (a p) t")
                    sp.dma_start(rqx[:, s, :], src.unsqueeze(1).broadcast_to([16, DB, NT])).then_inc(rqx_in[s], 16)
            with sp.Fori(0, NB * NT // CH) as n:
                sp.wait_ge(f_out, n + 5)
                sp.dma_start(out_dram[bass.ds(n, 1)].rearrange("a p k e -> p (a k) e"), x_out[:]).then_inc(out_stored, 16)
            sp.wait_ge(out_stored, 16 * NB * (NT // CH) + START_DMA)

        @block.gpsimd
        def _(pool):
            g = nc.gpsimd
            start(g, "pool")
            g.memset(xT[:, :, 0:EDGE], 0.0).then_inc(cleared, 1)
            g.memset(xT[:, :, EDGE + NT:], 0.0).then_inc(cleared, 1)
            g.memset(fx[:, :, 0:1], 0.0).then_inc(cleared, 1)
            g.memset(ones[:], 1.0).then_inc(cleared, 1)
            g.wait_ge(cleared, 4)
            with g.Fori(0, NB) as b:
                with g.Fori(0, NT // CH) as hf:
                    c = b * 2 + hf

                    def rot_add(p):
                        g.wait_ge(u_ev, c * NP_ + p + 1 + START)
                        if p >= 2:
                            g.wait_ge(s_ps, c * NP_ + p - 1 + START)
                        else:
                            g.wait_ge(s_ps, c * NP_ + START)
                        if p == 1:
                            g.wait_ge(rot_done, c * NP_ + 1 + START)
                        elif p >= 2:
                            g.wait_ge(sub_done, c * NP_ + p - 1)
                        g.tensor_tensor(qt[D:P, p % 2, 0, :], turn[D:P, p % 2, 0, :], turn[D:P, p % 2, 1, :],
                                        ALU.add).then_inc(rot_half, 1)
                        g.wait_ge(rot_half, c * NP_ + p + 1)
                        g.tensor_tensor(qt[0:D, p % 2, 1, :], turn[0:D, p % 2, 0, :], turn[0:D, p % 2, 1, :],
                                        ALU.add).then_inc(rot_done, 1)

                    def sub_max(p):
                        v = sm[:, p % 2].rearrange("p k h w -> p (k h) w")
                        g.wait_ge(mx_done, c * NP_ + p + 1)
                        g.wait_ge(rot_done, c * NP_ + min(p + 2, NP_) + START)
                        g.tensor_tensor(v, v, mx[:, p % 2].unsqueeze(2).broadcast_to([P, CB * 2, WIN]),
                                        ALU.subtract).then_inc(sub_done, 1)

                    def norm(p):
                        v = pr[:, p % 2].rearrange("p k h w -> p (k h) w")
                        g.wait_ge(rec_done, c * NP_ + p + 1)
                        g.wait_ge(rot_done, c * NP_ + min(p + 3, NP_) + START)
                        g.tensor_tensor(v, v, rtot[:, p % 2].unsqueeze(2).broadcast_to([P, CB * 2, WIN]),
                                        ALU.mult).then_inc(norm_done, 1)

                    g.wait_ge(b_rot, c + START)
                    rot_add(0)
                    for p in range(NP_ + 1):
                        if p >= 1:
                            sub_max(p - 1)
                        if p + 1 < NP_:
                            rot_add(p + 1)
                        if p >= 1:
                            norm(p - 1)
                    g.wait_ge(b_elu, c + 1)
                    blocks = bass.ds(hf * CB, CB)
                    src = qkv[:].rearrange("p k (h d) -> p k h d", d=DB)
                    t1 = fmix[:].rearrange("p a (k n) -> p (a k n)", k=2).rearrange("p (k h d) -> p k h d", k=CB, d=DB)
                    t2 = fprev[:].rearrange("p a (k n) -> p (a k n)", k=2).rearrange("p (k h d) -> p k h d", k=CB, d=DB)
                    NH2 = 2 * HB
                    wide = lambda t, lo: t.unsqueeze(2).broadcast_to([P, CB, NH2, lo])
                    g.tensor_tensor(t1, src, wide(rot_cos[:, blocks, :], DB), ALU.mult).then_inc(b_t1, 1)
                    for odd in range(2):
                        ins_ = g.tensor_tensor(t2[:, :, :, odd::2], src[:, :, :, 1 - odd::2],
                                               wide(rot_sin[:, blocks, odd::2], DB // 2), ALU.mult)
                    ins_.then_inc(b_t2, 1)
                    g.wait_ge(b_t1, c + 1)
                    g.wait_ge(b_t2, c + 1)
                    g.tensor_tensor(rq[:].rearrange("p k (h d) -> p k h d", d=DB), t1[:, :, 0:HB], t2[:, :, 0:HB], ALU.add)
                    g.tensor_tensor(rk[:, bass.ds(c * CB, CB), :].rearrange("p k (h d) -> p k h d", d=DB),
                                    t1[:, :, HB:], t2[:, :, HB:], ALU.add).then_inc(b_rot, 1)
            g.wait_ge(b_rot, NB * (NT // CH) + START)
            g.wait_ge(b_qkv, NB * (NT // CH) + START)
            def features(i, s):
                b, p = turn_no(i, s) // NP_, turn_no(i, s) % NP_
                for h in range(2):
                    at, keys = bass.ds((2 * p + h) * DB, DB), bass.ds(b * BLK, BLK)
                    ins_ = g.tensor_tensor(wf[:, s, h], rk[:, keys, at].unsqueeze(3).broadcast_to([P, BLK, DB, DB]),
                                           v_tok[:, keys, at].unsqueeze(2).broadcast_to([P, BLK, DB, DB]), ALU.mult)
                ins_.then_inc(wf_done, 1)

            def gather(i, s):
                it = turn_no(i, s)
                g.wait_ge(z_ev[s], i + 1)
                g.wait_ge(rqx_in[s], (i + 1) * 16)
                if not isinstance(i, int) or i > 0:
                    g.wait_ge(item_ps, it * PER - 2 - PER + 8)
                g.tensor_tensor(g_sb[:, s, :], z_sb[:, s, :], rqx[:, s, :], ALU.mult).then_inc(g_done[s], 1)
                if not isinstance(i, int) or i < NI - 1:
                    g.wait_ge(r_free, (it + 1) * 4 + RF)
                    features(i + 1, s)

            features(0, 0)
            features(0, 1)
            turns(g, gather)

        @block.tensor
        def _(pe):
            t = nc.tensor
            start(t, "pe")
            t.wait_ge(w_loaded, W_ALL)
            for k in range(4):
                for q4 in range(4):
                    p, slot = 2 * k + q4 // 2, q4 % 2
                    mm = t.matmul(ps[:, k, q4 * P:(q4 + 1) * P], wq_t[:, 2 * p + 1 - slot, :], rel[:, D:3 * D],
                                  start=True, stop=True)
                mm.then_inc(wu_ps, 1)
            t.matmul(ps[:, 4, 0:H], rel[:, 0:2 * D], rb_t[:], start=True, stop=True)
            t.matmul(ps[:, 4, H:2 * H], rel[:, 2 * D:4 * D], rb_t[:], start=True, stop=True).then_inc(ub_ps, 1)
            t.wait_ge(gap_ready, 2)
            t.matmul(ps[:, 5, 0:H], brel_wide[:], bias_gap[:], start=True, stop=True).then_inc(ub_ps, 1)
            for k in range(4):
                if k < 2:
                    bank = 6 + k
                else:
                    bank = k - 2
                    t.wait_ge(wu_ev, k - 1)
                for q4 in range(4):
                    h = 4 * k + q4
                    mm = t.matmul(ps[:, bank, q4 * P:(q4 + 1) * P], wv_t[:, h, :], wo[:, h, :], start=True, stop=True)
                mm.then_inc(wvo_ps, 1)
            for k in range(4):
                if k < 2:
                    t.wait_ge(wu_ev, k + 3)
                else:
                    t.wait_ge(ub_ev, k)
                t.wait_ge(xn0, k // 2 + 1)
                for q4 in range(4):
                    mm = t.transpose(ps[:, 2 + k, q4 * P:(q4 + 1) * P], xn[:, 4 * k + q4, :], ident[:])
                mm.then_inc(xt_ps, 1)
            t.wait_ge(enc_loaded, 64)
            t.wait_ge(cleared, 4)
            t.wait_ge(wvo_ev, 4)
            t.wait_ge(xt_ev, 4)

            with t.Fori(0, NB) as b:
                with t.Fori(0, NT // CH) as hf:
                    c = b * 2 + hf

                    def proj(p):
                        t.wait_ge(q_ev, c * NP_ + p + START)
                        t.matmul(ps[:, 0, :], wq[:, p * P:(p + 1) * P], xc[:, EDGE:EDGE + CH], start=True, stop=True).then_inc(q_ps, 1)
                        t.wait_ge(u_ev, c * NP_ + p + START)
                        for k in range(2):
                            mm = t.matmul(ps[:, 1 + k, :], wu[:, k, p].rearrange("p a d -> p (a d)"), xc[:, EDGE:EDGE + CH],
                                          start=True, stop=True)
                        mm.then_inc(u_ps, 1)
                        t.wait_ge(k_ev, c * NP_ + p + START)
                        for k in range(2):
                            mm = t.matmul(ps[:, 3 + k, 0:KH], wk[:, p * P:(p + 1) * P], xc[:, SIDE + k * KH:SIDE + (k + 1) * KH],
                                          start=True, stop=True)
                        mm.then_inc(k_ps, 1)

                    def scores(p):
                        t.wait_ge(q_ev, c * NP_ + p + 1 + START)
                        t.wait_ge(k_ev, c * NP_ + p + 1 + START)
                        t.wait_ge(rot_done, c * NP_ + p + 1 + START)
                        t.wait_ge(s_masked, c * NP_ + max(p - 1, 0) + START)
                        for blk in range(CB):
                            for par in range(2):
                                for j in range(P // SUB):
                                    q0 = blk * P + j * SUB
                                    mm = t.matmul(ps[j * SUB:(j + 1) * SUB, 5 + p % 2, (blk * 2 + par) * WIN:(blk * 2 + par + 1) * WIN],
                                                  qt[:, p % 2, par, q0:q0 + SUB], kt[:, p % 2, par, q0:q0 + WIN],
                                                  start=True, stop=True)
                        mm.then_inc(s_ps, 1)

                    def turn_probs(p):
                        t.wait_ge(norm_done, c * NP_ + p + 1 + START)
                        t.wait_ge(pt_ev, c * NP_ + p + START)
                        for blk in range(CB):
                            mm = t.transpose(ps[:, 7, blk * P:(blk + 1) * P], pr[:, p % 2, blk].rearrange("p h w -> p (h w)"), ident[:])
                        mm.then_inc(pt_ps, 1)

                    def values_out(blk):
                        t.wait_ge(ze_ev, c * 8 + 2 * blk + 2)
                        t.wait_ge(zo_ev, c * 8 + 2 * blk + 2)
                        dst = ps[:, 4, blk * P:(blk + 1) * P]
                        for h in range(H):
                            t.matmul(dst, zh[:, h, blk * P:(blk + 1) * P], wvo[:, h, :], start=(h == 0), stop=False)
                        mm = t.matmul(dst, ones[:], bo[:], start=False, stop=True)
                        if blk == CB - 1:
                            mm.then_inc(y_ps, 1)

                    t.wait_ge(xc_ready, c + 1)
                    t.wait_ge(b_qkv, c + START)
                    t.wait_ge(x1_done, c + START)
                    for k in range(NX):
                        mm = t.transpose(ps[:, k // 4, (k % 4) * P:(k % 4 + 1) * P], xc[:, k * SUB:k * SUB + P], ident[:])
                        if k % 4 == 3 or k == NX - 1:
                            mm.then_inc(xw_ps, 1)
                    t.wait_ge(xw_ev, c * 5 + 5)
                    t.wait_ge(b_rqt, c + START)
                    t.wait_ge(b_hi, 2 * c + START)
                    t.wait_ge(b_r1, 2 * c + START)
                    proj(0)
                    for p in range(NP_):
                        if p + 1 < NP_:
                            proj(p + 1)
                        if p >= 2:
                            turn_probs(p - 2)
                        scores(p)
                    turn_probs(NP_ - 2)
                    turn_probs(NP_ - 1)
                    t.wait_ge(pt_ev, c * NP_ + NP_ + START)
                    t.wait_ge(q_ev, c * NP_ + NP_ + START)
                    t.wait_ge(u_ev, c * NP_ + NP_ + START)
                    t.wait_ge(k_ev, c * NP_ + NP_ + START)
                    for v in range(NW // 2):
                        for par in range(2):
                            if v >= 2:
                                t.wait_ge(zo_ev if par else ze_ev, c * 8 + v - 1)
                            rows = slice(D * par, D * par + WIN)
                            for w2 in range(2):
                                w = 2 * v + w2
                                mm = t.matmul(ps[:, 2 * (v % 2) + par, w2 * 256:(w2 + 1) * 256].rearrange("p (g t) -> p g t", g=NP_),
                                              xw[rows, w + 2 * (1 - par), :], pt[rows, :, w * SUB:(w + 1) * SUB], start=True, stop=True)
                            mm.then_inc(pv_ps, 1)
                        if v % 2 and v > 1:
                            values_out(v // 2 - 1)
                    values_out(CB - 1)
                    ffn_pe(t, c)
                    t.wait_ge(ln["b"]["xh"], c + 1)
                    t.wait_ge(ln["f"]["t_ev"], c + 1)
                    t.wait_ge(f_exp, c + 1 + START)
                    for blk in range(CB):
                        mm = t.transpose(ps[:, 5, blk * P:(blk + 1) * P], xh[:, blk, :], ident[:])
                    mm.then_inc(ln["b"]["t_ps"], 1)
                    t.wait_ge(ln["b"]["t_ev"], c + 1)
                    for blk in range(CB):
                        mm = t.matmul(ps[:, blk, 0:3 * E], x3t[:, blk * P:(blk + 1) * P], wqkv[:], start=True, stop=True)
                    mm.then_inc(b_qkv_ps, 1)
                    t.wait_ge(b_elu, c + 1)
                    for side in range(2):
                        for blk in range(CB):
                            mm = t.transpose(ps[:, 6 + side, blk * P:(blk + 1) * P], qkv[:, blk, side * E:(side + 1) * E], ident[:])
                        mm.then_inc(b_qk_t, 1)
                    t.wait_ge(b_rot, c + 1 + START)
                    for blk in range(CB):
                        mm = t.transpose(ps[:, 5, blk * P:(blk + 1) * P], rq[:, blk, :], ident[:])
                    mm.then_inc(b_rq_t, 1)

            t.wait_ge(b_rqt, 4 + START)
            t.wait_ge(b_r1, 8 + START)

            def den(s, gi, ih, bank):
                h, jb = gi % 2, gi // 2
                return t.matmul(ps[:, bank, :], ks[0:KROWS, s, h, jb * P:(jb + 1) * P],
                                qs[0:KROWS, s, h, ih * 512:(ih + 1) * 512], start=True, stop=True)

            def den_a(i, s, n):
                no = turn_no(i, s) * NA + n
                bank = 2 * ((s * NA + n) % 2)
                if_any(t, ln_done, no - 1)
                gi = ACT_LIST[n]
                if gi == 15:
                    mm = den(s, gi, 1, bank)
                else:
                    den(s, gi, 0, bank)
                    mm = den(s, gi, 1, bank + 1)
                mm.then_inc(den_act, 1)

            def output(i, s, j, bank):
                t.wait_ge(g_done[s], i + 1 + START)
                p = turn_no(i, s) % NP_
                for blk in range(CB):
                    at = (j * CB + blk) * P
                    mm = t.matmul(ps[:, bank, blk * P:(blk + 1) * P], g_sb[:, s, at:at + P],
                                  wout[:, bass.ds(p, 1), :].rearrange("p a e -> p (a e)"), start=True, stop=True)
                return mm

            def item(i, s, k):
                items, base = items_of(turn_no(i, s))
                kind, j = items[k]
                bank = 4 + (s + k) % 2
                if_any(t, item_done, base + k - 1)
                if kind == "U":
                    mm = den(s, 4 * (j // 2) + 3, j % 2, bank)
                else:
                    mm = output(*before(i, s), j, bank)
                mm.then_inc(item_ps, 1)

            def items(i, s, names):
                lst, _ = items_of(turn_no(i, s))
                for x in names:
                    if x in lst:
                        item(i, s, lst.index(x))

            def z(i, s, jb, ih):
                it, m = turn_no(i, s), jb // 2
                t.wait_ge(r_act, it * NA + 3 * m + (2 if jb % 2 == 0 else 3 if m < 3 else 4))
                if jb % 2:
                    lst, base = items_of(it)
                    t.wait_ge(item_done, base + lst.index(("U", 2 * m + ih if m < 3 else 6)) + 1)
                for h in range(2):
                    mm = t.matmul(ps[D * h:D * (h + 1), 6 + ih, :], wf[:, s, h, jb].rearrange("p a d -> p (a d)"),
                                  r_buf[:, 4 * (m % 2) + 2 * (jb % 2) + h, ih * 512:(ih + 1) * 512],
                                  start=(jb == 0), stop=(jb == BLK - 1))
                return mm

            ORDER = ["u a a z z u a z z", "u u a a z z u a z z", "u a a z z u a z z a", "u a a z z u a z z"]

            def next_turn(i, s):
                return (i, 1) if s == 0 else (i + 1, 0)

            def turn_pe(i, s):
                it = turn_no(i, s)
                more = s == 0 or not isinstance(i, int) or i < NI - 1
                lst, _ = items_of(it)
                ahead_a = [(i, s, n) for n in range(3, NA)] + ([(*next_turn(i, s), n) for n in range(3)] if more else [])
                ahead_u = [(i, s, k) for k in range(2, len(lst))] + ([(*next_turn(i, s), k) for k in range(2)] if more else [])
                done, waited = 0, False
                for m in range(4):
                    for x in ORDER[m].split():
                        if x in ("a", "u"):
                            if not {"a": ahead_a, "u": ahead_u}[x]:
                                continue
                            which = {"a": ahead_a, "u": ahead_u}[x].pop(0)
                            if which[1] != s and not waited:
                                t.wait_ge(stack_in[which[1]], (which[0] + 1) * 192)
                                waited = True
                            {"a": den_a, "u": item}[x](*which)
                        elif x == "z":
                            if done == 0:
                                t.wait_ge(wf_done, it + 1)
                                pi, ps_ = before(i, s)
                                if_any(t, z_ev[ps_], pi + 1)
                            mm = z(i, s, done // 2, done % 2)
                            done += 1
                            if done % 4 == 0:
                                mm.then_inc(r_free, 1)

            t.wait_ge(stack_in[0], 192)
            items(0, 0, [("U", 0)])
            den_a(0, 0, 0)
            den_a(0, 0, 1)
            items(0, 0, [("U", 1)])
            den_a(0, 0, 2)
            turns(t, turn_pe)
            for j in range(2):
                t.wait_ge(item_done, NB * NP_ * PER - 2 + j - 1)
                output(NI - 1, 1, j, 4 + j).then_inc(item_ps, 1)
            with t.Fori(0, NB * NT // CH) as n:
                ffn_pe(t, n + 4)

        @block.scalar
        def _(act):
            a = nc.scalar
            start(a, "act")
            a.preload_act_table_set("natural_log_exp_and_others")
            for k in range(4):
                a.wait_ge(wu_ps, k + 1)
                src = ps[:, k, :].rearrange("p (g s w d) -> p g s w d", g=2, s=2, w=2)
                for w in range(2):
                    ins_ = a.copy(wu[:, w, 2 * k:2 * k + 2], src[:, :, :, w, :])
                ins_.then_inc(wu_ev, 1)
            a.wait_ge(mv0, 1)
            a.activation(lnv[:], mv[:, :, 1], ACT.Ln, bias=eps[:, 0:1]).then_inc(lnv0, 1)
            a.wait_ge(lnv0, 1)
            a.activation(rstd[:], lnv[:], ACT.Exp, scale=-0.5).then_inc(rstd0, 1)
            for k in range(4):
                a.wait_ge(wvo_ps, k + 1)
                bank = 6 + k if k < 2 else k - 2
                a.copy(wvo[:, 4 * k:4 * k + 4, :], ps[:, bank, :].rearrange("p (h e) -> p h e", h=4)).then_inc(wvo_ev, 1)
            for k in range(4):
                a.wait_ge(xt_ps, k + 1)
                a.copy(xT[:, k // 2, EDGE + CH * (k % 2):EDGE + CH * (k % 2 + 1)], ps[:, 2 + k, :]).then_inc(xt_ev, 1)
            with a.Fori(0, NB) as b:
                with a.Fori(0, NT // CH) as hf:
                    c = b * 2 + hf

                    def evac_proj(p):
                        a.wait_ge(q_ps, c * NP_ + p + 1)
                        a.wait_ge(s_ps, c * NP_ + max(p - 1, 0) + START)
                        a.activation(qt[0:D, p % 2, 0, :], ps[0:D, 0, :], ACT.Identity, bias=cb_pair[0:D, p:p + 1])
                        a.activation(qt[D:P, p % 2, 1, :], ps[D:P, 0, :], ACT.Identity, bias=cb_pair[D:P, p:p + 1]).then_inc(q_ev, 1)
                        a.wait_ge(k_ps, c * NP_ + p + 1 + START)
                        for par in range(2):
                            rows = slice(D * par, D * par + D)
                            ins_ = a.activation(kt[rows, p % 2, par, :].rearrange("p (a t) -> p a t", a=2), ps[rows, 3:5, 0:KH],
                                                ACT.Identity, bias=brel[rows, 0:1])
                        ins_.then_inc(k_ev, 1)

                    def exp_s(p):
                        a.wait_ge(sub_done, c * NP_ + p + 1)
                        a.wait_ge(pt_ps, c * NP_ + max(p - 1, 0) + START)
                        a.activation(pr[:, p % 2], sm[:, p % 2], ACT.Exp, scale=SCALE).then_inc(exp_done, 1)

                    def evac_probs(p):
                        a.wait_ge(pt_ps, c * NP_ + p + 1 + START)
                        if p == 0:
                            a.wait_ge(rq_stored, c * 16 + START_DMA)
                            a.wait_ge(b_rot, c + START)
                            a.wait_ge(b_lo, c * 2 + START)
                        a.copy(pt[:, p, :], ps[:, 7, :]).then_inc(pt_ev, 1)

                    for k in range(5):
                        a.wait_ge(xw_ps, c * 5 + k + 1)
                        a.wait_ge(pv_ps, c * 16 + START)
                        n = min(4, NX - 4 * k)
                        a.copy(xw[:, 4 * k:4 * k + n, :], ps[:, k, 0:n * E].rearrange("p (w e) -> p w e", w=n)).then_inc(xw_ev, 1)
                    evac_proj(0)
                    for p in range(NP_ + 1):
                        if p >= 1:
                            exp_s(p - 1)
                        if p + 1 < NP_:
                            evac_proj(p + 1)
                        if p >= 2:
                            evac_probs(p - 2)
                    evac_probs(NP_ - 1)
                    for v in range(NW // 2):
                        a.wait_ge(pv_ps, c * 16 + 2 * v + 1 + START)
                        a.wait_ge(y_ps, c + START)
                        a.copy(zh_view(v, 0), ps[:, 2 * (v % 2), :].rearrange("p (w g t) -> p w g t", w=2, g=NP_)).then_inc(ze_ev, 1)
                    ffn_act(a, c, b, hf)
                    ln_act(a, c, "b")
                    a.wait_ge(ln["b"]["t_ps"], c + 1)
                    a.copy(x3t[:], ps[:, 5, :]).then_inc(ln["b"]["t_ev"], 1)
                    a.wait_ge(b_min, c + 1)
                    a.activation(qk_neg[:], qk_neg[:], ACT.Exp).then_inc(b_exp, 1)
                    a.wait_ge(parts_stored, c * 32 + START_DMA)
                    for side in range(2):
                        a.wait_ge(b_qk_t, c * 2 + side + 1)
                        a.copy(parts[:, side, 0, :], ps[:, 6 + side, :]).then_inc(b_hi, 1)
                    for side in range(2):
                        a.wait_ge(b_r1, c * 2 + side + 1 + START)
                        a.copy(parts[:, side, 1, :], rest[:, side, :]).then_inc(b_mid, 1)
                    a.wait_ge(b_rq_t, c + 1)
                    a.wait_ge(rq_stored, c * 16 + START_DMA)
                    a.copy(rqt[:], ps[:, 5, :]).then_inc(b_rqt, 1)

            def parts_of(s, n):
                k = (s * NA + n) % 2
                gi = ACT_LIST[n]
                r = r_buf[:, gi % 8, :]
                if gi == 15:
                    return ps[:, 2 * k, :], r[:, 512:1024]
                return ps[:, 2 * k:2 * k + 2, :].rearrange("p a t -> p (a t)"), r

            def log(i, s, n):
                no = turn_no(i, s) * NA + n
                src, dst = parts_of(s, n)
                a.wait_ge(den_act, no + 1)
                a.wait_ge(r_free, turn_no(i, s) * 4 + ACT_LIST[n] // 4 - 1 + RF)
                a.activation(dst, src, ACT.Ln).then_inc(ln_done, 1)

            def inv(i, s, n):
                no = turn_no(i, s) * NA + n
                _, dst = parts_of(s, n)
                a.wait_ge(ln_done, no + 1)
                a.activation(dst, dst, ACT.Exp, scale=-1.0).then_inc(r_act, 1)

            def copy_sums(i, s):
                a.wait_ge(r_free, (turn_no(i, s) + 1) * 4 + RF)
                a.wait_ge(g_done[s], i + START)
                a.copy(z_sb[:, s, :], ps[:, 6:8, :].rearrange("p a t -> p (a t)")).then_inc(z_ev[s], 1)

            def turn_act(i, s):
                last = isinstance(i, int) and i == NI - 1 and s == 1
                for n in range(NA):
                    if n + 1 < NA:
                        log(i, s, n + 1)
                    elif not last:
                        log(*((i, 1) if s == 0 else (i + 1, 0)), 0)
                    inv(i, s, n)
                    if n == 1 and not (isinstance(i, int) and i == 0 and s == 0):
                        copy_sums(*before(i, s))

            log(0, 0, 0)
            turns(a, turn_act)
            copy_sums(NI - 1, 1)
            with a.Fori(0, NB) as b:
                with a.Fori(0, NT // CH) as hf:
                    ffn_act(a, b * 2 + hf + 4, b, hf)

        @block.vector
        def _(dve):
            d = nc.vector
            start(d, "dve")
            d.memset(eps[:], EPS).then_inc(small_ready, 1)
            d.wait_ge(x_loaded, 16)
            for k in range(NB * BLK):
                ins_ = d.bn_stats(stat[:, k, :], x_tok[:, k, :])
            ins_.then_inc(st0, 1)
            d.wait_ge(st0, 1)
            d.wait_ge(small_ready, 1)
            for k in range(NB * BLK):
                ins_ = d.bn_aggr(mv[:, k, :], stat[:, k, :])
            ins_.then_inc(mv0, 1)
            d.wait_ge(w_loaded, W_ALL)
            d.tensor_tensor(bias_gap[:], rb_t[:], cb_t[:], ALU.subtract).then_inc(gap_ready, 1)
            d.tensor_copy(brel_wide[:], brel[0:D, 0:1].broadcast_to([D, P])).then_inc(gap_ready, 1)
            d.tensor_scalar(mu_rest[:], mu[:], -1.0, 1.0, ALU.mult, ALU.add).then_inc(small_ready, 1)
            d.wait_ge(ub_ps, 1)
            for w in range(2):
                src = ps[:, 4, w * H:(w + 1) * H].rearrange("p (g two) -> p g two", two=2)
                d.tensor_copy(u_bias[0:D, w, :], src[0:D, :, 1])
                ins_ = d.tensor_copy(u_bias[D:P, w, :], src[D:P, :, 0])
            ins_.then_inc(ub_ev, 2)
            d.wait_ge(ub_ps, 2)
            d.tensor_copy(head_const[:], ps[:, 5, 0:H]).then_inc(ub_ev, 1)
            d.wait_ge(rstd0, 1)
            for k in range(NB * BLK):
                ins_ = d.tensor_scalar(xn[:, k, :], x_tok[:, k, :], mv[:, k, 0:1], rstd[:, k:k + 1], ALU.subtract, ALU.mult)
                if k % 8 == 7:
                    ins_.then_inc(xn0, 1)
            d.wait_ge(ub_ev, 3)
            d.wait_ge(small_ready, 2)
            d.wait_ge(cleared, 4)
            d.wait_ge(xt_ev, 4)
            with d.Fori(0, NB) as b:
                with d.Fori(0, NT // CH) as hf:
                    c = b * 2 + hf

                    def rotate(p):
                        d.wait_ge(u_ps, c * NP_ + p + 1)
                        d.wait_ge(rot_done, c * NP_ + max(p - 1, 0) + START)
                        d.scalar_tensor_tensor(turn[:, p % 2, 0, :], ps[:, 1, :], u_bias[:, 0, p:p + 1], sin_q[:], ALU.add, ALU.mult)
                        d.scalar_tensor_tensor(turn[:, p % 2, 1, :], ps[:, 2, :], u_bias[:, 1, p:p + 1], cos_q[:],
                                               ALU.add, ALU.mult).then_inc(u_ev, 1)

                    def mask_max(p):
                        d.wait_ge(s_ps, c * NP_ + p + 1 + START)
                        d.wait_ge(exp_done, c * NP_ + max(p - 1, 0) + START)
                        src = ps[:, 5 + p % 2, :].rearrange("p (k h w) -> p k h w", h=2, w=WIN)
                        for par in range(2):
                            ins_ = d.scalar_tensor_tensor(sm[:, p % 2, :, par, :], src[:, :, par, :], head_const[:, 2 * p + par:2 * p + par + 1],
                                                          mask[:, bass.ds(hf, 1)].rearrange("p a k w -> p (a k) w"), ALU.add, ALU.add)
                        ins_.then_inc(s_masked, 1)
                        d.wait_ge(s_masked, c * NP_ + p + 1 + START)
                        d.tensor_reduce(mx[:, p % 2, :], sm[:, p % 2].rearrange("p k h w -> p (k h) w"), AX.X, ALU.max).then_inc(mx_done, 1)

                    def total(p):
                        d.wait_ge(exp_done, c * NP_ + p + 1 + START)
                        d.tensor_reduce(tot[:, p % 2, :], pr[:, p % 2].rearrange("p k h w -> p (k h) w"), AX.X, ALU.add).then_inc(sum_done, 1)
                        d.wait_ge(sum_done, c * NP_ + p + 1)
                        d.wait_ge(norm_done, c * NP_ + max(p - 1, 0) + START)
                        d.reciprocal(rtot[:, p % 2, :], tot[:, p % 2, :]).then_inc(rec_done, 1)

                    d.wait_ge(k_ps, c * NP_ + START)
                    d.tensor_copy(xc[:], xT[:, bass.ds(b, 1), bass.ds(hf * CH, XC)].rearrange("p a t -> p (a t)")).then_inc(xc_ready, 1)
                    rotate(0)
                    for p in range(NP_ + 1):
                        if p + 1 < NP_:
                            rotate(p + 1)
                        if p >= 1:
                            total(p - 1)
                        if p < NP_:
                            mask_max(p)
                    for v in range(NW // 2):
                        d.wait_ge(pv_ps, c * 16 + 2 * v + 2 + START)
                        d.wait_ge(y_ps, c + START)
                        d.tensor_copy(zh_view(v, 1), ps[:, 2 * (v % 2) + 1, :].rearrange("p (w g t) -> p w g t", w=2, g=NP_)).then_inc(zo_ev, 1)
                    d.wait_ge(y_ps, c + 1 + START)
                    d.tensor_tensor(x1[:], ps[:, 4, :].rearrange("p (k e) -> p k e", e=E), x_tok[:, bass.ds(c * CB, CB), :],
                                    ALU.add).then_inc(x1_done, 1)
                    d.wait_ge(x1_done, c + 1 + START)
                    ffn_dve(d, c, b, hf, lambda k: x1[:, k, :], x1[:], x_mid[:, bass.ds(c * CB, CB), :])
                    d.wait_ge(f_out, c + 1)
                    ln_dve(d, c, "b", lambda k: x_mid[:, bass.ds(c * CB + k, 1), :].rearrange("p a e -> p (a e)"))
                    d.wait_ge(ln["b"]["xh"], c + 1)
                    x_c = x_mid[:, bass.ds(c * CB, CB), :]
                    d.tensor_tensor(x_c, x_c, bout[:].unsqueeze(1).broadcast_to([P, CB, E]), ALU.add).then_inc(b_bias, 1)
                    d.wait_ge(b_qkv_ps, c + 1)
                    bias = lambda lo, hi: bqkv[:, lo:hi].unsqueeze(1).broadcast_to([P, CB, hi - lo])
                    d.tensor_tensor(qkv[:], ps[:, 0:CB, 0:2 * E], bias(0, 2 * E), ALU.add)
                    d.tensor_tensor(v_tok[:, bass.ds(c * CB, CB), :], ps[:, 0:CB, 2 * E:3 * E], bias(2 * E, 3 * E), ALU.add).then_inc(b_qkv, 1)
                    d.wait_ge(b_qkv, c + 1 + START)
                    d.tensor_scalar(qk_neg[:], qkv[:], 0.0, None, ALU.min).then_inc(b_min, 1)
                    d.wait_ge(b_exp, c + 1)
                    d.scalar_tensor_tensor(qkv[:].rearrange("p k n -> p (k n)"), qkv[:].rearrange("p k n -> p (k n)"), 0.0,
                                           qk_neg[:].rearrange("p k n -> p (k n)"), ALU.max, ALU.add).then_inc(b_elu, 1)
                    for side in range(2):
                        d.wait_ge(b_hi, c * 2 + side + 1 + START)
                        d.tensor_tensor(rest[:, side, :], ps[:, 6 + side, :], parts[:, side, 0, :], ALU.subtract).then_inc(b_r1, 1)
                    for side in range(2):
                        d.wait_ge(b_mid, c * 2 + side + 1)
                        d.wait_ge(b_r1, c * 2 + side + 1 + START)
                        d.tensor_tensor(parts[:, side, 2, :], rest[:, side, :], parts[:, side, 1, :], ALU.subtract).then_inc(b_lo, 1)
            def take(i, s, k):
                it = turn_no(i, s)
                lst, base = items_of(it)
                kind, j = lst[k]
                bank = 4 + (s + k) % 2
                if kind == "U":
                    m = j // 2
                    d.wait_ge(r_free, it * 4 + m - 1 + RF)
                    d.wait_ge(item_ps, base + k + 1)
                    d.reciprocal(r_buf[:, (4 * m + 3) % 8, (j % 2) * 512:(j % 2 + 1) * 512], ps[:, bank, :]).then_inc(item_done, 1)
                else:
                    b = turn_no(*before(i, s)) // NP_
                    at = x_mid[:, bass.ds(b * BLK + j * CB, CB), :]
                    d.wait_ge(item_ps, base + k + 1)
                    if_any(d, item_done, base + k + 1 - PER + (1 if isinstance(it, int) and it <= 1 else 0))
                    d.tensor_tensor(at, ps[:, bank, :].rearrange("p (k e) -> p k e", e=E), at, ALU.add).then_inc(item_done, 1)

            def turn_dve(i, s):
                for k in range(len(items_of(turn_no(i, s))[0])):
                    take(i, s, k)

            d.wait_ge(b_bias, NB * (NT // CH))
            turns(d, turn_dve)
            total = NB * NP_ * PER - 2
            for j in range(2):
                b = NB - 1
                at = x_mid[:, b * BLK + j * CB:b * BLK + (j + 1) * CB, :]
                d.wait_ge(item_ps, total + j + 1)
                d.wait_ge(item_done, total)
                d.tensor_tensor(at, ps[:, 4 + j, :].rearrange("p (k e) -> p k e", e=E), at, ALU.add).then_inc(item_done, 1)
            d.wait_ge(item_done, total + 2)
            with d.Fori(0, NB) as b:
                with d.Fori(0, NT // CH) as hf:
                    n = b * 2 + hf
                    d.wait_ge(out_stored, n * 16 + START_DMA)
                    ffn_dve(d, n + 4, b, hf, lambda k: x_mid[:, bass.ds(n * CB + k, 1), :].rearrange("p a e -> p (a e)"),
                            x_mid[:, bass.ds(n * CB, CB), :], x_out[:])


def kernel(**inputs):
    import concourse.bacc as bacc
    from concourse.bass_utils import run_bass_kernel_spmd

    nc = bacc.Bacc("TRN2", target_bir_lowering=False, num_devices=1)
    arrays = {k: np.ascontiguousarray(v) for k, v in layouts(inputs).items()}
    arrays.update({k: np.ascontiguousarray(v.astype(np.float32)) for k, v in constants().items()})
    named = {f"in_{k}": v for k, v in arrays.items()}
    ins = {k: nc.dram_tensor(f"in_{k}", v.shape, mybir.dt.from_np(v.dtype), kind="ExternalInput").ap() for k, v in arrays.items()}
    out = nc.dram_tensor("out", [NB * NT // CH, P, CB, E], F32, kind="ExternalOutput").ap()
    split = nc.dram_tensor("split_parts", [2, NB, PARTS, P, NT], BF16, kind="Internal").ap()
    rq = nc.dram_tensor("rotated_q", [NB, P, NT], F32, kind="Internal").ap()
    program(nc, ins, out, split, rq)
    r = run_bass_kernel_spmd(nc, [named], core_ids=[0])
    got = np.asarray(r.results[0]["out"])
    return got.transpose(0, 2, 1, 3).reshape(NB, NT, E)
```

```python
from contextlib import ExitStack

import numpy as np
import concourse.bass as bass
from concourse import mybir

P = 128
E = 128
NB, NT = 2, 1024
BLK = NT // P
H, D = 16, 64
NP_ = H // 2
CH = 512
CB = CH // P
NC = NB * NT // CH
HALVES = NT // CH
HALO = 16
SUB = 32
WIN = SUB + 2 * HALO
NW = CH // SUB
CK = CH + 2 * HALO
KH = CK // 2
SIDE = WIN
EDGE = HALO + SIDE
XC = CK + 2 * SIDE
NX = NW + 2
HB, DB = 16, 8
PARTS = 3
KROWS = PARTS * PARTS * DB
EPS = 1e-5
INF = 10000.0
SCALE = 1.0 / float(np.sqrt(np.float32(H * D)))

ALU = mybir.AluOpType
ACT = mybir.ActivationFunctionType
AX = mybir.AxisListType
F32 = mybir.dt.float32
BF16 = mybir.dt.bfloat16


def constants():
    inv = (1.0 / np.float32(10000.0) ** (np.arange(0, D, 2, dtype=np.float32) / np.float32(D))).astype(np.float64)
    q_angle = inv[:, None] * np.arange(CH)[None, :]
    k_angle = inv[:, None] * (np.arange(CK) - HALO)[None, :]
    sin_q = np.concatenate([np.sin(q_angle)] * 4, 0)
    cos_q = np.concatenate([np.cos(q_angle), -np.cos(q_angle)] * 2, 0)
    enc_k = np.concatenate([np.cos(k_angle), np.sin(k_angle)], 0)
    mask = np.zeros((P, NT // CH, CB, WIN), np.float32)
    for half in range(NT // CH):
        for blk in range(CB):
            for p in range(P):
                ql = p % SUB
                rel = np.arange(WIN)
                key = half * CH + blk * P + (p // SUB) * SUB - HALO + rel
                ok = (rel >= ql) & (rel - ql <= 2 * HALO) & (key >= 0) & (key < NT)
                mask[p, half, blk] = np.where(ok, 0.0, -INF / SCALE)
    theta = (1.0 / np.float32(1250.0) ** (np.arange(0, DB // 2, dtype=np.float32) / np.float32(DB // 2))).astype(np.float32)
    angle = (np.arange(NT, dtype=np.float32)[:, None] * theta[None, :]).astype(np.float32).astype(np.float64)
    rot_cos = np.repeat(np.cos(angle), 2, axis=1)
    rot_sin = np.stack([-np.sin(angle), np.sin(angle)], -1).reshape(NT, DB)
    rows = lambda a: a.reshape(BLK, P, DB).transpose(1, 0, 2)
    return {
        "ident": np.eye(P), "sin_q": sin_q, "cos_q": cos_q, "enc_k": enc_k, "mask": mask,
        "rot_cos": rows(rot_cos), "rot_sin": rows(rot_sin),
    }


def layouts(i):
    a = {k: np.asarray(v) for k, v in i.items()}
    rel_t = a["L0_attn_a_W_rel"].T
    rel_sw = np.concatenate([rel_t[:, D // 2:], rel_t[:, :D // 2]], 1)
    heads_t = lambda w: w.reshape(E, H, D).transpose(2, 1, 0)
    w_out = a["L0_attn_b_w_out"].reshape(HB // 2, 2, 1, DB, E)
    w_out = np.broadcast_to(w_out, (HB // 2, 2, DB, DB, E)).reshape(HB // 2, P, E).transpose(1, 0, 2)
    return {
        "x": a["L0_attn_a_x"].reshape(NB * BLK, P, E).transpose(1, 0, 2),
        "wq": a["L0_attn_a_W_q"], "wk": a["L0_attn_a_W_k"],
        "wq_t": heads_t(a["L0_attn_a_W_q"]), "wv_t": heads_t(a["L0_attn_a_W_v"]),
        "wo": a["L0_attn_a_W_o"].reshape(H, D, E).transpose(1, 0, 2),
        "rel": np.concatenate([rel_t, rel_t, rel_sw, rel_sw], 1),
        "cb_pair": a["L0_attn_a_content_bias"].reshape(NP_, P).T,
        "cb_t": a["L0_attn_a_content_bias"].T, "rb_t": a["L0_attn_a_relative_bias"].T,
        "brel": np.tile(a["L0_attn_a_b_rel"], 2)[:, None],
        "bo": a["L0_attn_a_b_o"][None, :],
        "wr_t": a["L0_ffn_W_r"].T, "wk_t": a["L0_ffn_W_k"].T, "wv2_t": a["L0_ffn_W_v"].T,
        "mu": np.stack([a["L0_ffn_mu_r"], a["L0_ffn_mu_k"]], 1),
        "wqkv": a["L0_attn_b_w_qkv"], "bqkv": np.broadcast_to(a["L0_attn_b_b_qkv"], (P, 3 * HB * DB)),
        "wout": w_out, "bout": np.broadcast_to(a["L0_attn_b_b_out"], (P, E)),
    }


class NormSems:
    def __init__(self, sem, name):
        (self.st, self.mv, self.lnv, self.rstd, self.xh, self.t_ps, self.t_ev) = (
            sem(f"{name}_{n}") for n in ("st", "mv", "lnv", "rstd", "xh", "t_ps", "t_ev"))


class FfnSet:
    def __init__(self, sem, name, bank, xh, out, mix, prev, k, e, s, stats):
        self.bank, self.xh, self.out, self.mix, self.prev, self.k, self.e, self.s = bank, xh, out, mix, prev, k, e, s
        self.stat, self.mv, self.lnv, self.rstd = stats
        self.ln = NormSems(sem, name)
        (self.s_prev, self.s_mix, self.s_r_ps, self.s_k_ps, self.s_relu, self.s_sq, self.s_exp, self.s_one, self.s_sig,
         self.s_v_ps, self.s_gate, self.s_out) = (
            sem(f"{name}_{n}") for n in "prev mix r_ps k_ps relu sq exp one sig v_ps gate out".split())


def program(nc, ins, out_dram, split_dram, rq_dram):
    ctx = ExitStack()
    with ctx:
        def sb(name, shape, dt=F32):
            return ctx.enter_context(nc.sbuf_tensor(name, shape, dt))

        def sem(name):
            return ctx.enter_context(nc.semaphore(name))

        ps = ctx.enter_context(nc.psum_tensor("ps", [P, 8, 512], F32))

        x_tok = sb("x_tok", [P, NB * BLK, E])
        ident = sb("ident", [P, P])
        wq = sb("wq_sb", [P, H * D])
        wk = sb("wk_sb", [P, H * D])
        rel = sb("rel_sb", [D, 4 * D])
        cb_pair = sb("cb_pair_sb", [P, NP_])
        cb_t = sb("cb_t_sb", [D, H])
        rb_t = sb("rb_t_sb", [D, H])
        brel = sb("brel_sb", [P, 1])
        bo = sb("bo_sb", [1, E])
        bout = sb("bout_sb", [P, E])
        wr_t = sb("wr_t_sb", [P, E])
        wk_t = sb("wk_t_sb", [P, E])
        wv2_t = sb("wv2_t_sb", [P, E])
        mu = sb("mu_sb", [P, 2])
        wqkv = sb("wqkv_sb", [P, 3 * E])
        bqkv = sb("bqkv_sb", [P, 3 * E])
        wout = sb("wout_sb", [P, NP_, E])
        sin_q = sb("sin_q_sb", [P, CH])
        cos_q = sb("cos_q_sb", [P, CH])
        mask = sb("mask_sb", [P, NT // CH, CB, WIN])
        rot_cos = sb("rot_cos_sb", [P, BLK, DB])
        rot_sin = sb("rot_sin_sb", [P, BLK, DB])

        wu = sb("wu", [P, 2, NP_, 2, D])
        u_bias = sb("u_bias", [P, 2, NP_])
        head_const = sb("head_const", [P, H])
        bias_gap = sb("bias_gap", [D, H])
        brel_wide = sb("brel_wide", [D, P])
        ones = sb("ones", [1, P])
        mu_rest = sb("mu_rest", [P, 2])
        wvo = sb("wvo", [P, H, E])
        eps = sb("eps", [P, 1])
        idle = sb("idle", [P, 2])
        xT = sb("xT", [P, NB, NT + 2 * EDGE])

        xc = sb("xc", [P, XC])
        qt = sb("qt", [P, 2, 2, CH])
        kt = sb("kt", [P, 2, 2, CK])
        mx = sb("mx", [P, 2, CB * 2])
        tot = sb("tot", [P, 2, CB * 2])
        rtot = sb("rtot", [P, 2, CB * 2])
        xw = sb("xw", [P, NX, E])
        arena = sb("arena", [P, 16384])
        zh = arena[:, 0:8192].rearrange("p (h t) -> p h t", h=H)
        pt = arena[:, 8192:12288].rearrange("p (g t) -> p g t", g=NP_)
        turn = arena[:, 12288:14336].rearrange("p (b k t) -> p b k t", b=2, k=2)
        sm = arena[:, 14336:15360].rearrange("p (b k h w) -> p b k h w", b=2, k=CB, h=2)
        pr = arena[:, 15360:16384].rearrange("p (b k h w) -> p b k h w", b=2, k=CB, h=2)
        wq_t = arena[0:D, 0:2048].rearrange("p (h e) -> p h e", h=H)
        wv_t = arena[0:D, 2048:4096].rearrange("p (h e) -> p h e", h=H)
        wo = arena[0:D, 4096:6144].rearrange("p (h e) -> p h e", h=H)
        xn = arena[:, 6144:8192].rearrange("p (k e) -> p k e", e=E)
        z_sb = arena[:, 0:2048].rearrange("p (s t) -> p s t", s=2)
        g_sb = arena[:, 2048:4096].rearrange("p (s t) -> p s t", s=2)
        r_buf = arena[:, 8192:16384].rearrange("p (g t) -> p g t", g=8)

        stat = sb("stat", [P, NB * BLK, 6])
        mv = sb("mv", [P, NB * BLK, 2])
        lnv = sb("lnv", [P, NB * BLK])
        rstd = sb("rstd", [P, NB * BLK])
        x1 = sb("x1", [P, CB, E])
        xh = sb("xh", [P, CB, E])
        fx = sb("fx", [P, NB, NT + 1])
        x_mid = x_tok
        second = lambda k, n: arena[:, 8192 + 1024 * k:8192 + 1024 * k + n]
        pair_of = lambda v: v.rearrange("p (a t) -> p a t", a=2)
        blocks_of = lambda v: v.rearrange("p (k e) -> p k e", e=E)
        F = [FfnSet(sem, "f0", 5, xh[:], x1[:], sb("fmix", [P, 2, CH])[:], sb("fprev", [P, 2, CH])[:],
                    sb("fk", [P, CH])[:], sb("fe", [P, CH])[:], sb("fs", [P, CH])[:], (stat, mv, lnv, rstd)),
             FfnSet(sem, "f1", 1, blocks_of(second(0, CH)), blocks_of(second(1, CH)), pair_of(second(2, 2 * CH)),
                    pair_of(second(3, 2 * CH)), second(4, CH), second(5, CH), second(6, CH),
                    (stat[:, CB:], mv[:, CB:], lnv[:, CB:], rstd[:, CB:]))]
        x3t = arena[:, 12288:12800]
        qk_neg = arena[:, 12800:13824].rearrange("p (a t) -> p a t", a=2)
        rest = arena[:, 14336:15360].rearrange("p (a t) -> p a t", a=2)
        qkv = arena[:, 15360:16384].rearrange("p (a k n) -> p a k n", a=2, k=CB)
        rqt = F[0].e
        rq = sb("rq", [P, CB, E])
        rk = sb("rk", [P, NB * BLK, E])
        v_tok = sb("v_tok", [P, NB * BLK, E])
        parts = sb("parts", [P, 2, PARTS, CH], BF16)

        qs = wu[:].rearrange("p a g s d -> p (a g s d)").bitcast(BF16).rearrange("p (b h t) -> p b h t", b=2, h=2)
        ks = wvo[:].rearrange("p h e -> p (h e)").bitcast(BF16).rearrange("p (b h t) -> p b h t", b=2, h=2)
        rqx = qt[:].rearrange("p b h t -> p b (h t)")
        wf = xw[:].rearrange("p w e -> p (w e)")[:, 0:2 * 2 * BLK * DB * DB].rearrange("p (s h k a d) -> p s h k a d", s=2, h=2, k=BLK, a=DB)

        x_loaded, w_loaded, enc_loaded = sem("x_loaded"), sem("w_loaded"), sem("enc_loaded")
        cleared, small_ready, gap_ready = sem("cleared"), sem("small_ready"), sem("gap_ready")
        wu_ps, wu_ev, ub_ps, ub_ev, wvo_ps, wvo_ev = map(sem, ("wu_ps", "wu_ev", "ub_ps", "ub_ev", "wvo_ps", "wvo_ev"))
        st0, mv0, lnv0, rstd0, xn0, xt_ps, xt_ev = map(sem, ("st0", "mv0", "lnv0", "rstd0", "xn0", "xt_ps", "xt_ev"))
        names = ("xc_ready xw_ps xw_ev q_ps u_ps k_ps q_ev u_ev k_ev rot_half rot_done s_ps s_masked mx_done sub_done "
                 "exp_done sum_done rec_done norm_done pt_ps pt_ev pv_ps ze_ev zo_ev y_ps x1_done").split()
        (xc_ready, xw_ps, xw_ev, q_ps, u_ps, k_ps, q_ev, u_ev, k_ev, rot_half, rot_done, s_ps, s_masked, mx_done, sub_done,
         exp_done, sum_done, rec_done, norm_done, pt_ps, pt_ev, pv_ps, ze_ev, zo_ev, y_ps, x1_done) = map(sem, names)
        lnb = NormSems(sem, "b")
        f_exp, f_relu, f_gate = F[0].s_exp, F[0].s_relu, F[0].s_gate
        names = ("b_qkv_ps b_qkv b_min b_exp b_elu b_t2 b_rot b_qk_t b_rq_t b_hi b_r1 b_mid b_lo b_rqt "
                 "parts_stored rq_stored").split()
        (b_qkv_ps, b_qkv, b_min, b_exp, b_elu, b_t2, b_rot, b_qk_t, b_rq_t, b_hi, b_r1, b_mid, b_lo, b_rqt,
         parts_stored, rq_stored) = map(sem, names)
        names = "wf_done den_act ln_done r_act r_free item_ps item_done b_bias".split()
        (wf_done, den_act, ln_done, r_act, r_free, item_ps, item_done, b_bias) = map(sem, names)
        out_stored = [sem(f"out_stored{k}") for k in range(NB)]
        stack_in, rqx_in, z_ev, g_done = ([sem(f"{n}{s}") for s in range(2)]
                                                  for n in ("stack_in", "rqx_in", "z_ev", "g_done"))

        loads = [(ident, "ident"), (wq, "wq"), (wk, "wk"), (wq_t, "wq_t"), (wv_t, "wv_t"), (wo, "wo"), (rel, "rel"),
                 (cb_pair, "cb_pair"), (cb_t, "cb_t"), (rb_t, "rb_t"), (brel, "brel"), (bo, "bo"), (bout, "bout"),
                 (wr_t, "wr_t"), (wk_t, "wk_t"), (wv2_t, "wv2_t"), (mu, "mu"), (wqkv, "wqkv"), (bqkv, "bqkv"),
                 (wout, "wout"), (sin_q, "sin_q"), (cos_q, "cos_q"), (mask, "mask"), (rot_cos, "rot_cos"),
                 (rot_sin, "rot_sin")]
        W_ALL = 16 * len(loads)

        def zh_view(v, par):
            return zh[:, par::2, 2 * v * SUB:(2 * v + 2) * SUB].rearrange("p g (w t) -> p w g t", w=2)

        def ln_stats(d, f, q, n, src):
            d.memset(idle[:, 0:1], 0.0)
            for blk in range(CB):
                ins_ = d.bn_stats(f.stat[:, blk, :], src(blk))
            ins_.then_inc(q.st, 1)
            d.wait_ge(q.st, n + 1)
            d.memset(idle[:, 1:2], 0.0)
            for blk in range(CB):
                ins_ = d.bn_aggr(f.mv[:, blk, :], f.stat[:, blk, :])
            ins_.then_inc(q.mv, 1)

        def ln_apply(d, f, q, n, src):
            d.wait_ge(q.mv, n + 1)
            d.wait_ge(q.rstd, n + 1)
            for blk in range(CB):
                ins_ = d.tensor_scalar(f.xh[:, blk, :], src(blk), f.mv[:, blk, 0:1], f.rstd[:, blk:blk + 1], ALU.subtract, ALU.mult)
            ins_.then_inc(q.xh, 1)

        def ln_act(a, f, q, n):
            a.wait_ge(q.mv, n + 1)
            a.activation(f.lnv[:, 0:CB], f.mv[:, 0:CB, 1], ACT.Ln, bias=eps[:, 0:1]).then_inc(q.lnv, 1)
            a.wait_ge(q.lnv, n + 1)
            a.activation(f.rstd[:, 0:CB], f.lnv[:, 0:CB], ACT.Exp, scale=-0.5).then_inc(q.rstd, 1)

        def fx_at(b, hf, back=0):
            return fx[:, bass.ds(b, 1), bass.ds(hf * CH + 1 - back, CH)].rearrange("p a t -> p (a t)")

        def ffn_turn(t, f, n):
            t.wait_ge(f.ln.xh, n + 1)
            t.wait_ge(f.s_exp, n + START)
            for blk in range(CB):
                mm = t.transpose(ps[:, f.bank, blk * P:(blk + 1) * P], f.xh[:, blk, :], ident[:])
            mm.then_inc(f.ln.t_ps, 1)

        def ffn_key_gate(t, f, n):
            t.wait_ge(f.s_mix, n * 2 + 2)
            t.wait_ge(f.s_relu, n + START)
            t.matmul(ps[:, f.bank + 1, :], wk_t[:], f.mix[:, 1, :], start=True, stop=True).then_inc(f.s_k_ps, 1)
            t.wait_ge(f.ln.t_ev, n + 1)
            for blk in range(CB):
                mm = t.matmul(ps[:, f.bank, blk * P:(blk + 1) * P], f.mix[:, 0, blk * P:(blk + 1) * P], wr_t[:], start=True, stop=True)
            mm.then_inc(f.s_r_ps, 1)

        def ffn_value(t, f, n):
            t.wait_ge(f.s_sq, n + 1)
            t.wait_ge(f.s_gate, n + START)
            for blk in range(CB):
                mm = t.matmul(ps[:, f.bank + 2, blk * P:(blk + 1) * P], f.k[:, blk * P:(blk + 1) * P], wv2_t[:], start=True, stop=True)
            mm.then_inc(f.s_v_ps, 1)

        def ffn_turned(a, f, n, b, hf):
            a.wait_ge(f.ln.t_ps, n + 1)
            a.copy(fx_at(b, hf), ps[:, f.bank, :]).then_inc(f.ln.t_ev, 1)

        def ffn_act(a, f, n):
            a.wait_ge(f.s_k_ps, n + 1)
            a.wait_ge(f.s_v_ps, n + START)
            a.activation(f.k, ps[:, f.bank + 1, :], ACT.Relu).then_inc(f.s_relu, 1)
            a.wait_ge(f.s_relu, n + 1 + START)
            a.activation(f.k, f.k, ACT.Square).then_inc(f.s_sq, 1)
            a.wait_ge(f.s_r_ps, n + 1)
            a.wait_ge(f.s_one, n + START)
            a.activation(f.e, ps[:, f.bank, :], ACT.Exp, scale=-1.0).then_inc(f.s_exp, 1)

        def ffn_mix(d, f, n, b, hf):
            d.wait_ge(f.ln.t_ev, n + 1)
            for k in (1, 0):
                d.tensor_scalar(f.prev[:, k, :], fx_at(b, hf, 1), mu_rest[:, k:k + 1], None, ALU.mult).then_inc(f.s_prev, 1)
            for m, k in enumerate((1, 0)):
                d.wait_ge(f.s_prev, n * 2 + m + 1)
                d.scalar_tensor_tensor(f.mix[:, k, :], fx_at(b, hf), mu[:, k:k + 1], f.prev[:, k, :], ALU.mult, ALU.add).then_inc(f.s_mix, 1)

        def ffn_sigmoid(d, f, n):
            d.wait_ge(f.s_exp, n + 1 + START)
            d.tensor_scalar(f.s, f.e, 1.0, None, ALU.add).then_inc(f.s_one, 1)
            d.wait_ge(f.s_one, n + 1 + START)
            d.reciprocal(f.s, f.s).then_inc(f.s_sig, 1)

        def ffn_gate(d, f, n, res, dst):
            d.wait_ge(f.s_sig, n + 1)
            d.wait_ge(f.s_v_ps, n + 1 + START)
            d.tensor_tensor(f.s, ps[:, f.bank + 2, :], f.s, ALU.mult).then_inc(f.s_gate, 1)
            d.wait_ge(f.s_gate, n + 1 + START)
            d.tensor_tensor(dst, f.s.rearrange("p (k e) -> p k e", e=E), res, ALU.add).then_inc(f.s_out, 1)

        START, START_DMA = 1, 16
        RF = 5
        first = {
            "sp": (parts_stored, rq_stored, *out_stored),
            "pool": (rot_done, norm_done, b_rot, g_done[0], g_done[1]),
            "pe": (s_ps, pt_ps, pv_ps, y_ps, k_ps, b_qk_t, *(f.s_v_ps for f in F)),
            "act": (q_ev, k_ev, pt_ev, b_rqt, b_hi, b_exp, b_mid, exp_done, *(f.s_exp for f in F), *(f.s_relu for f in F)),
            "dve": (u_ev, x1_done, s_masked, b_qkv, b_elu, b_r1, b_lo, *(f.s_gate for f in F), *(f.s_one for f in F)),
        }

        def start(eng, name):
            for s in first[name]:
                eng.sem_inc(s, START_DMA if name == "sp" else START)
            if name == "pe":
                eng.sem_inc(r_free, RF)

        NI = NB * NP_ // 2
        ACT_LIST = [0, 1, 2, 4, 5, 6, 8, 9, 10, 12, 13, 15, 14]
        NA = len(ACT_LIST)
        ITEMS = [("U", 0), ("U", 1), ("U", 2), ("U", 3), ("O", 0), ("U", 4), ("U", 5), ("O", 1), ("U", 6)]
        PER = len(ITEMS)

        def turn_no(i, s):
            return 2 * i + s

        def items_of(it):
            if isinstance(it, int) and it == 0:
                return [x for x in ITEMS if x[0] == "U"], 0
            return ITEMS, it * PER - 2

        def before(i, s):
            return (i, 0) if s else (i - 1, 1)

        def if_any(eng, s, n):
            if not isinstance(n, int) or n > 0:
                eng.wait_ge(s, n)

        def turns(eng, body):
            for s in range(2):
                body(0, s)
            with eng.Fori(1, NI - 1) as i:
                for s in range(2):
                    body(i, s)
            for s in range(2):
                body(NI - 1, s)

        def nothing():
            pass

        def chunks(eng, body, background):
            body(0, False)
            with eng.Fori(1, NC) as c:
                body(c, True)
            for step in background(NC - 1):
                step()

        def behind(eng, s, per, c):
            if not isinstance(c, int):
                eng.wait_ge(s, (c - 1) * per + START)

        block = ctx.enter_context(nc.Block())

        @block.sync
        def _(sp):
            start(sp, "sp")
            sp.dma_start(x_tok[:], ins["x"]).then_inc(x_loaded, 16)
            for dst, name in loads:
                src = ins[name]
                sp.dma_start(dst[:] if not isinstance(dst, bass.AP) else dst, src).then_inc(w_loaded, 16)
            for buf in range(2):
                sp.dma_start(kt[D:P, buf, 0, :], ins["enc_k"]).then_inc(enc_loaded, 16)
                sp.dma_start(kt[0:D, buf, 1, :], ins["enc_k"]).then_inc(enc_loaded, 16)
            with sp.Fori(0, NC) as c:
                b, hf = c // HALVES, c % HALVES
                sp.wait_ge(b_lo, c * 2 + 2 + START)
                for w in range(2):
                    sp.dma_start(split_dram[w, bass.ds(b, 1), :, :, bass.ds(hf * CH, CH)].rearrange("a s p t -> p (a s) t"),
                                 parts[:, w]).then_inc(parts_stored, 16)
                sp.wait_ge(b_rqt, c + 1 + START)
                sp.dma_start(rq_dram[bass.ds(b, 1), :, bass.ds(hf * CH, CH)].rearrange("a p t -> p (a t)"),
                             rqt).then_inc(rq_stored, 16)
            sp.wait_ge(parts_stored, 2 * 16 * NB * (NT // CH) + START_DMA)
            sp.wait_ge(rq_stored, 16 * NB * (NT // CH) + START_DMA)
            with sp.Fori(0, NI) as i:
                for s in range(2):
                    it = turn_no(i, s)
                    sp.wait_ge(r_free, (it - 1) * 4 + RF)
                    for h in range(2):
                        b, row = it // NP_, ((it % NP_) * 2 + h) * DB
                        for side, dst in ((0, qs), (1, ks)):
                            src = split_dram[side, bass.ds(b, 1), :, bass.ds(row, DB), :].rearrange("a s p t -> (a s) p t")
                            src = src.unsqueeze(1 - side).broadcast_to([PARTS, PARTS, DB, NT])
                            for part in range(PARTS):
                                sp.dma_start(dst[part * PARTS * DB:(part + 1) * PARTS * DB, s, h, :],
                                             src[part]).then_inc(stack_in[s], 16)
                    sp.wait_ge(g_done[s], i + START)
                    src = rq_dram[bass.ds(it // NP_, 1), bass.ds((it % NP_) * 16, 16), :].rearrange("a p t -> (a p) t")
                    sp.dma_start(rqx[:, s, :], src.unsqueeze(1).broadcast_to([16, DB, NT])).then_inc(rqx_in[s], 16)
            with sp.Fori(0, HALVES) as hf:
                for k, f in enumerate(F):
                    sp.wait_ge(f.s_out, hf + 1 + (NC if k == 0 else 0))
                    sp.dma_start(out_dram[bass.ds(k * HALVES + hf, 1)].rearrange("a p k e -> p (a k) e"),
                                 f.out).then_inc(out_stored[k], 16)
            for k in range(NB):
                sp.wait_ge(out_stored[k], 16 * HALVES + START_DMA)

        @block.gpsimd
        def _(pool):
            g = nc.gpsimd
            start(g, "pool")
            g.memset(xT[:, :, 0:EDGE], 0.0).then_inc(cleared, 1)
            g.memset(xT[:, :, EDGE + NT:], 0.0).then_inc(cleared, 1)
            g.memset(fx[:, :, 0:1], 0.0).then_inc(cleared, 1)
            g.memset(ones[:], 1.0).then_inc(cleared, 1)
            g.wait_ge(cleared, 4)
            def pool_chunk(c, back):
                def rot_add(p):
                    g.wait_ge(u_ev, c * NP_ + p + 1 + START)
                    if p >= 2:
                        g.wait_ge(s_ps, c * NP_ + p - 1 + START)
                    else:
                        g.wait_ge(s_ps, c * NP_ + START)
                    if p == 1:
                        g.wait_ge(rot_done, c * NP_ + 1 + START)
                    elif p >= 2:
                        g.wait_ge(sub_done, c * NP_ + p - 1)
                    g.tensor_tensor(qt[D:P, p % 2, 0, :], turn[D:P, p % 2, 0, :], turn[D:P, p % 2, 1, :],
                                    ALU.add).then_inc(rot_half, 1)
                    g.wait_ge(rot_half, c * NP_ + p + 1)
                    g.tensor_tensor(qt[0:D, p % 2, 1, :], turn[0:D, p % 2, 0, :], turn[0:D, p % 2, 1, :],
                                    ALU.add).then_inc(rot_done, 1)

                def sub_max(p):
                    v = sm[:, p % 2].rearrange("p k h w -> p (k h) w")
                    g.wait_ge(mx_done, c * NP_ + p + 1)
                    g.wait_ge(rot_done, c * NP_ + min(p + 2, NP_) + START)
                    g.tensor_tensor(v, v, mx[:, p % 2].unsqueeze(2).broadcast_to([P, CB * 2, WIN]),
                                    ALU.subtract).then_inc(sub_done, 1)

                def norm(p):
                    v = pr[:, p % 2].rearrange("p k h w -> p (k h) w")
                    g.wait_ge(rec_done, c * NP_ + p + 1)
                    g.wait_ge(rot_done, c * NP_ + min(p + 3, NP_) + START)
                    g.tensor_tensor(v, v, rtot[:, p % 2].unsqueeze(2).broadcast_to([P, CB * 2, WIN]),
                                    ALU.mult).then_inc(norm_done, 1)

                g.wait_ge(norm_done, c * NP_ + START)
                behind(g, b_rot, 2, c)
                rot_add(0)
                for p in range(NP_ + 1):
                    if p >= 1:
                        sub_max(p - 1)
                    if p + 1 < NP_:
                        rot_add(p + 1)
                    if p >= 1:
                        norm(p - 1)
                if back:
                    rotation(c - 1)

            def rotation(n):
                g.wait_ge(b_elu, n + 1 + START)
                for side, dst in enumerate((rq[:], rk[:, bass.ds(n * CB, CB), :])):
                    blocks = bass.ds((n % HALVES) * CB, CB)
                    src = qkv[:, side].rearrange("p k (h d) -> p k h d", d=DB)
                    t1 = F[0].mix[:, side, :].rearrange("p (k h d) -> p k h d", k=CB, d=DB)
                    t2 = F[0].prev[:, side, :].rearrange("p (k h d) -> p k h d", k=CB, d=DB)
                    wide = lambda t, lo: t.unsqueeze(2).broadcast_to([P, CB, HB, lo])
                    g.tensor_tensor(t1, src, wide(rot_cos[:, blocks, :], DB), ALU.mult)
                    for odd in range(2):
                        ins_ = g.tensor_tensor(t2[:, :, :, odd::2], src[:, :, :, 1 - odd::2],
                                               wide(rot_sin[:, blocks, odd::2], DB // 2), ALU.mult)
                    ins_.then_inc(b_t2, 1)
                    g.wait_ge(b_t2, n * 2 + side + 1)
                    g.tensor_tensor(dst.rearrange("p k (h d) -> p k h d", d=DB), t1, t2, ALU.add).then_inc(b_rot, 1)

            chunks(g, pool_chunk, lambda n: [lambda: rotation(n)])
            g.wait_ge(b_rot, 2 * NC + START)
            g.wait_ge(b_qkv, 3 * NC + START)
            def features(i, s):
                b, p = turn_no(i, s) // NP_, turn_no(i, s) % NP_
                for h in range(2):
                    at, keys = bass.ds((2 * p + h) * DB, DB), bass.ds(b * BLK, BLK)
                    ins_ = g.tensor_tensor(wf[:, s, h], rk[:, keys, at].unsqueeze(3).broadcast_to([P, BLK, DB, DB]),
                                           v_tok[:, keys, at].unsqueeze(2).broadcast_to([P, BLK, DB, DB]), ALU.mult)
                ins_.then_inc(wf_done, 1)

            def gather(i, s):
                it = turn_no(i, s)
                g.wait_ge(z_ev[s], i + 1)
                g.wait_ge(rqx_in[s], (i + 1) * 16)
                if not isinstance(i, int) or i > 0:
                    g.wait_ge(item_ps, it * PER - 2 - PER + 8)
                g.tensor_tensor(g_sb[:, s, :], z_sb[:, s, :], rqx[:, s, :], ALU.mult).then_inc(g_done[s], 1)
                if not isinstance(i, int) or i < NI - 1:
                    g.wait_ge(r_free, (it + 1) * 4 + RF)
                    features(i + 1, s)

            features(0, 0)
            features(0, 1)
            turns(g, gather)

        @block.tensor
        def _(pe):
            t = nc.tensor
            start(t, "pe")
            t.wait_ge(w_loaded, W_ALL)
            for k in range(4):
                for q4 in range(4):
                    p, slot = 2 * k + q4 // 2, q4 % 2
                    mm = t.matmul(ps[:, k, q4 * P:(q4 + 1) * P], wq_t[:, 2 * p + 1 - slot, :], rel[:, D:3 * D],
                                  start=True, stop=True)
                mm.then_inc(wu_ps, 1)
            t.matmul(ps[:, 4, 0:H], rel[:, 0:2 * D], rb_t[:], start=True, stop=True)
            t.matmul(ps[:, 4, H:2 * H], rel[:, 2 * D:4 * D], rb_t[:], start=True, stop=True).then_inc(ub_ps, 1)
            t.wait_ge(gap_ready, 2)
            t.matmul(ps[:, 5, 0:H], brel_wide[:], bias_gap[:], start=True, stop=True).then_inc(ub_ps, 1)
            for k in range(4):
                if k < 2:
                    bank = 6 + k
                else:
                    bank = k - 2
                    t.wait_ge(wu_ev, k - 1)
                for q4 in range(4):
                    h = 4 * k + q4
                    mm = t.matmul(ps[:, bank, q4 * P:(q4 + 1) * P], wv_t[:, h, :], wo[:, h, :], start=True, stop=True)
                mm.then_inc(wvo_ps, 1)
            for k in range(4):
                if k < 2:
                    t.wait_ge(wu_ev, k + 3)
                else:
                    t.wait_ge(ub_ev, k)
                t.wait_ge(xn0, k // 2 + 1)
                for q4 in range(4):
                    mm = t.transpose(ps[:, 2 + k, q4 * P:(q4 + 1) * P], xn[:, 4 * k + q4, :], ident[:])
                mm.then_inc(xt_ps, 1)
            t.wait_ge(enc_loaded, 64)
            t.wait_ge(cleared, 4)
            t.wait_ge(wvo_ev, 4)
            t.wait_ge(xt_ev, 4)

            def pe_chunk(c, back):
                def proj(p):
                    t.wait_ge(q_ev, c * NP_ + p + START)
                    t.matmul(ps[:, 0, :], wq[:, p * P:(p + 1) * P], xc[:, EDGE:EDGE + CH], start=True, stop=True).then_inc(q_ps, 1)
                    t.wait_ge(u_ev, c * NP_ + p + START)
                    for k in range(2):
                        mm = t.matmul(ps[:, 1 + k, :], wu[:, k, p].rearrange("p a d -> p (a d)"), xc[:, EDGE:EDGE + CH],
                                      start=True, stop=True)
                    mm.then_inc(u_ps, 1)
                    t.wait_ge(k_ev, c * NP_ + p + START)
                    if p == 0:
                        t.wait_ge(x1_done, c + START)
                    for k in range(2):
                        mm = t.matmul(ps[:, 3 + k, 0:KH], wk[:, p * P:(p + 1) * P], xc[:, SIDE + k * KH:SIDE + (k + 1) * KH],
                                      start=True, stop=True)
                    mm.then_inc(k_ps, 1)

                def scores(p):
                    t.wait_ge(q_ev, c * NP_ + p + 1 + START)
                    t.wait_ge(k_ev, c * NP_ + p + 1 + START)
                    t.wait_ge(rot_done, c * NP_ + p + 1 + START)
                    t.wait_ge(s_masked, c * NP_ + max(p - 1, 0) + START)
                    for blk in range(CB):
                        for par in range(2):
                            for j in range(P // SUB):
                                q0 = blk * P + j * SUB
                                mm = t.matmul(ps[j * SUB:(j + 1) * SUB, 5 + p % 2, (blk * 2 + par) * WIN:(blk * 2 + par + 1) * WIN],
                                              qt[:, p % 2, par, q0:q0 + SUB], kt[:, p % 2, par, q0:q0 + WIN],
                                              start=True, stop=True)
                    mm.then_inc(s_ps, 1)

                def turn_probs(p):
                    t.wait_ge(norm_done, c * NP_ + p + 1 + START)
                    t.wait_ge(pt_ev, c * NP_ + p + START)
                    for blk in range(CB):
                        mm = t.transpose(ps[:, 7, blk * P:(blk + 1) * P], pr[:, p % 2, blk].rearrange("p h w -> p (h w)"), ident[:])
                    mm.then_inc(pt_ps, 1)

                def values_out(blk):
                    t.wait_ge(ze_ev, c * 8 + 2 * blk + 2)
                    t.wait_ge(zo_ev, c * 8 + 2 * blk + 2)
                    dst = ps[:, 4, blk * P:(blk + 1) * P]
                    for h in range(H):
                        t.matmul(dst, zh[:, h, blk * P:(blk + 1) * P], wvo[:, h, :], start=(h == 0), stop=False)
                    mm = t.matmul(dst, ones[:], bo[:], start=False, stop=True)
                    if blk == CB - 1:
                        mm.then_inc(y_ps, 1)

                def windows(k5):
                    bank = 5 + k5 % 3
                    if k5 >= 3:
                        t.wait_ge(xw_ev, c * 5 + k5 - 2)
                    for k in range(4 * k5, min(4 * k5 + 4, NX)):
                        mm = t.transpose(ps[:, bank, (k % 4) * P:(k % 4 + 1) * P], xc[:, k * SUB:k * SUB + P], ident[:])
                    mm.then_inc(xw_ps, 1)

                steps = pe_background(c - 1) if back else [nothing] * (NW // 2 + 2)
                t.wait_ge(xc_ready, c + 1)
                proj(0)
                behind(t, b_rqt, 1, c)
                behind(t, b_hi, 2, c)
                behind(t, b_r1, 2, c)
                t.wait_ge(s_masked, c * NP_ + START)
                t.wait_ge(pt_ev, c * NP_ + START)
                for k5 in range(3):
                    windows(k5)
                proj(1)
                for k5 in range(3, 5):
                    windows(k5)
                t.wait_ge(xw_ev, c * 5 + 5)
                for p in range(NP_):
                    if p > 0 and p + 1 < NP_:
                        proj(p + 1)
                    if p >= 2:
                        turn_probs(p - 2)
                    scores(p)
                turn_probs(NP_ - 2)
                turn_probs(NP_ - 1)
                t.wait_ge(s_masked, c * NP_ + NP_ + START)
                t.wait_ge(pt_ev, c * NP_ + NP_ + START)
                t.wait_ge(q_ev, c * NP_ + NP_ + START)
                t.wait_ge(u_ev, c * NP_ + NP_ + START)
                t.wait_ge(k_ev, c * NP_ + NP_ + START)
                for v in range(NW // 2):
                    if v >= 2:
                        t.wait_ge(ze_ev, c * 8 + v - 1)
                        t.wait_ge(zo_ev, c * 8 + v - 1)
                    for w2 in range(2):
                        for par in range(2):
                            rows = slice(D * par, D * par + WIN)
                            w = 2 * v + w2
                            mm = t.matmul(ps[:, 2 * (v % 2) + par, w2 * 256:(w2 + 1) * 256].rearrange("p (g t) -> p g t", g=NP_),
                                          xw[rows, w + 2 * (1 - par), :], pt[rows, :, w * SUB:(w + 1) * SUB], start=True, stop=True)
                            if w2:
                                mm.then_inc(pv_ps, 1)
                    if v < NW // 2 - 1:
                        steps[v + 1]()
                    if v % 2 and v > 1:
                        values_out(v // 2 - 1)
                steps[NW // 2]()
                values_out(CB - 1)
                steps[NW // 2 + 1]()

            def pe_background(n):
                def turn_out():
                    t.wait_ge(b_rqt, n + START)
                    t.wait_ge(b_hi, 2 * n + START)
                    t.wait_ge(b_r1, 2 * n + START)
                    ffn_turn(t, F[0], n)

                def turn_mid():
                    t.wait_ge(lnb.xh, n + 1)
                    t.wait_ge(f_exp, n + 1 + START)
                    for blk in range(CB):
                        mm = t.transpose(ps[:, 5, blk * P:(blk + 1) * P], xh[:, blk, :], ident[:])
                    mm.then_inc(lnb.t_ps, 1)

                def project(side):
                    t.wait_ge((lnb.t_ev, f_relu, f_gate)[side], n + 1 + (START if side else 0))
                    for blk in range(CB):
                        mm = t.matmul(ps[:, 5 + side, blk * P:(blk + 1) * P], x3t[:, blk * P:(blk + 1) * P],
                                      wqkv[:, side * E:(side + 1) * E], start=True, stop=True)
                    mm.then_inc(b_qkv_ps, 1)

                def projections():
                    for side in range(3):
                        project(side)

                def turn_qk():
                    t.wait_ge(b_elu, n + 1 + START)
                    t.wait_ge(b_qkv, n * 3 + 3 + START)
                    for side in range(2):
                        for blk in range(CB):
                            mm = t.transpose(ps[:, 6 + side, blk * P:(blk + 1) * P], qkv[:, side, blk], ident[:])
                        mm.then_inc(b_qk_t, 1)

                def turn_rotated():
                    t.wait_ge(b_rot, n * 2 + 1 + START)
                    for blk in range(CB):
                        mm = t.transpose(ps[:, 5, blk * P:(blk + 1) * P], rq[:, blk, :], ident[:])
                    mm.then_inc(b_rq_t, 1)

                return [nothing, turn_out, lambda: ffn_key_gate(t, F[0], n), lambda: ffn_value(t, F[0], n), nothing,
                        turn_mid, projections, nothing, turn_qk, turn_rotated]

            chunks(t, pe_chunk, pe_background)

            t.wait_ge(b_rqt, NC + START)
            t.wait_ge(b_r1, 2 * NC + START)

            def den(s, gi, ih, bank):
                h, jb = gi % 2, gi // 2
                return t.matmul(ps[:, bank, :], ks[0:KROWS, s, h, jb * P:(jb + 1) * P],
                                qs[0:KROWS, s, h, ih * 512:(ih + 1) * 512], start=True, stop=True)

            def den_a(i, s, n):
                no = turn_no(i, s) * NA + n
                bank = 2 * ((s * NA + n) % 2)
                if_any(t, ln_done, no - 1)
                gi = ACT_LIST[n]
                if gi == 15:
                    mm = den(s, gi, 1, bank)
                else:
                    den(s, gi, 0, bank)
                    mm = den(s, gi, 1, bank + 1)
                mm.then_inc(den_act, 1)

            def output(i, s, j, bank):
                t.wait_ge(g_done[s], i + 1 + START)
                p = turn_no(i, s) % NP_
                for blk in range(CB):
                    at = (j * CB + blk) * P
                    mm = t.matmul(ps[:, bank, blk * P:(blk + 1) * P], g_sb[:, s, at:at + P],
                                  wout[:, bass.ds(p, 1), :].rearrange("p a e -> p (a e)"), start=True, stop=True)
                return mm

            def item(i, s, k):
                items, base = items_of(turn_no(i, s))
                kind, j = items[k]
                bank = 4 + (s + k) % 2
                if_any(t, item_done, base + k - 1)
                if kind == "U":
                    mm = den(s, 4 * (j // 2) + 3, j % 2, bank)
                else:
                    mm = output(*before(i, s), j, bank)
                mm.then_inc(item_ps, 1)

            def items(i, s, names):
                lst, _ = items_of(turn_no(i, s))
                for x in names:
                    if x in lst:
                        item(i, s, lst.index(x))

            def z(i, s, jb, ih):
                it, m = turn_no(i, s), jb // 2
                t.wait_ge(r_act, it * NA + 3 * m + (2 if jb % 2 == 0 else 3 if m < 3 else 4))
                if jb % 2:
                    lst, base = items_of(it)
                    t.wait_ge(item_done, base + lst.index(("U", 2 * m + ih if m < 3 else 6)) + 1)
                for h in range(2):
                    mm = t.matmul(ps[D * h:D * (h + 1), 6 + ih, :], wf[:, s, h, jb].rearrange("p a d -> p (a d)"),
                                  r_buf[:, 4 * (m % 2) + 2 * (jb % 2) + h, ih * 512:(ih + 1) * 512],
                                  start=(jb == 0), stop=(jb == BLK - 1))
                return mm

            ORDER = ["u a a z z u a z z", "u u a a z z u a z z", "u a a z z u a z z a", "u a a z z u a z z"]

            def next_turn(i, s):
                return (i, 1) if s == 0 else (i + 1, 0)

            def turn_pe(i, s):
                it = turn_no(i, s)
                more = s == 0 or not isinstance(i, int) or i < NI - 1
                lst, _ = items_of(it)
                ahead_a = [(i, s, n) for n in range(3, NA)] + ([(*next_turn(i, s), n) for n in range(3)] if more else [])
                ahead_u = [(i, s, k) for k in range(2, len(lst))] + ([(*next_turn(i, s), k) for k in range(2)] if more else [])
                done, waited = 0, False
                for m in range(4):
                    for x in ORDER[m].split():
                        if x in ("a", "u"):
                            if not {"a": ahead_a, "u": ahead_u}[x]:
                                continue
                            which = {"a": ahead_a, "u": ahead_u}[x].pop(0)
                            if which[1] != s and not waited:
                                t.wait_ge(stack_in[which[1]], (which[0] + 1) * 192)
                                waited = True
                            {"a": den_a, "u": item}[x](*which)
                        elif x == "z":
                            if done == 0:
                                t.wait_ge(wf_done, it + 1)
                                pi, ps_ = before(i, s)
                                if_any(t, z_ev[ps_], pi + 1)
                            mm = z(i, s, done // 2, done % 2)
                            done += 1
                            if done % 4 == 0:
                                mm.then_inc(r_free, 1)

            t.wait_ge(stack_in[0], 192)
            items(0, 0, [("U", 0)])
            den_a(0, 0, 0)
            den_a(0, 0, 1)
            items(0, 0, [("U", 1)])
            den_a(0, 0, 2)
            turns(t, turn_pe)
            for j in range(2):
                t.wait_ge(item_done, NB * NP_ * PER - 2 + j - 1)
                output(NI - 1, 1, j, 4 + j).then_inc(item_ps, 1)
            t.wait_ge(item_done, NB * NP_ * PER - 2 + 2)
            t.wait_ge(r_act, NB * NP_ * NA)
            t.wait_ge(z_ev[1], NI)
            with t.Fori(0, HALVES) as hf:
                for part in (ffn_turn, ffn_key_gate, ffn_value):
                    for k, f in enumerate(F):
                        part(t, f, hf + (NC if k == 0 else 0))

        @block.scalar
        def _(act):
            a = nc.scalar
            start(a, "act")
            a.preload_act_table_set("natural_log_exp_and_others")
            for k in range(4):
                a.wait_ge(wu_ps, k + 1)
                src = ps[:, k, :].rearrange("p (g s w d) -> p g s w d", g=2, s=2, w=2)
                for w in range(2):
                    ins_ = a.copy(wu[:, w, 2 * k:2 * k + 2], src[:, :, :, w, :])
                ins_.then_inc(wu_ev, 1)
            a.wait_ge(mv0, 1)
            a.activation(lnv[:], mv[:, :, 1], ACT.Ln, bias=eps[:, 0:1]).then_inc(lnv0, 1)
            a.wait_ge(lnv0, 1)
            a.activation(rstd[:], lnv[:], ACT.Exp, scale=-0.5).then_inc(rstd0, 1)
            for k in range(4):
                a.wait_ge(wvo_ps, k + 1)
                bank = 6 + k if k < 2 else k - 2
                a.copy(wvo[:, 4 * k:4 * k + 4, :], ps[:, bank, :].rearrange("p (h e) -> p h e", h=4)).then_inc(wvo_ev, 1)
            for k in range(4):
                a.wait_ge(xt_ps, k + 1)
                a.copy(xT[:, k // 2, EDGE + CH * (k % 2):EDGE + CH * (k % 2 + 1)], ps[:, 2 + k, :]).then_inc(xt_ev, 1)
            def act_chunk(c, back):
                def evac_proj(p):
                    a.wait_ge(q_ps, c * NP_ + p + 1)
                    a.wait_ge(s_ps, c * NP_ + max(p - 1, 0) + START)
                    a.activation(qt[0:D, p % 2, 0, :], ps[0:D, 0, :], ACT.Identity, bias=cb_pair[0:D, p:p + 1])
                    a.activation(qt[D:P, p % 2, 1, :], ps[D:P, 0, :], ACT.Identity, bias=cb_pair[D:P, p:p + 1]).then_inc(q_ev, 1)
                    a.wait_ge(k_ps, c * NP_ + p + 1 + START)
                    for par in range(2):
                        rows = slice(D * par, D * par + D)
                        ins_ = a.activation(kt[rows, p % 2, par, :].rearrange("p (a t) -> p a t", a=2), ps[rows, 3:5, 0:KH],
                                            ACT.Identity, bias=brel[rows, 0:1])
                    ins_.then_inc(k_ev, 1)

                def exp_s(p):
                    a.wait_ge(sub_done, c * NP_ + p + 1)
                    a.wait_ge(pt_ps, c * NP_ + max(p - 1, 0) + START)
                    a.activation(pr[:, p % 2], sm[:, p % 2], ACT.Exp, scale=SCALE).then_inc(exp_done, 1)

                def evac_probs(p):
                    a.wait_ge(pt_ps, c * NP_ + p + 1 + START)
                    a.copy(pt[:, p, :], ps[:, 7, :]).then_inc(pt_ev, 1)

                def evac_windows(k5):
                    a.wait_ge(xw_ps, c * 5 + k5 + 1)
                    if k5 == 0:
                        a.wait_ge(pv_ps, c * 16 + START)
                    n = min(4, NX - 4 * k5)
                    a.copy(xw[:, 4 * k5:4 * k5 + n, :], ps[:, 5 + k5 % 3, 0:n * E].rearrange("p (w e) -> p w e", w=n)).then_inc(xw_ev, 1)

                steps = act_background(c - 1) if back else [nothing] * (NW // 2 + 2)
                evac_proj(0)
                for k5 in range(3):
                    evac_windows(k5)
                evac_proj(1)
                for k5 in range(3, 5):
                    evac_windows(k5)
                behind(a, b_rot, 2, c)
                behind(a, b_qk_t, 2, c)
                behind(a, b_r1, 2, c)
                for p in range(NP_ + 1):
                    if p >= 1:
                        exp_s(p - 1)
                    if p > 0 and p + 1 < NP_:
                        evac_proj(p + 1)
                    if p >= 2:
                        evac_probs(p - 2)
                evac_probs(NP_ - 1)
                steps[0]()
                for v in range(NW // 2):
                    a.wait_ge(pv_ps, c * 16 + 2 * v + 1 + START)
                    a.wait_ge(y_ps, c + START)
                    a.copy(zh_view(v, 0), ps[:, 2 * (v % 2), :].rearrange("p (w g t) -> p w g t", w=2, g=NP_)).then_inc(ze_ev, 1)
                    steps[v + 1]()
                steps[NW // 2 + 1]()

            def act_background(n):
                b, hf = n // HALVES, n % HALVES

                def turned():
                    a.wait_ge(lnb.t_ps, n + 1)
                    a.copy(x3t, ps[:, 5, :]).then_inc(lnb.t_ev, 1)

                def exp_neg():
                    for side in range(2):
                        a.wait_ge(b_min, n * 2 + side + 1)
                        a.activation(qk_neg[:, side], qk_neg[:, side], ACT.Exp).then_inc(b_exp, 1)

                def split():
                    a.wait_ge(parts_stored, n * 32 + START_DMA)
                    for side in range(2):
                        a.wait_ge(b_qk_t, n * 2 + side + 1 + START)
                        a.copy(parts[:, side, 0, :], ps[:, 6 + side, :]).then_inc(b_hi, 1)
                    for side in range(2):
                        a.wait_ge(b_r1, n * 2 + side + 1 + START)
                        a.copy(parts[:, side, 1, :], rest[:, side, :]).then_inc(b_mid, 1)

                def rotated():
                    a.wait_ge(b_rq_t, n + 1)
                    a.copy(rqt, ps[:, 5, :]).then_inc(b_rqt, 1)

                def first():
                    a.wait_ge(rq_stored, n * 16 + START_DMA)
                    ffn_act(a, F[0], n)

                return [lambda: ln_act(a, F[0], F[0].ln, n), lambda: ffn_turned(a, F[0], n, b, hf), first, nothing,
                        lambda: ln_act(a, F[0], lnb, n), turned, exp_neg, nothing, split, rotated]

            chunks(a, act_chunk, act_background)

            def parts_of(s, n):
                k = (s * NA + n) % 2
                gi = ACT_LIST[n]
                r = r_buf[:, gi % 8, :]
                if gi == 15:
                    return ps[:, 2 * k, :], r[:, 512:1024]
                return ps[:, 2 * k:2 * k + 2, :].rearrange("p a t -> p (a t)"), r

            def log(i, s, n):
                no = turn_no(i, s) * NA + n
                src, dst = parts_of(s, n)
                a.wait_ge(den_act, no + 1)
                a.wait_ge(r_free, turn_no(i, s) * 4 + ACT_LIST[n] // 4 - 1 + RF)
                a.activation(dst, src, ACT.Ln).then_inc(ln_done, 1)

            def inv(i, s, n):
                no = turn_no(i, s) * NA + n
                _, dst = parts_of(s, n)
                a.wait_ge(ln_done, no + 1)
                a.activation(dst, dst, ACT.Exp, scale=-1.0).then_inc(r_act, 1)

            def copy_sums(i, s):
                a.wait_ge(r_free, (turn_no(i, s) + 1) * 4 + RF)
                a.wait_ge(g_done[s], i + START)
                a.copy(z_sb[:, s, :], ps[:, 6:8, :].rearrange("p a t -> p (a t)")).then_inc(z_ev[s], 1)

            def turn_act(i, s):
                last = isinstance(i, int) and i == NI - 1 and s == 1
                for n in range(NA):
                    if n + 1 < NA:
                        log(i, s, n + 1)
                    elif not last:
                        log(*((i, 1) if s == 0 else (i + 1, 0)), 0)
                    inv(i, s, n)
                    if n == 1 and not (isinstance(i, int) and i == 0 and s == 0):
                        copy_sums(*before(i, s))

            log(0, 0, 0)
            turns(a, turn_act)
            copy_sums(NI - 1, 1)
            a.wait_ge(rq_stored, NC * 16 + START_DMA)
            with a.Fori(0, HALVES) as hf:
                n_of = [hf + NC, hf]
                for f, n in zip(F, n_of):
                    ln_act(a, f, f.ln, n)
                for k, (f, n) in enumerate(zip(F, n_of)):
                    ffn_turned(a, f, n, k, hf)
                for f, n in zip(F, n_of):
                    ffn_act(a, f, n)

        @block.vector
        def _(dve):
            d = nc.vector
            start(d, "dve")
            d.memset(eps[:], EPS).then_inc(small_ready, 1)
            d.wait_ge(x_loaded, 16)
            for k in range(NB * BLK):
                ins_ = d.bn_stats(stat[:, k, :], x_tok[:, k, :])
            ins_.then_inc(st0, 1)
            d.wait_ge(st0, 1)
            d.wait_ge(small_ready, 1)
            for k in range(NB * BLK):
                ins_ = d.bn_aggr(mv[:, k, :], stat[:, k, :])
            ins_.then_inc(mv0, 1)
            d.wait_ge(w_loaded, W_ALL)
            d.tensor_tensor(bias_gap[:], rb_t[:], cb_t[:], ALU.subtract).then_inc(gap_ready, 1)
            d.tensor_copy(brel_wide[:], brel[0:D, 0:1].broadcast_to([D, P])).then_inc(gap_ready, 1)
            d.tensor_scalar(mu_rest[:], mu[:], -1.0, 1.0, ALU.mult, ALU.add).then_inc(small_ready, 1)
            d.wait_ge(ub_ps, 1)
            for w in range(2):
                src = ps[:, 4, w * H:(w + 1) * H].rearrange("p (g two) -> p g two", two=2)
                d.tensor_copy(u_bias[0:D, w, :], src[0:D, :, 1])
                ins_ = d.tensor_copy(u_bias[D:P, w, :], src[D:P, :, 0])
            ins_.then_inc(ub_ev, 2)
            d.wait_ge(ub_ps, 2)
            d.tensor_copy(head_const[:], ps[:, 5, 0:H]).then_inc(ub_ev, 1)
            d.wait_ge(rstd0, 1)
            for k in range(NB * BLK):
                ins_ = d.tensor_scalar(xn[:, k, :], x_tok[:, k, :], mv[:, k, 0:1], rstd[:, k:k + 1], ALU.subtract, ALU.mult)
                if k % 8 == 7:
                    ins_.then_inc(xn0, 1)
            d.wait_ge(ub_ev, 3)
            d.wait_ge(small_ready, 2)
            d.wait_ge(cleared, 4)
            d.wait_ge(xt_ev, 4)
            def dve_chunk(c, back):
                b, hf = c // HALVES, c % HALVES
                def rotate(p):
                    d.wait_ge(u_ps, c * NP_ + p + 1)
                    d.wait_ge(rot_done, c * NP_ + max(p - 1, 0) + START)
                    d.scalar_tensor_tensor(turn[:, p % 2, 0, :], ps[:, 1, :], u_bias[:, 0, p:p + 1], sin_q[:], ALU.add, ALU.mult)
                    d.scalar_tensor_tensor(turn[:, p % 2, 1, :], ps[:, 2, :], u_bias[:, 1, p:p + 1], cos_q[:],
                                           ALU.add, ALU.mult).then_inc(u_ev, 1)

                def mask_max(p):
                    d.wait_ge(s_ps, c * NP_ + p + 1 + START)
                    d.wait_ge(exp_done, c * NP_ + max(p - 1, 0) + START)
                    src = ps[:, 5 + p % 2, :].rearrange("p (k h w) -> p k h w", h=2, w=WIN)
                    for par in range(2):
                        ins_ = d.scalar_tensor_tensor(sm[:, p % 2, :, par, :], src[:, :, par, :], head_const[:, 2 * p + par:2 * p + par + 1],
                                                      mask[:, bass.ds(hf, 1)].rearrange("p a k w -> p (a k) w"), ALU.add, ALU.add)
                    ins_.then_inc(s_masked, 1)
                    d.wait_ge(s_masked, c * NP_ + p + 1 + START)
                    d.tensor_reduce(mx[:, p % 2, :], sm[:, p % 2].rearrange("p k h w -> p (k h) w"), AX.X, ALU.max).then_inc(mx_done, 1)

                def total(p):
                    d.wait_ge(exp_done, c * NP_ + p + 1 + START)
                    d.tensor_reduce(tot[:, p % 2, :], pr[:, p % 2].rearrange("p k h w -> p (k h) w"), AX.X, ALU.add).then_inc(sum_done, 1)
                    d.wait_ge(sum_done, c * NP_ + p + 1)
                    d.wait_ge(norm_done, c * NP_ + max(p - 1, 0) + START)
                    d.reciprocal(rtot[:, p % 2, :], tot[:, p % 2, :]).then_inc(rec_done, 1)

                steps = dve_background(c - 1) if back else [nothing] * (NW // 2 + 2)
                d.wait_ge(k_ps, c * NP_ + START)
                if back:
                    d.wait_ge(xw_ps, c * 5)
                d.tensor_copy(xc[:], xT[:, bass.ds(b, 1), bass.ds(hf * CH, XC)].rearrange("p a t -> p (a t)")).then_inc(xc_ready, 1)
                behind(d, b_exp, 2, c)
                behind(d, b_elu, 1, c)
                behind(d, b_mid, 2, c)
                behind(d, b_lo, 2, c)
                behind(d, b_qkv, 3, c)
                rotate(0)
                for p in range(NP_ + 1):
                    if p + 1 < NP_:
                        rotate(p + 1)
                    if p >= 1:
                        total(p - 1)
                    if p < NP_:
                        mask_max(p)
                steps[0]()
                for v in range(NW // 2):
                    d.wait_ge(pv_ps, c * 16 + 2 * v + 2 + START)
                    d.wait_ge(y_ps, c + START)
                    d.tensor_copy(zh_view(v, 1), ps[:, 2 * (v % 2) + 1, :].rearrange("p (w g t) -> p w g t", w=2, g=NP_)).then_inc(zo_ev, 1)
                    steps[v + 1]()
                d.wait_ge(y_ps, c + 1 + START)
                d.tensor_tensor(x1[:], ps[:, 4, :].rearrange("p (k e) -> p k e", e=E), x_tok[:, bass.ds(c * CB, CB), :],
                                ALU.add).then_inc(x1_done, 1)

            def dve_background(n):
                b, hf = n // HALVES, n % HALVES
                x_c = x_mid[:, bass.ds(n * CB, CB), :]
                mid = lambda k: x_mid[:, bass.ds(n * CB + k, 1), :].rearrange("p a e -> p (a e)")
                bias = lambda side: bqkv[:, side * E:(side + 1) * E].unsqueeze(1).broadcast_to([P, CB, E])

                def norm_in():
                    d.wait_ge(x1_done, n + 1 + START)
                    ln_stats(d, F[0], F[0].ln, n, lambda k: x1[:, k, :])
                    ln_apply(d, F[0], F[0].ln, n, lambda k: x1[:, k, :])

                def mix():
                    d.wait_ge(b_rot, 2 * n + START)
                    ffn_mix(d, F[0], n, b, hf)

                def gate_norm():
                    ffn_gate(d, F[0], n, x1[:], x_c)
                    d.wait_ge(F[0].s_out, n + 1)
                    ln_stats(d, F[0], lnb, n, mid)
                    ln_apply(d, F[0], lnb, n, mid)
                    d.wait_ge(lnb.xh, n + 1)
                    d.tensor_tensor(x_c, x_c, bout[:].unsqueeze(1).broadcast_to([P, CB, E]), ALU.add).then_inc(b_bias, 1)

                def add_bias():
                    for side in range(3):
                        dst = qkv[:, side] if side < 2 else v_tok[:, bass.ds(n * CB, CB), :]
                        d.wait_ge(b_qkv_ps, n * 3 + side + 1)
                        d.tensor_tensor(dst, ps[:, 5 + side, :].rearrange("p (k e) -> p k e", e=E), bias(side), ALU.add).then_inc(b_qkv, 1)
                        if side < 2:
                            d.wait_ge(b_qkv, n * 3 + side + 1 + START)
                            d.tensor_scalar(qk_neg[:, side], qkv[:, side].rearrange("p k n -> p (k n)"), 0.0, None, ALU.min).then_inc(b_min, 1)

                def elu_one():
                    d.wait_ge(b_exp, n * 2 + 2 + START)
                    flat = qkv[:].rearrange("p a k n -> p (a k n)")
                    d.scalar_tensor_tensor(flat, flat, 0.0, qk_neg[:].rearrange("p a t -> p (a t)"), ALU.max, ALU.add).then_inc(b_elu, 1)

                def split():
                    for side in range(2):
                        d.wait_ge(b_hi, n * 2 + side + 1 + START)
                        d.tensor_tensor(rest[:, side, :], ps[:, 6 + side, :], parts[:, side, 0, :], ALU.subtract).then_inc(b_r1, 1)
                    for side in range(2):
                        d.wait_ge(b_mid, n * 2 + side + 1 + START)
                        d.wait_ge(b_r1, n * 2 + side + 1 + START)
                        d.tensor_tensor(parts[:, side, 2, :], rest[:, side, :], parts[:, side, 1, :], ALU.subtract).then_inc(b_lo, 1)

                return [norm_in, mix, nothing, lambda: ffn_sigmoid(d, F[0], n), gate_norm,
                        nothing, add_bias, elu_one, split, nothing]

            chunks(d, dve_chunk, dve_background)

            def take(i, s, k):
                it = turn_no(i, s)
                lst, base = items_of(it)
                kind, j = lst[k]
                bank = 4 + (s + k) % 2
                if kind == "U":
                    m = j // 2
                    d.wait_ge(r_free, it * 4 + m - 1 + RF)
                    d.wait_ge(item_ps, base + k + 1)
                    d.reciprocal(r_buf[:, (4 * m + 3) % 8, (j % 2) * 512:(j % 2 + 1) * 512], ps[:, bank, :]).then_inc(item_done, 1)
                else:
                    b = turn_no(*before(i, s)) // NP_
                    at = x_mid[:, bass.ds(b * BLK + j * CB, CB), :]
                    d.wait_ge(item_ps, base + k + 1)
                    if_any(d, item_done, base + k + 1 - PER + (1 if isinstance(it, int) and it <= 1 else 0))
                    d.tensor_tensor(at, ps[:, bank, :].rearrange("p (k e) -> p k e", e=E), at, ALU.add).then_inc(item_done, 1)

            def turn_dve(i, s):
                for k in range(len(items_of(turn_no(i, s))[0])):
                    take(i, s, k)

            d.wait_ge(b_bias, NB * (NT // CH))
            turns(d, turn_dve)
            total = NB * NP_ * PER - 2
            for j in range(2):
                b = NB - 1
                at = x_mid[:, b * BLK + j * CB:b * BLK + (j + 1) * CB, :]
                d.wait_ge(item_ps, total + j + 1)
                d.wait_ge(item_done, total)
                d.tensor_tensor(at, ps[:, 4 + j, :].rearrange("p (k e) -> p k e", e=E), at, ALU.add).then_inc(item_done, 1)
            d.wait_ge(item_done, total + 2)
            with d.Fori(0, HALVES) as hf:
                def half(k):
                    return [(x_mid[:, bass.ds(k * BLK + hf * CB + j, 1), :].rearrange("p a e -> p (a e)")) for j in range(CB)]
                sets = [(f, hf + (NC if k == 0 else 0), k, half(k).__getitem__) for k, f in enumerate(F)]
                for f, n, k, src in sets:
                    ln_stats(d, f, f.ln, n, src)
                for f, n, k, src in sets:
                    ln_apply(d, f, f.ln, n, src)
                for f, n, k, src in sets:
                    ffn_mix(d, f, n, k, hf)
                for f, n, k, src in sets:
                    ffn_sigmoid(d, f, n)
                for f, n, k, src in sets:
                    d.wait_ge(out_stored[k], hf * 16 + START_DMA)
                    ffn_gate(d, f, n, x_mid[:, bass.ds(k * BLK + hf * CB, CB), :], f.out)


def kernel(**inputs):
    import concourse.bacc as bacc
    from concourse.bass_utils import run_bass_kernel_spmd

    nc = bacc.Bacc("TRN2", target_bir_lowering=False, num_devices=1)
    arrays = {k: np.ascontiguousarray(v) for k, v in layouts(inputs).items()}
    arrays.update({k: np.ascontiguousarray(v.astype(np.float32)) for k, v in constants().items()})
    named = {f"in_{k}": v for k, v in arrays.items()}
    ins = {k: nc.dram_tensor(f"in_{k}", v.shape, mybir.dt.from_np(v.dtype), kind="ExternalInput").ap() for k, v in arrays.items()}
    out = nc.dram_tensor("out", [NB * NT // CH, P, CB, E], F32, kind="ExternalOutput").ap()
    split = nc.dram_tensor("split_parts", [2, NB, PARTS, P, NT], BF16, kind="Internal").ap()
    rq = nc.dram_tensor("rotated_q", [NB, P, NT], F32, kind="Internal").ap()
    program(nc, ins, out, split, rq)
    r = run_bass_kernel_spmd(nc, [named], core_ids=[0])
    got = np.asarray(r.results[0]["out"])
    return got.transpose(0, 2, 1, 3).reshape(NB, NT, E)
```

```python
from contextlib import ExitStack

import numpy as np
import concourse.bass as bass
from concourse import mybir

P = 128
E = 128
NB, NT = 2, 1024
BLK = NT // P
H, D = 16, 64
NP_ = H // 2
CH = 512
CB = CH // P
NC = NB * NT // CH
HALVES = NT // CH
HALO = 16
SUB = 32
WIN = SUB + 2 * HALO
NW = CH // SUB
CK = CH + 2 * HALO
KH = CK // 2
SIDE = WIN
EDGE = HALO + SIDE
XC = CK + 2 * SIDE
NX = NW + 2
HB, DB = 16, 8
PARTS = 3
KROWS = PARTS * PARTS * DB
EPS = 1e-5
INF = 10000.0
SCALE = 1.0 / float(np.sqrt(np.float32(H * D)))

ALU = mybir.AluOpType
ACT = mybir.ActivationFunctionType
AX = mybir.AxisListType
F32 = mybir.dt.float32
BF16 = mybir.dt.bfloat16


def constants():
    inv = (1.0 / np.float32(10000.0) ** (np.arange(0, D, 2, dtype=np.float32) / np.float32(D))).astype(np.float64)
    q_angle = inv[:, None] * np.arange(CH)[None, :]
    k_angle = inv[:, None] * (np.arange(CK) - HALO)[None, :]
    sin_q = np.concatenate([np.sin(q_angle)] * 4, 0)
    cos_q = np.concatenate([np.cos(q_angle), -np.cos(q_angle)] * 2, 0)
    enc_k = np.concatenate([np.cos(k_angle), np.sin(k_angle)], 0)
    mask = np.zeros((P, NT // CH, CB, WIN), np.float32)
    for half in range(NT // CH):
        for blk in range(CB):
            for p in range(P):
                ql = p % SUB
                rel = np.arange(WIN)
                key = half * CH + blk * P + (p // SUB) * SUB - HALO + rel
                ok = (rel >= ql) & (rel - ql <= 2 * HALO) & (key >= 0) & (key < NT)
                mask[p, half, blk] = np.where(ok, 0.0, -INF / SCALE)
    theta = (1.0 / np.float32(1250.0) ** (np.arange(0, DB // 2, dtype=np.float32) / np.float32(DB // 2))).astype(np.float32)
    angle = (np.arange(NT, dtype=np.float32)[:, None] * theta[None, :]).astype(np.float32).astype(np.float64)
    rot_cos = np.repeat(np.cos(angle), 2, axis=1)
    rot_sin = np.stack([-np.sin(angle), np.sin(angle)], -1).reshape(NT, DB)
    rows = lambda a: a.reshape(BLK, P, DB).transpose(1, 0, 2)
    return {
        "ident": np.eye(P), "sin_q": sin_q, "cos_q": cos_q, "enc_k": enc_k, "mask": mask,
        "rot_cos": rows(rot_cos), "rot_sin": rows(rot_sin),
    }


def layouts(i):
    a = {k: np.asarray(v) for k, v in i.items()}
    rel_t = a["L0_attn_a_W_rel"].T
    rel_sw = np.concatenate([rel_t[:, D // 2:], rel_t[:, :D // 2]], 1)
    heads_t = lambda w: w.reshape(E, H, D).transpose(2, 1, 0)
    w_out = a["L0_attn_b_w_out"].reshape(HB // 2, 2, 1, DB, E)
    w_out = np.broadcast_to(w_out, (HB // 2, 2, DB, DB, E)).reshape(HB // 2, P, E).transpose(1, 0, 2)
    return {
        "x": a["L0_attn_a_x"].reshape(NB * BLK, P, E).transpose(1, 0, 2),
        "wq": a["L0_attn_a_W_q"], "wk": a["L0_attn_a_W_k"],
        "wq_t": heads_t(a["L0_attn_a_W_q"]), "wv_t": heads_t(a["L0_attn_a_W_v"]),
        "wo": a["L0_attn_a_W_o"].reshape(H, D, E).transpose(1, 0, 2),
        "rel": np.concatenate([rel_t, rel_t, rel_sw, rel_sw], 1),
        "cb_pair": a["L0_attn_a_content_bias"].reshape(NP_, P).T,
        "cb_t": a["L0_attn_a_content_bias"].T, "rb_t": a["L0_attn_a_relative_bias"].T,
        "brel": np.tile(a["L0_attn_a_b_rel"], 2)[:, None],
        "bo": a["L0_attn_a_b_o"][None, :],
        "wr_t": a["L0_ffn_W_r"].T, "wk_t": a["L0_ffn_W_k"].T, "wv2_t": a["L0_ffn_W_v"].T,
        "mu": np.stack([a["L0_ffn_mu_r"], a["L0_ffn_mu_k"]], 1),
        "wqkv": a["L0_attn_b_w_qkv"], "bqkv": np.broadcast_to(a["L0_attn_b_b_qkv"], (P, 3 * HB * DB)),
        "wout": w_out, "bout": np.broadcast_to(a["L0_attn_b_b_out"], (P, E)),
    }


class NormSems:
    def __init__(self, sem, name):
        (self.st, self.mv, self.lnv, self.rstd, self.xh, self.t_ps, self.t_ev) = (
            sem(f"{name}_{n}") for n in ("st", "mv", "lnv", "rstd", "xh", "t_ps", "t_ev"))


class FfnSet:
    def __init__(self, sem, name, banks, xh, out, mix, prev, k, e, s, stats):
        self.gate_bank, self.key_bank, self.value_bank = banks
        self.xh, self.out, self.mix, self.prev, self.k, self.e, self.s = xh, out, mix, prev, k, e, s
        self.stat, self.mv, self.lnv, self.rstd = stats
        self.ln = NormSems(sem, name)
        (self.s_prev, self.s_mix, self.s_r_ps, self.s_k_ps, self.s_relu, self.s_sq, self.s_exp, self.s_one, self.s_sig,
         self.s_v_ps, self.s_gate, self.s_out) = (
            sem(f"{name}_{n}") for n in "prev mix r_ps k_ps relu sq exp one sig v_ps gate out".split())


def program(nc, ins, out_dram, split_dram, rq_dram):
    ctx = ExitStack()
    with ctx:
        def sb(name, shape, dt=F32):
            return ctx.enter_context(nc.sbuf_tensor(name, shape, dt))

        def sem(name):
            return ctx.enter_context(nc.semaphore(name))

        ps = ctx.enter_context(nc.psum_tensor("ps", [P, 8, 512], F32))

        x_tok = sb("x_tok", [P, NB * BLK, E])
        ident = sb("ident", [P, P])
        wq = sb("wq_sb", [P, H * D])
        wk = sb("wk_sb", [P, H * D])
        rel = sb("rel_sb", [D, 4 * D])
        cb_pair = sb("cb_pair_sb", [P, NP_])
        cb_t = sb("cb_t_sb", [D, H])
        rb_t = sb("rb_t_sb", [D, H])
        brel = sb("brel_sb", [P, 1])
        bo = sb("bo_sb", [1, E])
        bout = sb("bout_sb", [P, E])
        wr_t = sb("wr_t_sb", [P, E])
        wk_t = sb("wk_t_sb", [P, E])
        wv2_t = sb("wv2_t_sb", [P, E])
        mu = sb("mu_sb", [P, 2])
        wqkv = sb("wqkv_sb", [P, 3 * E])
        bqkv = sb("bqkv_sb", [P, 3 * E])
        wout = sb("wout_sb", [P, NP_, E])
        sin_q = sb("sin_q_sb", [P, CH])
        cos_q = sb("cos_q_sb", [P, CH])
        mask = sb("mask_sb", [P, NT // CH, CB, WIN])
        rot_cos = sb("rot_cos_sb", [P, BLK, DB])
        rot_sin = sb("rot_sin_sb", [P, BLK, DB])

        wu = sb("wu", [P, 2, NP_, 2, D])
        u_bias = sb("u_bias", [P, 2, NP_])
        head_const = sb("head_const", [P, H])
        bias_gap = sb("bias_gap", [D, H])
        brel_wide = sb("brel_wide", [D, P])
        ones = sb("ones", [1, P])
        mu_rest = sb("mu_rest", [P, 2])
        wvo = sb("wvo", [P, H, E])
        eps = sb("eps", [P, 1])
        idle = sb("idle", [P, 2])
        xT = sb("xT", [P, NB, NT + 2 * EDGE])

        xc = sb("xc", [P, XC])
        qt = sb("qt", [P, 2, 2, CH])
        kt = sb("kt", [P, 2, 2, CK])
        mx = sb("mx", [P, 2, CB * 2])
        tot = sb("tot", [P, 2, CB * 2])
        rtot = sb("rtot", [P, 2, CB * 2])
        xw = sb("xw", [P, NX, E])
        arena = sb("arena", [P, 16384])
        zh = arena[:, 0:8192].rearrange("p (h t) -> p h t", h=H)
        pt = arena[:, 8192:12288].rearrange("p (g t) -> p g t", g=NP_)
        turn = arena[:, 12288:14336].rearrange("p (b k t) -> p b k t", b=2, k=2)
        sm = arena[:, 14336:15360].rearrange("p (b k h w) -> p b k h w", b=2, k=CB, h=2)
        pr = arena[:, 15360:16384].rearrange("p (b k h w) -> p b k h w", b=2, k=CB, h=2)
        wq_t = arena[0:D, 0:2048].rearrange("p (h e) -> p h e", h=H)
        wv_t = arena[0:D, 2048:4096].rearrange("p (h e) -> p h e", h=H)
        wo = arena[0:D, 4096:6144].rearrange("p (h e) -> p h e", h=H)
        xn = arena[:, 6144:8192].rearrange("p (k e) -> p k e", e=E)
        z_sb = arena[:, 0:2048].rearrange("p (s t) -> p s t", s=2)
        g_sb = arena[:, 2048:4096].rearrange("p (s t) -> p s t", s=2)
        r_buf = arena[:, 4096:12288].rearrange("p (g t) -> p g t", g=8)

        stat = sb("stat", [P, NB * BLK, 6])
        mv = sb("mv", [P, NB * BLK, 2])
        lnv = sb("lnv", [P, NB * BLK])
        rstd = sb("rstd", [P, NB * BLK])
        x1 = sb("x1", [P, CB, E])
        xh = sb("xh", [P, CB, E])
        fx = sb("fx", [P, NB, NT + 1])
        x_mid = x_tok
        second = lambda lo, hi: arena[:, 12288 + lo * CH:12288 + hi * CH]
        pair_of = lambda v: v.rearrange("p (a t) -> p a t", a=2)
        blocks_of = lambda v: v.rearrange("p (k e) -> p k e", e=E)
        F = [FfnSet(sem, "f0", (0, 1, 4), xh[:], x1[:], sb("fmix", [P, 2, CH])[:], sb("fprev", [P, 2, CH])[:],
                    sb("fk", [P, CH])[:], sb("fe", [P, CH])[:], sb("fs", [P, CH])[:], (stat, mv, lnv, rstd)),
             FfnSet(sem, "f1", (2, 3, 5), blocks_of(second(0, 1)), blocks_of(second(1, 2)), pair_of(second(2, 4)),
                    pair_of(second(4, 6)), xT[:, 0, 0:CH], second(6, 7), second(7, 8),
                    (stat[:, CB:], mv[:, CB:], lnv[:, CB:], rstd[:, CB:]))]
        x3t = arena[:, 12288:12800]
        qk_neg = arena[:, 12800:13824].rearrange("p (a t) -> p a t", a=2)
        rest = arena[:, 14336:15360].rearrange("p (a t) -> p a t", a=2)
        qkv = arena[:, 15360:16384].rearrange("p (a k n) -> p a k n", a=2, k=CB)
        rqt = F[0].e
        rq = sb("rq", [P, CB, E])
        rk = sb("rk", [P, NB * BLK, E])
        v_tok = sb("v_tok", [P, NB * BLK, E])
        parts = sb("parts", [P, 2, PARTS, CH], BF16)

        qs = wu[:].rearrange("p a g s d -> p (a g s d)").bitcast(BF16).rearrange("p (b h t) -> p b h t", b=2, h=2)
        ks = wvo[:].rearrange("p h e -> p (h e)").bitcast(BF16).rearrange("p (b h t) -> p b h t", b=2, h=2)
        rqx = qt[:].rearrange("p b h t -> p b (h t)")
        wf = xw[:].rearrange("p w e -> p (w e)")[:, 0:2 * 2 * BLK * DB * DB].rearrange("p (s h k a d) -> p s h k a d", s=2, h=2, k=BLK, a=DB)

        x_loaded, enc_loaded = sem("x_loaded"), sem("enc_loaded")
        cleared, small_ready, gap_ready = sem("cleared"), sem("small_ready"), sem("gap_ready")
        wu_ps, wu_ev, ub_ps, ub_ev, wvo_ps, wvo_ev = map(sem, ("wu_ps", "wu_ev", "ub_ps", "ub_ev", "wvo_ps", "wvo_ev"))
        st0, mv0, lnv0, rstd0, xn0, xt_ps, xt_ev = map(sem, ("st0", "mv0", "lnv0", "rstd0", "xn0", "xt_ps", "xt_ev"))
        names = ("xc_ready xw_ps xw_ev q_ps u_ps k_ps q_ev u_ev k_ev rot_half rot_done s_ps s_masked mx_done sub_done "
                 "exp_done sum_done rec_done norm_done pt_ps pt_ev pv_ps ze_ev zo_ev y_ps x1_done").split()
        (xc_ready, xw_ps, xw_ev, q_ps, u_ps, k_ps, q_ev, u_ev, k_ev, rot_half, rot_done, s_ps, s_masked, mx_done, sub_done,
         exp_done, sum_done, rec_done, norm_done, pt_ps, pt_ev, pv_ps, ze_ev, zo_ev, y_ps, x1_done) = map(sem, names)
        lnb = NormSems(sem, "b")
        ln_end = [NormSems(sem, f"end{b}") for b in range(NB)]
        f_exp, f_relu, f_gate = F[0].s_exp, F[0].s_relu, F[0].s_gate
        names = ("b_qkv_ps b_qkv b_min b_exp b_elu b_t2 b_rot b_qk_t b_rq_t b_hi b_r1 b_mid b_lo b_rqt "
                 "parts_stored rq_stored").split()
        (b_qkv_ps, b_qkv, b_min, b_exp, b_elu, b_t2, b_rot, b_qk_t, b_rq_t, b_hi, b_r1, b_mid, b_lo, b_rqt,
         parts_stored, rq_stored) = map(sem, names)
        names = "wf_done den_act ln_done r_act r_free item_ps item_done b_bias".split()
        (wf_done, den_act, ln_done, r_act, r_free, item_ps, item_done, b_bias) = map(sem, names)
        out_stored = [sem(f"out_stored{k}") for k in range(NB)]
        stack_in, rqx_in, z_ev, g_done = ([sem(f"{n}{s}") for s in range(2)]
                                                  for n in ("stack_in", "rqx_in", "z_ev", "g_done"))

        loads = {
            "ident": [(ident, "ident")],
            "fold": [(wq_t, "wq_t"), (rel, "rel"), (rb_t, "rb_t"), (cb_t, "cb_t"), (brel, "brel"), (mu, "mu")],
            "value": [(wv_t, "wv_t"), (wo, "wo")],
            "band": [(wq, "wq"), (wk, "wk"), (cb_pair, "cb_pair"), (sin_q, "sin_q"), (cos_q, "cos_q"), (mask, "mask")],
            "rest": [(bo, "bo"), (bout, "bout"), (wr_t, "wr_t"), (wk_t, "wk_t"), (wv2_t, "wv2_t"), (wqkv, "wqkv"),
                     (bqkv, "bqkv"), (rot_cos, "rot_cos"), (rot_sin, "rot_sin"), (wout, "wout")],
        }
        loaded = {name: sem(f"{name}_loaded") for name in loads}

        def wait_loads(eng, *names):
            for name in names:
                eng.wait_ge(loaded[name], 16 * len(loads[name]))

        def zh_view(v, par):
            return zh[:, par::2, 2 * v * SUB:(2 * v + 2) * SUB].rearrange("p g (w t) -> p w g t", w=2)

        def ln_stats(d, f, q, n, src):
            d.memset(idle[:, 0:1], 0.0)
            for blk in range(CB):
                ins_ = d.bn_stats(f.stat[:, blk, :], src(blk))
            ins_.then_inc(q.st, 1)
            d.wait_ge(q.st, n + 1)
            d.memset(idle[:, 1:2], 0.0)
            for blk in range(CB):
                ins_ = d.bn_aggr(f.mv[:, blk, :], f.stat[:, blk, :])
            ins_.then_inc(q.mv, 1)

        def ln_apply(d, f, q, n, src):
            d.wait_ge(q.mv, n + 1)
            d.wait_ge(q.rstd, n + 1)
            for blk in range(CB):
                ins_ = d.tensor_scalar(f.xh[:, blk, :], src(blk), f.mv[:, blk, 0:1], f.rstd[:, blk:blk + 1], ALU.subtract, ALU.mult)
            ins_.then_inc(q.xh, 1)

        def ln_act(a, f, q, n):
            a.wait_ge(q.mv, n + 1)
            a.activation(f.lnv[:, 0:CB], f.mv[:, 0:CB, 1], ACT.Ln, bias=eps[:, 0:1]).then_inc(q.lnv, 1)
            a.wait_ge(q.lnv, n + 1)
            a.activation(f.rstd[:, 0:CB], f.lnv[:, 0:CB], ACT.Exp, scale=-0.5).then_inc(q.rstd, 1)

        def fx_at(b, hf, back=0):
            return fx[:, bass.ds(b, 1), bass.ds(hf * CH + 1 - back, CH)].rearrange("p a t -> p (a t)")

        def ffn_turn(t, f, n):
            t.wait_ge(f.ln.xh, n + 1)
            t.wait_ge(f.s_exp, n + START)
            for blk in range(CB):
                mm = t.transpose(ps[:, f.gate_bank, blk * P:(blk + 1) * P], f.xh[:, blk, :], ident[:])
            mm.then_inc(f.ln.t_ps, 1)

        def ffn_key_gate(t, f, n):
            t.wait_ge(f.s_mix, n * 2 + 2)
            t.wait_ge(f.s_relu, n + START)
            t.matmul(ps[:, f.key_bank, :], wk_t[:], f.mix[:, 1, :], start=True, stop=True).then_inc(f.s_k_ps, 1)
            t.wait_ge(f.ln.t_ev, n + 1)
            for blk in range(CB):
                mm = t.matmul(ps[:, f.gate_bank, blk * P:(blk + 1) * P], f.mix[:, 0, blk * P:(blk + 1) * P], wr_t[:], start=True, stop=True)
            mm.then_inc(f.s_r_ps, 1)

        def ffn_value(t, f, n):
            t.wait_ge(f.s_sq, n + 1)
            t.wait_ge(f.s_gate, n + START)
            for blk in range(CB):
                mm = t.matmul(ps[:, f.value_bank, blk * P:(blk + 1) * P], f.k[:, blk * P:(blk + 1) * P], wv2_t[:], start=True, stop=True)
            mm.then_inc(f.s_v_ps, 1)

        def ffn_turned(a, f, n, b, hf):
            a.wait_ge(f.ln.t_ps, n + 1)
            a.copy(fx_at(b, hf), ps[:, f.gate_bank, :]).then_inc(f.ln.t_ev, 1)

        def relu_square(a, f, n):
            a.wait_ge(f.s_k_ps, n + 1)
            a.wait_ge(f.s_v_ps, n + START)
            a.activation(f.k, ps[:, f.key_bank, :], ACT.Relu).then_inc(f.s_relu, 1)
            a.wait_ge(f.s_relu, n + 1 + START)
            a.activation(f.k, f.k, ACT.Square).then_inc(f.s_sq, 1)

        def ffn_act(a, f, n):
            relu_square(a, f, n)
            a.wait_ge(f.s_r_ps, n + 1)
            a.wait_ge(f.s_one, n + START)
            a.activation(f.e, ps[:, f.gate_bank, :], ACT.Exp, scale=-1.0).then_inc(f.s_exp, 1)

        def ffn_mix(d, f, n, b, hf):
            d.wait_ge(f.ln.t_ev, n + 1)
            for k in (1, 0):
                d.tensor_scalar(f.prev[:, k, :], fx_at(b, hf, 1), mu_rest[:, k:k + 1], None, ALU.mult).then_inc(f.s_prev, 1)
            for m, k in enumerate((1, 0)):
                d.wait_ge(f.s_prev, n * 2 + m + 1)
                d.scalar_tensor_tensor(f.mix[:, k, :], fx_at(b, hf), mu[:, k:k + 1], f.prev[:, k, :], ALU.mult, ALU.add).then_inc(f.s_mix, 1)

        def ffn_sigmoid(d, f, n):
            d.wait_ge(f.s_exp, n + 1 + START)
            d.tensor_scalar(f.s, f.e, 1.0, None, ALU.add).then_inc(f.s_one, 1)
            d.wait_ge(f.s_one, n + 1 + START)
            d.reciprocal(f.s, f.s).then_inc(f.s_sig, 1)

        def ffn_gate(d, f, n, res, dst):
            d.wait_ge(f.s_sig, n + 1)
            d.wait_ge(f.s_v_ps, n + 1 + START)
            d.tensor_tensor(f.s, ps[:, f.value_bank, :], f.s, ALU.mult).then_inc(f.s_gate, 1)
            d.wait_ge(f.s_gate, n + 1 + START)
            d.tensor_tensor(dst, f.s.rearrange("p (k e) -> p k e", e=E), res, ALU.add).then_inc(f.s_out, 1)

        QUARTERS = [(F[1 - b], hf + (NC if b == 1 else 0), b, hf) for b in range(NB) for hf in range(HALVES)]

        def in_order(text, **parts):
            for word in text.split():
                parts[word[:-1]](*QUARTERS[int(word[-1])])

        def end_stats(d, b):
            d.memset(idle[:, 0:1], 0.0)
            for blk in range(b * BLK, (b + 1) * BLK):
                ins_ = d.bn_stats(stat[:, blk, :], x_mid[:, blk, :])
            ins_.then_inc(ln_end[b].st, 1)
            d.wait_ge(ln_end[b].st, 1)
            for blk in range(b * BLK, (b + 1) * BLK):
                ins_ = d.bn_aggr(mv[:, blk, :], stat[:, blk, :])
            ins_.then_inc(ln_end[b].mv, 1)

        def end_rstd(a, b):
            at = slice(b * BLK, (b + 1) * BLK)
            a.wait_ge(ln_end[b].mv, 1)
            a.activation(lnv[:, at], mv[:, at, 1], ACT.Ln, bias=eps[:, 0:1]).then_inc(ln_end[b].lnv, 1)
            a.wait_ge(ln_end[b].lnv, 1)
            a.activation(rstd[:, at], lnv[:, at], ACT.Exp, scale=-0.5).then_inc(ln_end[b].rstd, 1)

        WU_BANKS = (6, 7, 0, 1)
        VALUE_BANKS = (2, 0)

        START, START_DMA = 1, 16
        RF = 5
        first = {
            "sp": (parts_stored, rq_stored, *out_stored),
            "pool": (rot_done, norm_done, b_rot, g_done[0], g_done[1]),
            "pe": (s_ps, pt_ps, pv_ps, y_ps, k_ps, b_qk_t, *(f.s_v_ps for f in F)),
            "act": (q_ev, k_ev, pt_ev, b_rqt, b_hi, b_exp, b_mid, exp_done, *(f.s_exp for f in F), *(f.s_relu for f in F)),
            "dve": (u_ev, x1_done, s_masked, b_qkv, b_elu, b_r1, b_lo, *(f.s_gate for f in F), *(f.s_one for f in F)),
        }

        def start(eng, name):
            for s in first[name]:
                eng.sem_inc(s, START_DMA if name == "sp" else START)
            if name == "pe":
                eng.sem_inc(r_free, RF)

        NI = NB * NP_ // 2
        ACT_LIST = [0, 1, 2, 4, 5, 6, 8, 9, 10, 12, 13, 15, 14]
        NA = len(ACT_LIST)
        ITEMS = [("U", 0), ("U", 1), ("U", 2), ("U", 3), ("O", 0), ("U", 4), ("U", 5), ("O", 1), ("U", 6)]
        PER = len(ITEMS)

        def turn_no(i, s):
            return 2 * i + s

        def items_of(it):
            if isinstance(it, int) and it == 0:
                return [x for x in ITEMS if x[0] == "U"], 0
            return ITEMS, it * PER - 2

        def before(i, s):
            return (i, 0) if s else (i - 1, 1)

        def if_any(eng, s, n):
            if not isinstance(n, int) or n > 0:
                eng.wait_ge(s, n)

        def turns(eng, body):
            for s in range(2):
                body(0, s)
            with eng.Fori(1, NI - 1) as i:
                for s in range(2):
                    body(i, s)
            for s in range(2):
                body(NI - 1, s)

        def nothing():
            pass

        def chunks(eng, body, background, ahead={}):
            body(0, False)
            with eng.Fori(1, NC) as c:
                body(c, True)
            for k, step in enumerate(background(NC - 1)):
                if k in ahead:
                    ahead[k]()
                step()

        def item_bank(it, s, k):
            if isinstance(it, int) and it == 0:
                return 4 + (k + 1) % 2 if k else 4
            return 4 + (s + k) % 2

        def behind(eng, s, per, c):
            if not isinstance(c, int):
                eng.wait_ge(s, (c - 1) * per + START)

        block = ctx.enter_context(nc.Block())

        @block.sync
        def _(sp):
            start(sp, "sp")
            sp.dma_start(x_tok[:], ins["x"]).then_inc(x_loaded, 16)
            for group, items in loads.items():
                for dst, name in items:
                    sp.dma_start(dst[:] if not isinstance(dst, bass.AP) else dst, ins[name]).then_inc(loaded[group], 16)
            for buf in range(2):
                sp.dma_start(kt[D:P, buf, 0, :], ins["enc_k"]).then_inc(enc_loaded, 16)
                sp.dma_start(kt[0:D, buf, 1, :], ins["enc_k"]).then_inc(enc_loaded, 16)

            def store_projected(c):
                b, hf = c // HALVES, c % HALVES
                sp.wait_ge(b_lo, c * 2 + 2 + START)
                for w in range(2):
                    sp.dma_start(split_dram[w, bass.ds(b, 1), :, :, bass.ds(hf * CH, CH)].rearrange("a s p t -> p (a s) t"),
                                 parts[:, w]).then_inc(parts_stored, 16)
                sp.wait_ge(b_rqt, c + 1 + START)
                sp.dma_start(rq_dram[bass.ds(b, 1), :, bass.ds(hf * CH, CH)].rearrange("a p t -> p (a t)"),
                             rqt).then_inc(rq_stored, 16)

            def load_stacks(i, s, sides=(0, 1)):
                it = turn_no(i, s)
                for h in range(2):
                    b, row = it // NP_, ((it % NP_) * 2 + h) * DB
                    for side in sides:
                        dst = (qs, ks)[side]
                        src = split_dram[side, bass.ds(b, 1), :, bass.ds(row, DB), :].rearrange("a s p t -> (a s) p t")
                        src = src.unsqueeze(1 - side).broadcast_to([PARTS, PARTS, DB, NT])
                        for part in range(PARTS):
                            sp.dma_start(dst[part * PARTS * DB:(part + 1) * PARTS * DB, s, h, :],
                                         src[part]).then_inc(stack_in[s], 16)

            def load_rotated(i, s):
                it = turn_no(i, s)
                src = rq_dram[bass.ds(it // NP_, 1), bass.ds((it % NP_) * 16, 16), :].rearrange("a p t -> (a p) t")
                sp.dma_start(rqx[:, s, :], src.unsqueeze(1).broadcast_to([16, DB, NT])).then_inc(rqx_in[s], 16)

            with sp.Fori(0, NC - 1) as c:
                store_projected(c)
            sp.wait_ge(parts_stored, 2 * 16 * (NC - 1) + START_DMA)
            sp.wait_ge(rq_stored, 16 * (NC - 1) + START_DMA)
            sp.wait_ge(u_ps, NC * NP_)
            for s in range(2):
                load_stacks(0, s, (0,))
            sp.wait_ge(y_ps, NC + START)
            for s in range(2):
                load_stacks(0, s, (1,))
            for s in range(2):
                load_rotated(0, s)
            store_projected(NC - 1)
            sp.wait_ge(parts_stored, 2 * 16 * NC + START_DMA)
            sp.wait_ge(rq_stored, 16 * NC + START_DMA)
            with sp.Fori(1, NI) as i:
                for s in range(2):
                    sp.wait_ge(r_free, (turn_no(i, s) - 1) * 4 + RF)
                    load_stacks(i, s)
                    sp.wait_ge(g_done[s], i + START)
                    load_rotated(i, s)
            for q in (0, 2, 1, 3):
                f, n, b, hf = QUARTERS[q]
                sp.wait_ge(f.s_out, n + 1)
                sp.dma_start(out_dram[b * HALVES + hf], f.out).then_inc(out_stored[b], 16)
            for k in range(NB):
                sp.wait_ge(out_stored[k], 16 * HALVES + START_DMA)

        @block.gpsimd
        def _(pool):
            g = nc.gpsimd
            start(g, "pool")
            g.memset(xT[:, :, 0:EDGE], 0.0).then_inc(cleared, 1)
            g.memset(xT[:, :, EDGE + NT:], 0.0).then_inc(cleared, 1)
            g.memset(fx[:, :, 0:1], 0.0).then_inc(cleared, 1)
            g.memset(ones[:], 1.0).then_inc(cleared, 1)
            g.wait_ge(cleared, 4)
            def pool_chunk(c, back):
                def rot_add(p):
                    g.wait_ge(u_ev, c * NP_ + p + 1 + START)
                    if p >= 2:
                        g.wait_ge(s_ps, c * NP_ + p - 1 + START)
                    else:
                        g.wait_ge(s_ps, c * NP_ + START)
                    if p == 1:
                        g.wait_ge(rot_done, c * NP_ + 1 + START)
                    elif p >= 2:
                        g.wait_ge(sub_done, c * NP_ + p - 1)
                    g.tensor_tensor(qt[D:P, p % 2, 0, :], turn[D:P, p % 2, 0, :], turn[D:P, p % 2, 1, :],
                                    ALU.add).then_inc(rot_half, 1)
                    g.wait_ge(rot_half, c * NP_ + p + 1)
                    g.tensor_tensor(qt[0:D, p % 2, 1, :], turn[0:D, p % 2, 0, :], turn[0:D, p % 2, 1, :],
                                    ALU.add).then_inc(rot_done, 1)

                def sub_max(p):
                    v = sm[:, p % 2].rearrange("p k h w -> p (k h) w")
                    g.wait_ge(mx_done, c * NP_ + p + 1)
                    g.wait_ge(rot_done, c * NP_ + min(p + 2, NP_) + START)
                    g.tensor_tensor(v, v, mx[:, p % 2].unsqueeze(2).broadcast_to([P, CB * 2, WIN]),
                                    ALU.subtract).then_inc(sub_done, 1)

                def norm(p):
                    v = pr[:, p % 2].rearrange("p k h w -> p (k h) w")
                    g.wait_ge(rec_done, c * NP_ + p + 1)
                    g.wait_ge(rot_done, c * NP_ + min(p + 3, NP_) + START)
                    g.tensor_tensor(v, v, rtot[:, p % 2].unsqueeze(2).broadcast_to([P, CB * 2, WIN]),
                                    ALU.mult).then_inc(norm_done, 1)

                g.wait_ge(norm_done, c * NP_ + START)
                behind(g, b_rot, 2, c)
                rot_add(0)
                for p in range(NP_ + 1):
                    if p >= 1:
                        sub_max(p - 1)
                    if p + 1 < NP_:
                        rot_add(p + 1)
                    if p >= 1:
                        norm(p - 1)
                if back:
                    rotation(c - 1)

            def rotation(n):
                g.wait_ge(b_elu, n + 1 + START)
                for side, dst in enumerate((rq[:], rk[:, bass.ds(n * CB, CB), :])):
                    blocks = bass.ds((n % HALVES) * CB, CB)
                    src = qkv[:, side].rearrange("p k (h d) -> p k h d", d=DB)
                    t1 = F[0].mix[:, side, :].rearrange("p (k h d) -> p k h d", k=CB, d=DB)
                    t2 = F[0].prev[:, side, :].rearrange("p (k h d) -> p k h d", k=CB, d=DB)
                    wide = lambda t, lo: t.unsqueeze(2).broadcast_to([P, CB, HB, lo])
                    g.tensor_tensor(t1, src, wide(rot_cos[:, blocks, :], DB), ALU.mult)
                    for odd in range(2):
                        ins_ = g.tensor_tensor(t2[:, :, :, odd::2], src[:, :, :, 1 - odd::2],
                                               wide(rot_sin[:, blocks, odd::2], DB // 2), ALU.mult)
                    ins_.then_inc(b_t2, 1)
                    g.wait_ge(b_t2, n * 2 + side + 1)
                    g.tensor_tensor(dst.rearrange("p k (h d) -> p k h d", d=DB), t1, t2, ALU.add).then_inc(b_rot, 1)

            def features(i, s):
                b, p = turn_no(i, s) // NP_, turn_no(i, s) % NP_
                for h in range(2):
                    at, keys = bass.ds((2 * p + h) * DB, DB), bass.ds(b * BLK, BLK)
                    ins_ = g.tensor_tensor(wf[:, s, h], rk[:, keys, at].unsqueeze(3).broadcast_to([P, BLK, DB, DB]),
                                           v_tok[:, keys, at].unsqueeze(2).broadcast_to([P, BLK, DB, DB]), ALU.mult)
                ins_.then_inc(wf_done, 1)

            def first_features():
                g.wait_ge(b_rot, 2 * (NC - 1) + START)
                g.wait_ge(b_qkv, 3 * (NC - 1) + START)
                g.wait_ge(y_ps, NC + START)
                features(0, 0)
                features(0, 1)

            chunks(g, pool_chunk, lambda n: [lambda: rotation(n)], {0: first_features})
            g.wait_ge(b_rot, 2 * NC + START)
            g.wait_ge(b_qkv, 3 * NC + START)

            def gather(i, s):
                it = turn_no(i, s)
                g.wait_ge(z_ev[s], i + 1)
                g.wait_ge(rqx_in[s], (i + 1) * 16)
                if not isinstance(i, int) or i > 0:
                    g.wait_ge(item_ps, it * PER - 2 - PER + 8)
                g.tensor_tensor(g_sb[:, s, :], z_sb[:, s, :], rqx[:, s, :], ALU.mult).then_inc(g_done[s], 1)
                if not isinstance(i, int) or i < NI - 1:
                    g.wait_ge(r_free, (it + 1) * 4 + RF)
                    features(i + 1, s)

            turns(g, gather)

            def out(f, n, b, hf):
                g.wait_ge(f.s_gate, n + 1 + START)
                g.wait_ge(out_stored[b], hf * 16 + START_DMA)
                at = b * BLK + hf * CB
                g.tensor_tensor(f.out, f.s.rearrange("p (k e) -> p k e", e=E), x_mid[:, at:at + CB, :], ALU.add).then_inc(f.s_out, 1)

            in_order("out0 out2 out1 out3", out=out)

        @block.tensor
        def _(pe):
            t = nc.tensor
            start(t, "pe")
            wait_loads(t, "ident")
            for k in range(4):
                t.wait_ge(xn0, k + 1)
                for q4 in range(4):
                    mm = t.transpose(ps[:, k, q4 * P:(q4 + 1) * P], xn[:, 4 * k + q4, :], ident[:])
                mm.then_inc(xt_ps, 1)
            wait_loads(t, "fold")
            t.matmul(ps[:, 4, 0:H], rel[:, 0:2 * D], rb_t[:], start=True, stop=True)
            t.matmul(ps[:, 4, H:2 * H], rel[:, 2 * D:4 * D], rb_t[:], start=True, stop=True).then_inc(ub_ps, 1)
            for k in range(4):
                if k >= 2:
                    t.wait_ge(xt_ev, k - 1)
                for q4 in range(4):
                    p, slot = 2 * k + q4 // 2, q4 % 2
                    mm = t.matmul(ps[:, WU_BANKS[k], q4 * P:(q4 + 1) * P], wq_t[:, 2 * p + 1 - slot, :], rel[:, D:3 * D],
                                  start=True, stop=True)
                mm.then_inc(wu_ps, 1)
            t.wait_ge(gap_ready, 2)
            t.matmul(ps[:, 5, 0:H], brel_wide[:], bias_gap[:], start=True, stop=True).then_inc(ub_ps, 1)
            wait_loads(t, "band", "rest")
            t.wait_ge(enc_loaded, 64)
            t.wait_ge(cleared, 4)
            t.wait_ge(wu_ev, 4)
            t.wait_ge(xt_ev, 4)

            def value_weights(k):
                for q4 in range(4):
                    h = 4 * k + q4
                    mm = t.matmul(ps[:, k, q4 * P:(q4 + 1) * P], wv_t[:, h, :], wo[:, h, :], start=True, stop=True)
                mm.then_inc(wvo_ps, 1)

            def pe_chunk(c, back):
                def proj(p):
                    t.wait_ge(q_ev, c * NP_ + p + START)
                    t.matmul(ps[:, 0, :], wq[:, p * P:(p + 1) * P], xc[:, EDGE:EDGE + CH], start=True, stop=True).then_inc(q_ps, 1)
                    t.wait_ge(u_ev, c * NP_ + p + START)
                    for k in range(2):
                        mm = t.matmul(ps[:, 1 + k, :], wu[:, k, p].rearrange("p a d -> p (a d)"), xc[:, EDGE:EDGE + CH],
                                      start=True, stop=True)
                    mm.then_inc(u_ps, 1)
                    t.wait_ge(k_ev, c * NP_ + p + START)
                    if p == 0:
                        t.wait_ge(x1_done, c + START)
                    for k in range(2):
                        mm = t.matmul(ps[:, 3 + k, 0:KH], wk[:, p * P:(p + 1) * P], xc[:, SIDE + k * KH:SIDE + (k + 1) * KH],
                                      start=True, stop=True)
                    mm.then_inc(k_ps, 1)

                def scores(p):
                    t.wait_ge(q_ev, c * NP_ + p + 1 + START)
                    t.wait_ge(k_ev, c * NP_ + p + 1 + START)
                    t.wait_ge(rot_done, c * NP_ + p + 1 + START)
                    t.wait_ge(s_masked, c * NP_ + max(p - 1, 0) + START)
                    for blk in range(CB):
                        for par in range(2):
                            for j in range(P // SUB):
                                q0 = blk * P + j * SUB
                                mm = t.matmul(ps[j * SUB:(j + 1) * SUB, 5 + p % 2, (blk * 2 + par) * WIN:(blk * 2 + par + 1) * WIN],
                                              qt[:, p % 2, par, q0:q0 + SUB], kt[:, p % 2, par, q0:q0 + WIN],
                                              start=True, stop=True)
                    mm.then_inc(s_ps, 1)

                def turn_probs(p):
                    t.wait_ge(norm_done, c * NP_ + p + 1 + START)
                    t.wait_ge(pt_ev, c * NP_ + p + START)
                    for blk in range(CB):
                        mm = t.transpose(ps[:, 7, blk * P:(blk + 1) * P], pr[:, p % 2, blk].rearrange("p h w -> p (h w)"), ident[:])
                    mm.then_inc(pt_ps, 1)

                def values_out(blk):
                    t.wait_ge(ze_ev, c * 8 + 2 * blk + 2)
                    t.wait_ge(zo_ev, c * 8 + 2 * blk + 2)
                    dst = ps[:, 4, blk * P:(blk + 1) * P]
                    for h in range(H):
                        t.matmul(dst, zh[:, h, blk * P:(blk + 1) * P], wvo[:, h, :], start=(h == 0), stop=False)
                    mm = t.matmul(dst, ones[:], bo[:], start=False, stop=True)
                    if blk == CB - 1:
                        mm.then_inc(y_ps, 1)

                def windows(k5):
                    bank = 2 + k5 % 3
                    if k5 >= 3:
                        t.wait_ge(xw_ev, c * 5 + k5 - 2)
                    for k in range(4 * k5, min(4 * k5 + 4, NX)):
                        mm = t.transpose(ps[:, bank, (k % 4) * P:(k % 4 + 1) * P], xc[:, k * SUB:k * SUB + P], ident[:])
                    mm.then_inc(xw_ps, 1)

                turn_in, key_gate, value, turn_mid, projections, turn_qk, turn_rotated = (
                    pe_background(c - 1) if back else [nothing] * 7)
                t.wait_ge(xc_ready, c + 1)
                proj(0)
                proj(1)
                behind(t, b_rqt, 1, c)
                behind(t, b_hi, 2, c)
                behind(t, b_r1, 2, c)
                for p in range(NP_):
                    if p > 0 and p + 1 < NP_:
                        proj(p + 1)
                    if p == NP_ - 1:
                        t.wait_ge(q_ev, c * NP_ + NP_ + START)
                        if not back:
                            wait_loads(t, "value")
                            value_weights(0)
                        turn_in()
                    if p == NP_ - 1:
                        scores(p)
                        turn_probs(p - 2)
                        t.wait_ge(u_ev, c * NP_ + NP_ + START)
                        t.wait_ge(k_ev, c * NP_ + NP_ + START)
                        for k5 in range(3):
                            windows(k5)
                    else:
                        if p >= 2:
                            turn_probs(p - 2)
                        scores(p)
                turn_probs(NP_ - 2)
                key_gate()
                if not back:
                    value_weights(1)
                for k5 in range(3, 5):
                    windows(k5)
                turn_probs(NP_ - 1)
                t.wait_ge(xw_ev, c * 5 + 5)
                if not back:
                    value_weights(2)
                    value_weights(3)
                t.wait_ge(s_masked, c * NP_ + NP_ + START)
                t.wait_ge(pt_ev, c * NP_ + NP_ + START)
                if not back:
                    t.wait_ge(wvo_ev, 4)
                for v in range(NW // 2):
                    if v >= 2:
                        t.wait_ge(ze_ev, c * 8 + v - 1)
                        t.wait_ge(zo_ev, c * 8 + v - 1)
                    if v == 1:
                        value()
                        if back:
                            t.wait_ge(f_exp, c + START)
                            t.wait_ge(f_relu, c + START)
                    for w2 in range(2):
                        for par in range(2):
                            rows = slice(D * par, D * par + WIN)
                            w = 2 * v + w2
                            mm = t.matmul(ps[:, VALUE_BANKS[v % 2] + par, w2 * 256:(w2 + 1) * 256].rearrange("p (g t) -> p g t", g=NP_),
                                          xw[rows, w + 2 * (1 - par), :], pt[rows, :, w * SUB:(w + 1) * SUB], start=True, stop=True)
                            if w2:
                                mm.then_inc(pv_ps, 1)
                    if v == 3:
                        turn_mid()
                        if back:
                            t.wait_ge(f_gate, c + START)
                    if v == 4:
                        projections()
                    if v == NW // 2 - 1:
                        turn_qk()
                    if v % 2 and v > 1:
                        values_out(v // 2 - 1)
                turn_rotated()
                values_out(CB - 1)

            def pe_background(n):
                def turn_mid():
                    t.wait_ge(b_rqt, n + START)
                    t.wait_ge(b_hi, 2 * n + START)
                    t.wait_ge(b_r1, 2 * n + START)
                    t.wait_ge(lnb.xh, n + 1)
                    for blk in range(CB):
                        mm = t.transpose(ps[:, 5, blk * P:(blk + 1) * P], xh[:, blk, :], ident[:])
                    mm.then_inc(lnb.t_ps, 1)

                def value():
                    t.wait_ge(x1_done, n + 1 + START)
                    ffn_value(t, F[0], n)

                def project(side):
                    t.wait_ge(lnb.t_ev, n + 1)
                    for blk in range(CB):
                        mm = t.matmul(ps[:, 5 + side, blk * P:(blk + 1) * P], x3t[:, blk * P:(blk + 1) * P],
                                      wqkv[:, side * E:(side + 1) * E], start=True, stop=True)
                    mm.then_inc(b_qkv_ps, 1)

                def projections():
                    for side in range(3):
                        project(side)

                def turn_qk():
                    t.wait_ge(b_elu, n + 1 + START)
                    t.wait_ge(b_qkv, n * 3 + 3 + START)
                    for side in range(2):
                        for blk in range(CB):
                            mm = t.transpose(ps[:, 6 + side, blk * P:(blk + 1) * P], qkv[:, side, blk], ident[:])
                        mm.then_inc(b_qk_t, 1)

                def turn_rotated():
                    t.wait_ge(b_rot, n * 2 + 1 + START)
                    for blk in range(CB):
                        mm = t.transpose(ps[:, 5, blk * P:(blk + 1) * P], rq[:, blk, :], ident[:])
                    mm.then_inc(b_rq_t, 1)

                return [lambda: ffn_turn(t, F[0], n), lambda: ffn_key_gate(t, F[0], n), value, turn_mid, projections,
                        turn_qk, turn_rotated]



            def den(s, gi, ih, bank):
                h, jb = gi % 2, gi // 2
                return t.matmul(ps[:, bank, :], ks[0:KROWS, s, h, jb * P:(jb + 1) * P],
                                qs[0:KROWS, s, h, ih * 512:(ih + 1) * 512], start=True, stop=True)

            def den_a(i, s, n):
                no = turn_no(i, s) * NA + n
                bank = 2 * ((s * NA + n) % 2)
                if_any(t, ln_done, no - 1)
                gi = ACT_LIST[n]
                if gi == 15:
                    mm = den(s, gi, 1, bank)
                else:
                    den(s, gi, 0, bank)
                    mm = den(s, gi, 1, bank + 1)
                mm.then_inc(den_act, 1)

            def output(i, s, j, bank):
                t.wait_ge(g_done[s], i + 1 + START)
                p = turn_no(i, s) % NP_
                for blk in range(CB):
                    at = (j * CB + blk) * P
                    mm = t.matmul(ps[:, bank, blk * P:(blk + 1) * P], g_sb[:, s, at:at + P],
                                  wout[:, bass.ds(p, 1), :].rearrange("p a e -> p (a e)"), start=True, stop=True)
                return mm

            def item(i, s, k):
                items, base = items_of(turn_no(i, s))
                kind, j = items[k]
                bank = item_bank(turn_no(i, s), s, k)
                if_any(t, item_done, base + k - (0 if isinstance(i, int) and (i, s, k) == (0, 1, 0) else 1))
                if kind == "U":
                    mm = den(s, 4 * (j // 2) + 3, j % 2, bank)
                else:
                    mm = output(*before(i, s), j, bank)
                mm.then_inc(item_ps, 1)

            def z(i, s, jb, ih):
                it, m = turn_no(i, s), jb // 2
                t.wait_ge(r_act, it * NA + 3 * m + (2 if jb % 2 == 0 else 3 if m < 3 else 4))
                if jb % 2:
                    lst, base = items_of(it)
                    t.wait_ge(item_done, base + lst.index(("U", 2 * m + ih if m < 3 else 6)) + 1)
                for h in range(2):
                    mm = t.matmul(ps[D * h:D * (h + 1), 6 + ih, :], wf[:, s, h, jb].rearrange("p a d -> p (a d)"),
                                  r_buf[:, 4 * (m % 2) + 2 * (jb % 2) + h, ih * 512:(ih + 1) * 512],
                                  start=(jb == 0), stop=(jb == BLK - 1))
                return mm

            ORDER = "u a a z u z a z z a u u a z u z a z z a u a z u z a z z a u a a z u z a z z"

            def next_turn(i, s):
                return (i, 1) if s == 0 else (i + 1, 0)

            def turn_pe(i, s):
                it = turn_no(i, s)
                more = s == 0 or not isinstance(i, int) or i < NI - 1
                lst, _ = items_of(it)
                ahead_a = [(i, s, n) for n in range(3, NA)] + ([(*next_turn(i, s), n) for n in range(3)] if more else [])
                ahead_u = [(i, s, k) for k in range(2, len(lst))] + ([(*next_turn(i, s), k) for k in range(2)] if more else [])
                if isinstance(it, int) and it == 0:
                    ahead_u[0] = None
                    ahead_u.insert(2, None)
                    ahead_u.insert(5, None)
                done, waited = 0, False
                for x in ORDER.split():
                    if x == "z":
                        if done == 0:
                            t.wait_ge(wf_done, it + 1)
                            pi, ps_ = before(i, s)
                            if_any(t, z_ev[ps_], pi + 1)
                        mm = z(i, s, done // 2, done % 2)
                        done += 1
                        if done % 4 == 0:
                            mm.then_inc(r_free, 1)
                        continue
                    todo, issue = (ahead_a, den_a) if x == "a" else (ahead_u, item)
                    if todo:
                        which = todo.pop(0)
                        if which is None:
                            continue
                        if which[1] != s and not waited:
                            t.wait_ge(stack_in[which[1]], (which[0] + 1) * 192)
                            waited = True
                        issue(*which)

            def first_item():
                t.wait_ge(stack_in[0], 192)
                t.wait_ge(f_gate, NC + START)
                item(0, 0, 0)

            def first_arrays():
                t.wait_ge(f_exp, NC + START)
                t.wait_ge(f_relu, NC + START)
                for n in range(3):
                    den_a(0, 0, n)

            def second_item():
                t.wait_ge(item_done, 1)
                item(0, 0, 1)

            chunks(t, pe_chunk, pe_background, {3: first_item, 5: first_arrays, 6: second_item})
            t.wait_ge(b_rqt, NC + START)
            item(0, 0, 2)
            t.wait_ge(b_r1, 2 * NC + START)
            turns(t, turn_pe)
            parts_pe = dict(turn=lambda f, n, b, hf: ffn_turn(t, f, n), key=lambda f, n, b, hf: ffn_key_gate(t, f, n),
                            value=lambda f, n, b, hf: ffn_value(t, f, n))
            t.wait_ge(r_act, NB * NP_ * NA)
            in_order("turn0", **parts_pe)
            for j in range(2):
                t.wait_ge(item_done, NB * NP_ * PER - 2 + j - 1)
                output(NI - 1, 1, j, 4 + j).then_inc(item_ps, 1)
            in_order("key0", **parts_pe)
            t.wait_ge(item_done, NB * NP_ * PER - 2 + 2)
            t.wait_ge(z_ev[1], NI)
            in_order("value0 turn2 turn1 key2 key1 value2 turn3 value1 key3 value3", **parts_pe)

        @block.scalar
        def _(act):
            a = nc.scalar
            start(a, "act")
            a.preload_act_table_set("natural_log_exp_and_others")
            a.wait_ge(mv0, 1)
            a.activation(lnv[:], mv[:, :, 1], ACT.Ln, bias=eps[:, 0:1]).then_inc(lnv0, 1)
            a.wait_ge(lnv0, 1)
            a.activation(rstd[:], lnv[:], ACT.Exp, scale=-0.5).then_inc(rstd0, 1)
            for k in range(4):
                a.wait_ge(xt_ps, k + 1)
                a.copy(xT[:, k // 2, EDGE + CH * (k % 2):EDGE + CH * (k % 2 + 1)], ps[:, k, :]).then_inc(xt_ev, 1)
            for k in range(4):
                a.wait_ge(wu_ps, k + 1)
                src = ps[:, WU_BANKS[k], :].rearrange("p (g s w d) -> p g s w d", g=2, s=2, w=2)
                for w in range(2):
                    ins_ = a.copy(wu[:, w, 2 * k:2 * k + 2], src[:, :, :, w, :])
                ins_.then_inc(wu_ev, 1)
            def evac_value_weights(k):
                a.wait_ge(wvo_ps, k + 1)
                a.copy(wvo[:, 4 * k:4 * k + 4, :], ps[:, k, :].rearrange("p (h e) -> p h e", h=4)).then_inc(wvo_ev, 1)

            def act_chunk(c, back):
                def evac_proj(p):
                    a.wait_ge(q_ps, c * NP_ + p + 1)
                    a.wait_ge(s_ps, c * NP_ + max(p - 1, 0) + START)
                    a.activation(qt[0:D, p % 2, 0, :], ps[0:D, 0, :], ACT.Identity, bias=cb_pair[0:D, p:p + 1])
                    a.activation(qt[D:P, p % 2, 1, :], ps[D:P, 0, :], ACT.Identity, bias=cb_pair[D:P, p:p + 1]).then_inc(q_ev, 1)
                    a.wait_ge(k_ps, c * NP_ + p + 1 + START)
                    for par in range(2):
                        rows = slice(D * par, D * par + D)
                        ins_ = a.activation(kt[rows, p % 2, par, :].rearrange("p (a t) -> p a t", a=2), ps[rows, 3:5, 0:KH],
                                            ACT.Identity, bias=brel[rows, 0:1])
                    ins_.then_inc(k_ev, 1)

                def exp_s(p):
                    a.wait_ge(sub_done, c * NP_ + p + 1)
                    a.wait_ge(pt_ps, c * NP_ + max(p - 1, 0) + START)
                    a.activation(pr[:, p % 2], sm[:, p % 2], ACT.Exp, scale=SCALE).then_inc(exp_done, 1)

                def evac_probs(p):
                    a.wait_ge(pt_ps, c * NP_ + p + 1 + START)
                    a.copy(pt[:, p, :], ps[:, 7, :]).then_inc(pt_ev, 1)

                def evac_windows(k5):
                    a.wait_ge(xw_ps, c * 5 + k5 + 1)
                    if k5 == 0:
                        a.wait_ge(pv_ps, c * 16 + START)
                    n = min(4, NX - 4 * k5)
                    a.copy(xw[:, 4 * k5:4 * k5 + n, :], ps[:, 2 + k5 % 3, 0:n * E].rearrange("p (w e) -> p w e", w=n)).then_inc(xw_ev, 1)

                ln_first, turned, key_gate, ln_mid, turned_mid, exp_neg, split, rotated = (
                    act_background(c - 1) if back else [nothing] * 8)
                evac_proj(0)
                evac_proj(1)
                behind(a, b_rot, 2, c)
                behind(a, b_qk_t, 2, c)
                behind(a, b_r1, 2, c)
                for p in range(NP_ + 1):
                    if p >= 1:
                        exp_s(p - 1)
                    if p == NP_ - 1:
                        turned()
                        if not back:
                            evac_value_weights(0)
                    if p > 0 and p + 1 < NP_:
                        evac_proj(p + 1)
                    if p == 3:
                        ln_first()
                    if p >= 2:
                        evac_probs(p - 2)
                    if p == NP_ - 1:
                        for k5 in range(3):
                            evac_windows(k5)
                    if p == NP_:
                        key_gate()
                if not back:
                    evac_value_weights(1)
                for k5 in range(3, 5):
                    evac_windows(k5)
                evac_probs(NP_ - 1)
                if not back:
                    evac_value_weights(2)
                    evac_value_weights(3)
                for v in range(NW // 2):
                    a.wait_ge(pv_ps, c * 16 + 2 * v + 1 + START)
                    a.wait_ge(y_ps, c + START)
                    a.copy(zh_view(v, 0), ps[:, VALUE_BANKS[v % 2], :].rearrange("p (w g t) -> p w g t", w=2, g=NP_)).then_inc(ze_ev, 1)
                    if v == 1:
                        ln_mid()
                    if v == 3:
                        turned_mid()
                    if v == 5:
                        exp_neg()
                split()
                rotated()

            def act_background(n):
                b, hf = n // HALVES, n % HALVES

                def turned():
                    a.wait_ge(lnb.t_ps, n + 1)
                    a.copy(x3t, ps[:, 5, :]).then_inc(lnb.t_ev, 1)

                def exp_neg():
                    for side in range(2):
                        a.wait_ge(b_min, n * 2 + side + 1)
                        a.activation(qk_neg[:, side], qk_neg[:, side], ACT.Exp).then_inc(b_exp, 1)

                def split():
                    a.wait_ge(parts_stored, n * 32 + START_DMA)
                    for side in range(2):
                        a.wait_ge(b_qk_t, n * 2 + side + 1 + START)
                        a.copy(parts[:, side, 0, :], ps[:, 6 + side, :]).then_inc(b_hi, 1)
                    for side in range(2):
                        a.wait_ge(b_r1, n * 2 + side + 1 + START)
                        a.copy(parts[:, side, 1, :], rest[:, side, :]).then_inc(b_mid, 1)

                def rotated():
                    a.wait_ge(b_rq_t, n + 1)
                    a.copy(rqt, ps[:, 5, :]).then_inc(b_rqt, 1)

                def first():
                    a.wait_ge(rq_stored, n * 16 + START_DMA)
                    ffn_act(a, F[0], n)

                return [lambda: ln_act(a, F[0], F[0].ln, n), lambda: ffn_turned(a, F[0], n, b, hf), first,
                        lambda: ln_act(a, F[0], lnb, n), turned, exp_neg, split, rotated]


            def parts_of(s, n):
                k = (s * NA + n) % 2
                gi = ACT_LIST[n]
                r = r_buf[:, gi % 8, :]
                if gi == 15:
                    return ps[:, 2 * k, :], r[:, 512:1024]
                return ps[:, 2 * k:2 * k + 2, :].rearrange("p a t -> p (a t)"), r

            def log(i, s, n):
                no = turn_no(i, s) * NA + n
                src, dst = parts_of(s, n)
                a.wait_ge(den_act, no + 1)
                a.wait_ge(r_free, turn_no(i, s) * 4 + ACT_LIST[n] // 4 - 1 + RF)
                a.activation(dst, src, ACT.Ln).then_inc(ln_done, 1)

            def inv(i, s, n):
                no = turn_no(i, s) * NA + n
                _, dst = parts_of(s, n)
                a.wait_ge(ln_done, no + 1)
                a.activation(dst, dst, ACT.Exp, scale=-1.0).then_inc(r_act, 1)

            def copy_sums(i, s):
                a.wait_ge(r_free, (turn_no(i, s) + 1) * 4 + RF)
                a.wait_ge(g_done[s], i + START)
                a.copy(z_sb[:, s, :], ps[:, 6:8, :].rearrange("p a t -> p (a t)")).then_inc(z_ev[s], 1)

            def turn_act(i, s):
                last = isinstance(i, int) and i == NI - 1 and s == 1
                for n in range(2 if isinstance(i, int) and i == 0 and s == 0 else 0, NA):
                    if n + 1 < NA:
                        log(i, s, n + 1)
                    elif not last:
                        log(*((i, 1) if s == 0 else (i + 1, 0)), 0)
                    inv(i, s, n)
                    if n == 1 and not (isinstance(i, int) and i == 0 and s == 0):
                        copy_sums(*before(i, s))

            def first_two():
                log(0, 0, 0)
                log(0, 0, 1)
                inv(0, 0, 0)

            def third():
                log(0, 0, 2)
                inv(0, 0, 1)

            chunks(a, act_chunk, act_background, {6: first_two, 7: third})
            turns(a, turn_act)
            end_rstd(a, 0)
            copy_sums(NI - 1, 1)

            def gate(f, n, b, hf):
                a.wait_ge(f.s_r_ps, n + 1)
                a.wait_ge(f.s_gate, n + START)
                a.activation(f.e, ps[:, f.gate_bank, :], ACT.Sigmoid).then_inc(f.s_exp, 1)

            parts_act = dict(turned=lambda f, n, b, hf: ffn_turned(a, f, n, b, hf),
                             square=lambda f, n, b, hf: relu_square(a, f, n), gate=gate)
            in_order("turned0 square0", **parts_act)
            end_rstd(a, 1)
            a.wait_ge(rq_stored, NC * 16 + START_DMA)
            in_order("gate0 turned2 turned1 square2 gate2 turned3 square1 gate1 square3 gate3", **parts_act)

        @block.vector
        def _(dve):
            d = nc.vector
            start(d, "dve")
            d.memset(eps[:], EPS).then_inc(small_ready, 1)
            d.wait_ge(x_loaded, 16)
            for k in range(NB * BLK):
                ins_ = d.bn_stats(stat[:, k, :], x_tok[:, k, :])
            ins_.then_inc(st0, 1)
            d.wait_ge(st0, 1)
            d.wait_ge(small_ready, 1)
            for k in range(NB * BLK):
                ins_ = d.bn_aggr(mv[:, k, :], stat[:, k, :])
            ins_.then_inc(mv0, 1)
            d.wait_ge(rstd0, 1)
            for k in range(NB * BLK):
                ins_ = d.tensor_scalar(xn[:, k, :], x_tok[:, k, :], mv[:, k, 0:1], rstd[:, k:k + 1], ALU.subtract, ALU.mult)
                if k % 4 == 3:
                    ins_.then_inc(xn0, 1)
            wait_loads(d, "fold")
            d.tensor_tensor(bias_gap[:], rb_t[:], cb_t[:], ALU.subtract).then_inc(gap_ready, 1)
            d.tensor_copy(brel_wide[:], brel[0:D, 0:1].broadcast_to([D, P])).then_inc(gap_ready, 1)
            d.tensor_scalar(mu_rest[:], mu[:], -1.0, 1.0, ALU.mult, ALU.add).then_inc(small_ready, 1)
            d.wait_ge(ub_ps, 1)
            for w in range(2):
                src = ps[:, 4, w * H:(w + 1) * H].rearrange("p (g two) -> p g two", two=2)
                d.tensor_copy(u_bias[0:D, w, :], src[0:D, :, 1])
                ins_ = d.tensor_copy(u_bias[D:P, w, :], src[D:P, :, 0])
            ins_.then_inc(ub_ev, 2)
            d.wait_ge(ub_ps, 2)
            d.tensor_copy(head_const[:], ps[:, 5, 0:H]).then_inc(ub_ev, 1)
            wait_loads(d, "band", "rest")
            d.wait_ge(ub_ev, 3)
            d.wait_ge(small_ready, 2)
            d.wait_ge(cleared, 4)
            d.wait_ge(xt_ev, 4)
            def keys_of(c):
                b, hf = c // HALVES, c % HALVES
                d.tensor_copy(xc[:], xT[:, bass.ds(b, 1), bass.ds(hf * CH, XC)].rearrange("p a t -> p (a t)")).then_inc(xc_ready, 1)

            keys_of(0)

            def dve_chunk(c, back):
                b, hf = c // HALVES, c % HALVES
                def rotate(p):
                    d.wait_ge(u_ps, c * NP_ + p + 1)
                    d.wait_ge(rot_done, c * NP_ + max(p - 1, 0) + START)
                    d.scalar_tensor_tensor(turn[:, p % 2, 0, :], ps[:, 1, :], u_bias[:, 0, p:p + 1], sin_q[:], ALU.add, ALU.mult)
                    d.scalar_tensor_tensor(turn[:, p % 2, 1, :], ps[:, 2, :], u_bias[:, 1, p:p + 1], cos_q[:],
                                           ALU.add, ALU.mult).then_inc(u_ev, 1)

                def mask_max(p):
                    d.wait_ge(s_ps, c * NP_ + p + 1 + START)
                    d.wait_ge(exp_done, c * NP_ + max(p - 1, 0) + START)
                    src = ps[:, 5 + p % 2, :].rearrange("p (k h w) -> p k h w", h=2, w=WIN)
                    for par in range(2):
                        ins_ = d.scalar_tensor_tensor(sm[:, p % 2, :, par, :], src[:, :, par, :], head_const[:, 2 * p + par:2 * p + par + 1],
                                                      mask[:, bass.ds(hf, 1)].rearrange("p a k w -> p (a k) w"), ALU.add, ALU.add)
                    ins_.then_inc(s_masked, 1)
                    d.wait_ge(s_masked, c * NP_ + p + 1 + START)
                    d.tensor_reduce(mx[:, p % 2, :], sm[:, p % 2].rearrange("p k h w -> p (k h) w"), AX.X, ALU.max).then_inc(mx_done, 1)

                def total(p):
                    d.wait_ge(exp_done, c * NP_ + p + 1 + START)
                    d.tensor_reduce(tot[:, p % 2, :], pr[:, p % 2].rearrange("p k h w -> p (k h) w"), AX.X, ALU.add).then_inc(sum_done, 1)
                    d.wait_ge(sum_done, c * NP_ + p + 1)
                    d.wait_ge(norm_done, c * NP_ + max(p - 1, 0) + START)
                    d.reciprocal(rtot[:, p % 2, :], tot[:, p % 2, :]).then_inc(rec_done, 1)

                norm_stats, norm_in, mix, sigmoid, gate, norm_mid, add_bias, elu_one, split, _ = (
                    dve_background(c - 1) if back else [nothing] * 10)
                behind(d, b_exp, 2, c)
                behind(d, b_elu, 1, c)
                behind(d, b_mid, 2, c)
                behind(d, b_lo, 2, c)
                behind(d, b_qkv, 3, c)
                rotate(0)
                for p in range(NP_ + 1):
                    if p + 1 < NP_:
                        rotate(p + 1)
                    if p == NP_ - 1:
                        mask_max(p)
                    if p >= 1:
                        total(p - 1)
                    if p == NP_ - 1:
                        mix()
                    elif p < NP_:
                        mask_max(p)
                    if p == 2:
                        norm_stats()
                    if p == 4:
                        norm_in()
                sigmoid()
                for v in range(NW // 2):
                    d.wait_ge(pv_ps, c * 16 + 2 * v + 2 + START)
                    d.wait_ge(y_ps, c + START)
                    d.tensor_copy(zh_view(v, 1), ps[:, VALUE_BANKS[v % 2] + 1, :].rearrange("p (w g t) -> p w g t", w=2, g=NP_)).then_inc(zo_ev, 1)
                    if v == 3:
                        keys_of((c + 1) % NC)
                    if v in (0, 1, 5, 6):
                        {0: gate, 1: norm_mid, 5: add_bias, 6: elu_one}[v]()
                split()
                d.wait_ge(y_ps, c + 1 + START)
                d.tensor_tensor(x1[:], ps[:, 4, :].rearrange("p (k e) -> p k e", e=E), x_tok[:, bass.ds(c * CB, CB), :],
                                ALU.add).then_inc(x1_done, 1)

            def dve_background(n):
                b, hf = n // HALVES, n % HALVES
                x_c = x_mid[:, bass.ds(n * CB, CB), :]
                mid = lambda k: x_mid[:, bass.ds(n * CB + k, 1), :].rearrange("p a e -> p (a e)")
                bias = lambda side: bqkv[:, side * E:(side + 1) * E].unsqueeze(1).broadcast_to([P, CB, E])

                def norm_stats():
                    d.wait_ge(x1_done, n + 1 + START)
                    ln_stats(d, F[0], F[0].ln, n, lambda k: x1[:, k, :])

                def norm_in():
                    ln_apply(d, F[0], F[0].ln, n, lambda k: x1[:, k, :])

                def mix():
                    d.wait_ge(b_rot, 2 * n + START)
                    ffn_mix(d, F[0], n, b, hf)

                def gate():
                    ffn_gate(d, F[0], n, x1[:], x_c)
                    d.wait_ge(F[0].s_out, n + 1)
                    ln_stats(d, F[0], lnb, n, mid)

                def norm_mid():
                    ln_apply(d, F[0], lnb, n, mid)
                    d.wait_ge(lnb.xh, n + 1)
                    d.tensor_tensor(x_c, x_c, bout[:].unsqueeze(1).broadcast_to([P, CB, E]), ALU.add).then_inc(b_bias, 1)

                def add_bias():
                    for side in range(3):
                        dst = qkv[:, side] if side < 2 else v_tok[:, bass.ds(n * CB, CB), :]
                        d.wait_ge(b_qkv_ps, n * 3 + side + 1)
                        d.tensor_tensor(dst, ps[:, 5 + side, :].rearrange("p (k e) -> p k e", e=E), bias(side), ALU.add).then_inc(b_qkv, 1)
                        if side < 2:
                            d.wait_ge(b_qkv, n * 3 + side + 1 + START)
                            d.tensor_scalar(qk_neg[:, side], qkv[:, side].rearrange("p k n -> p (k n)"), 0.0, None, ALU.min).then_inc(b_min, 1)

                def elu_one():
                    d.wait_ge(b_exp, n * 2 + 2 + START)
                    flat = qkv[:].rearrange("p a k n -> p (a k n)")
                    d.scalar_tensor_tensor(flat, flat, 0.0, qk_neg[:].rearrange("p a t -> p (a t)"), ALU.max, ALU.add).then_inc(b_elu, 1)

                def split():
                    for side in range(2):
                        d.wait_ge(b_hi, n * 2 + side + 1 + START)
                        d.tensor_tensor(rest[:, side, :], ps[:, 6 + side, :], parts[:, side, 0, :], ALU.subtract).then_inc(b_r1, 1)
                    for side in range(2):
                        d.wait_ge(b_mid, n * 2 + side + 1 + START)
                        d.wait_ge(b_r1, n * 2 + side + 1 + START)
                        d.tensor_tensor(parts[:, side, 2, :], rest[:, side, :], parts[:, side, 1, :], ALU.subtract).then_inc(b_lo, 1)

                return [norm_stats, norm_in, mix, lambda: ffn_sigmoid(d, F[0], n), gate, norm_mid, add_bias, elu_one, split,
                        nothing]


            def take(i, s, k):
                it = turn_no(i, s)
                lst, base = items_of(it)
                kind, j = lst[k]
                bank = item_bank(it, s, k)
                if kind == "U":
                    m = j // 2
                    d.wait_ge(r_free, it * 4 + m - 1 + RF)
                    d.wait_ge(item_ps, base + k + 1)
                    d.reciprocal(r_buf[:, (4 * m + 3) % 8, (j % 2) * 512:(j % 2 + 1) * 512], ps[:, bank, :]).then_inc(item_done, 1)
                else:
                    b = turn_no(*before(i, s)) // NP_
                    at = x_mid[:, bass.ds(b * BLK + j * CB, CB), :]
                    d.wait_ge(item_ps, base + k + 1)
                    if_any(d, item_done, base + k + 1 - PER + (1 if isinstance(it, int) and it <= 1 else 0))
                    d.tensor_tensor(at, ps[:, bank, :].rearrange("p (k e) -> p k e", e=E), at, ALU.add).then_inc(item_done, 1)

            def turn_dve(i, s):
                for k in range(2 if isinstance(i, int) and i == 0 and s == 0 else 0, len(items_of(turn_no(i, s))[0])):
                    take(i, s, k)

            chunks(d, dve_chunk, dve_background, {6: lambda: take(0, 0, 0), 9: lambda: take(0, 0, 1)})
            d.wait_ge(b_bias, NC)
            turns(d, turn_dve)
            def norm(f, n, b, hf):
                d.wait_ge(ln_end[b].mv, 1)
                d.wait_ge(ln_end[b].rstd, 1)
                if hf:
                    d.wait_ge(f.ln.t_ps, n)
                for blk in range(CB):
                    at = b * BLK + hf * CB + blk
                    ins_ = d.tensor_scalar(f.xh[:, blk, :], x_mid[:, at, :], mv[:, at, 0:1], rstd[:, at:at + 1], ALU.subtract, ALU.mult)
                ins_.then_inc(f.ln.xh, 1)

            def mix(f, n, b, hf):
                if hf:
                    d.wait_ge(f.s_r_ps, n)
                ffn_mix(d, f, n, b, hf)

            def gate(f, n, b, hf):
                d.wait_ge(f.s_exp, n + 1 + START)
                d.wait_ge(f.s_v_ps, n + 1 + START)
                if hf:
                    d.wait_ge(f.s_out, n)
                d.tensor_tensor(f.s, ps[:, f.value_bank, :], f.e, ALU.mult).then_inc(f.s_gate, 1)

            total = NB * NP_ * PER - 2
            end_stats(d, 0)
            in_order("norm0 mix0", norm=norm, mix=mix)
            for j in range(2):
                b = NB - 1
                at = x_mid[:, b * BLK + j * CB:b * BLK + (j + 1) * CB, :]
                d.wait_ge(item_ps, total + j + 1)
                d.wait_ge(item_done, total)
                d.tensor_tensor(at, ps[:, 4 + j, :].rearrange("p (k e) -> p k e", e=E), at, ALU.add).then_inc(item_done, 1)
            d.wait_ge(item_done, total + 2)
            end_stats(d, 1)
            in_order("norm2 norm1 gate0 mix2 mix1 norm3 gate2 mix3 gate1 gate3",
                     norm=norm, mix=mix, gate=gate)


def kernel(**inputs):
    import concourse.bacc as bacc
    from concourse.bass_utils import run_bass_kernel_spmd

    nc = bacc.Bacc("TRN2", target_bir_lowering=False, num_devices=1)
    arrays = {k: np.ascontiguousarray(v) for k, v in layouts(inputs).items()}
    arrays.update({k: np.ascontiguousarray(v.astype(np.float32)) for k, v in constants().items()})
    named = {f"in_{k}": v for k, v in arrays.items()}
    ins = {k: nc.dram_tensor(f"in_{k}", v.shape, mybir.dt.from_np(v.dtype), kind="ExternalInput").ap() for k, v in arrays.items()}
    out = nc.dram_tensor("out", [NB * NT // CH, P, CB, E], F32, kind="ExternalOutput").ap()
    split = nc.dram_tensor("split_parts", [2, NB, PARTS, P, NT], BF16, kind="Internal").ap()
    rq = nc.dram_tensor("rotated_q", [NB, P, NT], F32, kind="Internal").ap()
    program(nc, ins, out, split, rq)
    r = run_bass_kernel_spmd(nc, [named], core_ids=[0])
    got = np.asarray(r.results[0]["out"])
    return got.transpose(0, 2, 1, 3).reshape(NB, NT, E)
```
